# Optimizing a Trainium2 kernel written in Bass

```python
import numpy as np
import jax
import jax.numpy as jnp

def _softmax(x, axis=-1):
    return jax.nn.softmax(x, axis=axis)

def _gelu(x):
    return jax.nn.gelu(x, approximate=True)

def _silu(x):
    return jax.nn.silu(x)

def _sigmoid(x):
    return jax.nn.sigmoid(x)

def _layernorm(x, axis=-1, eps=1e-05):
    m = jnp.mean(x, axis=axis, keepdims=True)
    v = jnp.var(x, axis=axis, keepdims=True)
    return (x - m) / jnp.sqrt(v + eps)

def _scatter_add(tgt, idx, src, axis=0):
    return tgt.at[idx].add(src)

def _segment_sum(src, seg, n):
    return jax.ops.segment_sum(src, seg, n)
kernel_name = 'mk_seq_postln_d2_jaxref_r4_eaa70e'

def setup_inputs(seed: int=0):
    np.random.seed(seed)
    _w = jnp.asarray

    def _L0_attn_setup():
        import jax, jax.numpy as jnp
        import numpy as np
        HEAD_NUM = 16
        key = jax.random.key(seed)
        ks = jax.random.split(key, 9)
        B, S, D = (4, 512, 256)

        def xavier(k, shape):
            limit = jnp.sqrt(6.0 / (shape[0] + shape[1]))
            return jax.random.uniform(k, shape, jnp.float32, -limit, limit)
        return {'x': jax.random.normal(ks[0], (B, S, D), jnp.float32), 'Wq': xavier(ks[1], (D, D)), 'bq': jnp.zeros((D,), jnp.float32), 'Wk': xavier(ks[2], (D, D)), 'bk': jnp.zeros((D,), jnp.float32), 'Wv': xavier(ks[3], (D, D)), 'bv': jnp.zeros((D,), jnp.float32), 'Wo': xavier(ks[4], (D, D)), 'bo': jnp.zeros((D,), jnp.float32)}
    _L0_attn_in = _L0_attn_setup()

    def _L0_ffn_setup():
        import jax, jax.numpy as jnp
        import numpy as np
        D_MODEL = 256
        N_EXPERTS = 8
        TOP_K = 2
        FFN_HIDDEN = 4 * D_MODEL
        key = jax.random.key(seed)
        ks = jax.random.split(key, 6)

        def xavier(k, shape):
            fan_in, fan_out = (shape[-2], shape[-1])
            lim = jnp.sqrt(6.0 / (fan_in + fan_out))
            return jax.random.uniform(k, shape, jnp.float32, -lim, lim)
        x = jax.random.normal(ks[0], (4, 512, D_MODEL), jnp.float32)
        w_gate = xavier(ks[1], (N_EXPERTS, D_MODEL))
        W1 = xavier(ks[2], (N_EXPERTS, D_MODEL, FFN_HIDDEN))
        b1 = jnp.zeros((N_EXPERTS, FFN_HIDDEN), jnp.float32)
        W2 = xavier(ks[3], (N_EXPERTS, FFN_HIDDEN, D_MODEL))
        b2 = jnp.zeros((N_EXPERTS, D_MODEL), jnp.float32)
        return {'x': x, 'w_gate': w_gate, 'W1': W1, 'b1': b1, 'W2': W2, 'b2': b2}
    _L0_ffn_in = _L0_ffn_setup()

    def _L1_attn_setup():
        import jax, jax.numpy as jnp
        import numpy as np
        from jax import lax
        NUM_LEVELS = 2
        NUM_HEADS = 16
        LN_EPS = 1e-05
        ATTN_EPS = 1e-06

        def dwconv(x, filt):
            C = x.shape[-1]
            return lax.conv_general_dilated(x, filt[:, None, :], window_strides=(1,), padding='SAME', dimension_numbers=('NWC', 'WIO', 'NWC'), feature_group_count=C)

        def linear_attention(x, num_heads):
            B, N, C = x.shape
            d = C // num_heads
            h = x.reshape(B, N, num_heads, d)
            q = jax.nn.elu(h) + 1.0
            k = q
            v = h
            kv = jnp.einsum('bnhd,bnhe->bhde', k, v)
            z = k.sum(axis=1)
            num = jnp.einsum('bnhd,bhde->bnhe', q, kv)
            den = jnp.einsum('bnhd,bhd->bnh', q, z)[..., None] + ATTN_EPS
            return (num / den).reshape(B, N, C)

        def layer_norm(x, gamma, beta):
            mu = jnp.mean(x, axis=-1, keepdims=True)
            var = jnp.mean(jnp.square(x - mu), axis=-1, keepdims=True)
            return (x - mu) * lax.rsqrt(var + LN_EPS) * gamma + beta
        key = jax.random.key(seed)
        ks = jax.random.split(key, 7)
        B, S, C, K = (8, 1024, 256, 4)
        x = jax.random.normal(ks[0], (B, S, C), dtype=jnp.float32)
        scale = 1.0 / np.sqrt(K)
        h_filter = jax.random.normal(ks[1], (K, C), dtype=jnp.float32) * scale
        g_filter = jax.random.normal(ks[2], (K, C), dtype=jnp.float32) * scale
        h_synth = jax.random.normal(ks[3], (K, C), dtype=jnp.float32) * scale
        g_synth = jax.random.normal(ks[4], (K, C), dtype=jnp.float32) * scale
        norm_gamma = jnp.ones((C,), dtype=jnp.float32)
        norm_beta = jnp.zeros((C,), dtype=jnp.float32)
        return {'x': x, 'h_filter': h_filter, 'g_filter': g_filter, 'h_synth': h_synth, 'g_synth': g_synth, 'norm_gamma': norm_gamma, 'norm_beta': norm_beta}
    _L1_attn_in = _L1_attn_setup()

    def _L1_ffn_setup():
        import jax, jax.numpy as jnp
        import numpy as np
        CAPACITY_FACTOR = 1.25
        key = jax.random.key(seed)
        ks = jax.random.split(key, 6)
        B, S, H, E = (4, 1024, 256, 8)
        scale = 1.0 / np.sqrt(H)
        return {'tokens': jax.random.normal(ks[0], (B, S, H), dtype=jnp.float32), 'gate_w': jax.random.normal(ks[1], (E, H), dtype=jnp.float32) * scale, 'w1': jax.random.normal(ks[2], (E, H, H), dtype=jnp.float32) * scale, 'b1': jax.random.normal(ks[3], (E, H), dtype=jnp.float32) * 0.01, 'w2': jax.random.normal(ks[4], (E, H, H), dtype=jnp.float32) * scale, 'b2': jax.random.normal(ks[5], (E, H), dtype=jnp.float32) * 0.01}
    _L1_ffn_in = _L1_ffn_setup()
    _d = {'L0_attn_x': _L0_attn_in['x'], 'L0_attn_Wq': _L0_attn_in['Wq'], 'L0_attn_bq': _L0_attn_in['bq'], 'L0_attn_Wk': _L0_attn_in['Wk'], 'L0_attn_bk': _L0_attn_in['bk'], 'L0_attn_Wv': _L0_attn_in['Wv'], 'L0_attn_bv': _L0_attn_in['bv'], 'L0_attn_Wo': _L0_attn_in['Wo'], 'L0_attn_bo': _L0_attn_in['bo'], 'L0_ffn_w_gate': _L0_ffn_in['w_gate'], 'L0_ffn_W1': _L0_ffn_in['W1'], 'L0_ffn_b1': _L0_ffn_in['b1'], 'L0_ffn_W2': _L0_ffn_in['W2'], 'L0_ffn_b2': _L0_ffn_in['b2'], 'L1_attn_h_filter': _L1_attn_in['h_filter'], 'L1_attn_g_filter': _L1_attn_in['g_filter'], 'L1_attn_h_synth': _L1_attn_in['h_synth'], 'L1_attn_g_synth': _L1_attn_in['g_synth'], 'L1_attn_norm_gamma': _L1_attn_in['norm_gamma'], 'L1_attn_norm_beta': _L1_attn_in['norm_beta'], 'L1_ffn_gate_w': _L1_ffn_in['gate_w'], 'L1_ffn_w1': _L1_ffn_in['w1'], 'L1_ffn_b1': _L1_ffn_in['b1'], 'L1_ffn_w2': _L1_ffn_in['w2'], 'L1_ffn_b2': _L1_ffn_in['b2']}
    _x0 = _d['L0_attn_x']
    _d['L0_attn_x'] = jax.random.normal(jax.random.fold_in(jax.random.key(seed), 1), (4, 1024, 256), dtype=_x0.dtype)
    del _x0
    return _d

def reference(L0_attn_x, L0_attn_Wq, L0_attn_bq, L0_attn_Wk, L0_attn_bk, L0_attn_Wv, L0_attn_bv, L0_attn_Wo, L0_attn_bo, L0_ffn_w_gate, L0_ffn_W1, L0_ffn_b1, L0_ffn_W2, L0_ffn_b2, L1_attn_h_filter, L1_attn_g_filter, L1_attn_h_synth, L1_attn_g_synth, L1_attn_norm_gamma, L1_attn_norm_beta, L1_ffn_gate_w, L1_ffn_w1, L1_ffn_b1, L1_ffn_w2, L1_ffn_b2):

    def _L0_attn_ref(x, Wq, bq, Wk, bk, Wv, bv, Wo, bo):
        import jax, jax.numpy as jnp
        import numpy as np
        HEAD_NUM = 16
        B, S, D = x.shape
        H = HEAD_NUM
        hd = D // H

        def proj(W, b):
            return (x @ W.T + b).reshape(B, S, H, hd).transpose(0, 2, 1, 3)
        Q, K, V = (proj(Wq, bq), proj(Wk, bk), proj(Wv, bv))
        scale = 1.0 / jnp.sqrt(jnp.float32(hd))
        scores = jnp.einsum('bhqd,bhkd->bhqk', Q, K) * scale
        attn = jax.nn.softmax(scores, axis=-1)
        out = jnp.einsum('bhqk,bhkd->bhqd', attn, V)
        out = out.transpose(0, 2, 1, 3).reshape(B, S, D)
        return out @ Wo.T + bo

    def _L0_ffn_ref(x, w_gate, W1, b1, W2, b2):
        import jax, jax.numpy as jnp
        import numpy as np
        D_MODEL = 256
        N_EXPERTS = 8
        TOP_K = 2
        FFN_HIDDEN = 4 * D_MODEL
        B, S, D = x.shape
        flat_x = x.reshape(-1, D)
        gate = jax.nn.softmax(flat_x @ w_gate.T, axis=-1)
        topk_scores, topk_idx = jax.lax.top_k(gate, TOP_K)
        cw = (jax.nn.one_hot(topk_idx, N_EXPERTS, dtype=flat_x.dtype) * topk_scores[..., None]).sum(axis=1)
        h = jax.nn.gelu(jnp.einsum('td,edh->teh', flat_x, W1) + b1, approximate=False)
        y = jnp.einsum('teh,ehd->ted', h, W2) + b2
        out = jnp.einsum('ted,te->td', y, cw)
        return out.reshape(B, S, D)

    def _L1_attn_ref(x, h_filter, g_filter, h_synth, g_synth, norm_gamma, norm_beta):
        import jax, jax.numpy as jnp
        import numpy as np
        from jax import lax
        NUM_LEVELS = 2
        NUM_HEADS = 16
        LN_EPS = 1e-05
        ATTN_EPS = 1e-06

        def dwconv(x, filt):
            C = x.shape[-1]
            return lax.conv_general_dilated(x, filt[:, None, :], window_strides=(1,), padding='SAME', dimension_numbers=('NWC', 'WIO', 'NWC'), feature_group_count=C)

        def linear_attention(x, num_heads):
            B, N, C = x.shape
            d = C // num_heads
            h = x.reshape(B, N, num_heads, d)
            q = jax.nn.elu(h) + 1.0
            k = q
            v = h
            kv = jnp.einsum('bnhd,bnhe->bhde', k, v)
            z = k.sum(axis=1)
            num = jnp.einsum('bnhd,bhde->bnhe', q, kv)
            den = jnp.einsum('bnhd,bhd->bnh', q, z)[..., None] + ATTN_EPS
            return (num / den).reshape(B, N, C)

        def layer_norm(x, gamma, beta):
            mu = jnp.mean(x, axis=-1, keepdims=True)
            var = jnp.mean(jnp.square(x - mu), axis=-1, keepdims=True)
            return (x - mu) * lax.rsqrt(var + LN_EPS) * gamma + beta
        low = x
        highs = []
        lens = []
        for _ in range(NUM_LEVELS):
            lens.append(low.shape[1])
            l = dwconv(low, h_filter)[:, ::2]
            h = dwconv(low, g_filter)[:, ::2]
            highs.append(h)
            low = l
        low = linear_attention(low, NUM_HEADS)
        for h, L in zip(reversed(highs), reversed(lens)):
            up_l = jnp.repeat(low, 2, axis=1)[:, :L]
            up_h = jnp.repeat(h, 2, axis=1)[:, :L]
            low = dwconv(up_l, h_synth) + dwconv(up_h, g_synth)
        return layer_norm(x + low, norm_gamma, norm_beta)

    def _L1_ffn_ref(tokens, gate_w, w1, b1, w2, b2):
        import jax, jax.numpy as jnp
        import numpy as np
        CAPACITY_FACTOR = 1.25
        B, S, H = tokens.shape
        E = gate_w.shape[0]
        N = B * S
        cap = int(CAPACITY_FACTOR * N / E)
        x = tokens.reshape(N, H)
        probs = jax.nn.softmax(x @ gate_w.T, axis=-1)
        top2_w, top2_idx = jax.lax.top_k(probs, 2)
        a_e = top2_idx.reshape(-1)
        a_w = top2_w.reshape(-1)
        tok_id = jnp.arange(2 * N) // 2
        counts = jnp.bincount(a_e, length=E)
        keep = counts <= cap
        valid = keep[a_e]
        onehot = jax.nn.one_hot(a_e, E, dtype=jnp.int32)
        pos = jnp.take_along_axis(jnp.cumsum(onehot, axis=0) - 1, a_e[:, None], axis=1)[:, 0]
        p = jnp.where(valid, jnp.minimum(pos, cap - 1), cap)
        x_a = x[tok_id]
        buf = jnp.zeros((E, cap + 1, H), dtype=x.dtype).at[a_e, p].set(x_a)
        h = jax.nn.silu(jnp.einsum('ech,efh->ecf', buf, w1) + b1[:, None, :])
        y = jnp.einsum('ecf,egf->ecg', h, w2) + b2[:, None, :]
        contrib = y[a_e, p] * (a_w * valid.astype(x.dtype))[:, None]
        out = contrib.reshape(N, 2, H).sum(axis=1)
        return out.reshape(B, S, H)
    x = L0_attn_x
    x = _layernorm(x + _L0_attn_ref(x, L0_attn_Wq, L0_attn_bq, L0_attn_Wk, L0_attn_bk, L0_attn_Wv, L0_attn_bv, L0_attn_Wo, L0_attn_bo), axis=-1)
    x = _layernorm(x + _L0_ffn_ref(x, L0_ffn_w_gate, L0_ffn_W1, L0_ffn_b1, L0_ffn_W2, L0_ffn_b2), axis=-1)
    x = _layernorm(x + _L1_attn_ref(x, L1_attn_h_filter, L1_attn_g_filter, L1_attn_h_synth, L1_attn_g_synth, L1_attn_norm_gamma, L1_attn_norm_beta), axis=-1)
    x = _layernorm(x + _L1_ffn_ref(x, L1_ffn_gate_w, L1_ffn_w1, L1_ffn_b1, L1_ffn_w2, L1_ffn_b2), axis=-1)
    return x

_drawn_inputs = setup_inputs


def setup_inputs(seed=0):
    import zlib

    import numpy as np

    out = dict(_drawn_inputs(seed))
    spreads = {'L0_attn_bq': (0.0, 0.465),
     'L0_attn_bk': (0.0, 2.0),
     'L0_attn_bv': (0.0, 0.1),
     'L0_attn_bo': (0.0, 0.1),
     'L0_ffn_b1': (0.0, 0.1),
     'L0_ffn_b2': (0.0, 0.1),
     'L1_attn_norm_gamma': (1.0, 0.2),
     'L1_attn_norm_beta': (0.0, 0.1)}
    factors = {'L1_ffn_b1': 64.0, 'L1_ffn_b2': 48.402}
    for name, (base, spread) in spreads.items():
        noise = np.random.default_rng([zlib.crc32(name.encode()), seed]).standard_normal(out[name].shape)
        drawn = base * np.exp(spread * noise) if base else spread * noise
        out[name] = jnp.asarray(drawn.astype(out[name].dtype))
    for name, factor in factors.items():
        out[name] = (out[name] * factor).astype(out[name].dtype)
    return out
```

```python
from contextlib import ExitStack

import concourse.bass as bass
from concourse import mybir

FP32 = mybir.dt.float32
BF16 = mybir.dt.bfloat16
I32 = mybir.dt.int32
ALU = mybir.AluOpType
ACT = mybir.ActivationFunctionType
AX = mybir.AxisListType

P = 128
B, S, D = 4, 1024, 256
N = B * S
H, HD = 16, 16
KC = D // P
NT = N // P
TB = S // P
E = 8
NH = B * H
L1, L2 = S // 2, S // 4
HALF = 512
SCALE = float(HD) ** -0.5
PARTS = 3
STACK = 6 * HD
RING = 3
MAXROWS = 2
SLOTS = 4


class Mem:

    uses = {}

    def __init__(self, nc, stack):
        self.nc, self.stack, self.sems = nc, stack, []

    def clear(self):
        for sem in self.sems:
            self.nc.gpsimd.sem_clear(sem)

    @staticmethod
    def label(name):
        n = Mem.uses[name] = Mem.uses.get(name, -1) + 1
        return f"{name}_{n}" if n else name

    def sb(self, name, shape, dt=FP32):
        return self.stack.enter_context(self.nc.sbuf_tensor(self.label(name), shape, dt))

    def ps(self, name, shape=(P, HALF), dt=FP32):
        return self.stack.enter_context(self.nc.psum_tensor(self.label(name), list(shape), dt))

    def sem(self, name):
        self.sems.append(self.stack.enter_context(self.nc.semaphore(self.label(name))))
        return self.sems[-1]


def wait_from(eng, sem, value):
    if not isinstance(value, int) or value > 0:
        eng.wait_ge(sem, value)


def wait_apart(eng, spare, sem, value):
    if not isinstance(value, int) or value > 0:
        eng.wait_ge(sem, value)
        eng.sem_inc(spare, 1)


def row_stats(nc, c, i):
    nc.vector.bn_stats(c.six[:, bass.ds(i, 1), :].rearrange("p a d -> p (a d)"),
                       c.y[:, bass.ds(i, 1), :].rearrange("p a d -> p (a d)"))


def peeled(eng, count, body):
    body(0)
    with eng.Fori(1, count) as i:
        body(i)


def peeled_ends(eng, count, body):
    body(0, True, False)
    with eng.Fori(1, count - 1) as i:
        body(i, False, False)
    body(count - 1, False, True)


def stage_constants(nc, mem, c):
    c.ident = mem.sb("ident", [P, P])
    c.identb = mem.sb("identb", [P, P], BF16)
    c.fold = mem.sb("fold", [P, 2 * 32])
    zeroed, made = mem.sem("consts_zeroed"), mem.sem("consts_made")
    with nc.Block() as block:
        @block.gpsimd
        def _(pool):
            nc.gpsimd.memset(c.ident[:, :], 0.0).then_inc(zeroed, 1)
            nc.gpsimd.memset(c.identb[:, :], 0.0).then_inc(zeroed, 1)
            nc.gpsimd.memset(c.fold[:, :], 0.0).then_inc(zeroed, 1)
            pool.wait_ge(zeroed, 3)
            for m in (c.ident, c.identb):
                nc.gpsimd.affine_select(out=m[:, :], in_=m[:, :], compare_op=ALU.not_equal, fill=1.0, base=0,
                                        pattern=[[-1, P]], channel_multiplier=1).then_inc(made, 1)
            fold = c.fold[:, :].rearrange("p (q r) -> p q r", q=2)
            for kh in range(2):
                pool.wait_ge(made, 2 + kh)
                nc.gpsimd.affine_select(out=fold, in_=fold, compare_op=ALU.not_equal, fill=1.0, base=-32 * kh,
                                        pattern=[[-64, 2], [-1, 32]], channel_multiplier=1).then_inc(made, 1)


def stage_project(nc, outer, a, c):
    CH = HALF
    with ExitStack() as stack:
        mem = Mem(nc, stack)
        w = mem.sb("w_qkv", [P, KC, 3 * D])
        bias = mem.sb("b_qk", [P, 2, KC])
        bv = mem.sb("bv_all", [P, D])
        xt = [mem.sb(f"xt{u}", [P, KC, CH]) for u in range(2)]
        full = [mem.sb(f"qk_full{u}", [P, CH]) for u in range(2)]
        part = [mem.sb(f"qk_part{u}", [P, PARTS, CH], BF16) for u in range(4)]
        rest = [mem.sb(f"qk_rest{u}", [P, CH]) for u in range(2)]
        pq = [mem.ps(f"ps_qk{u}") for u in range(4)]
        pv = [mem.ps(f"ps_v{u}") for u in range(4)]
        loaded_w = mem.sem("a_weights")
        loaded_x = [mem.sem(f"a_x{u}") for u in range(2)]
        qk_ready, v_ready = mem.sem("a_qk_ready"), mem.sem("a_v_ready")
        full_ready, part1_ready = mem.sem("a_full"), mem.sem("a_part1")
        rest_ready, part2_ready, part3_ready = mem.sem("a_rest"), mem.sem("a_part2"), mem.sem("a_part3")
        v_done = mem.sem("a_v_done")
        spare_p = mem.sem("a_spare")
        stored = [mem.sem(f"a_stored{u}") for u in range(4)]
        with nc.Block() as block:
            @block.sync
            def _(sp):
                sp.dma_start(w[:, :, :], a.wqkv.rearrange("(c p) n -> p c n", p=P)).then_inc(loaded_w, 16)
                sp.dma_start(bias[:, :, :], a.bqk).then_inc(loaded_w, 16)
                sp.dma_start(bv[:, :], a.bv.partition_broadcast(P)).then_inc(loaded_w, 16)

                def store(b):
                    for u in range(2):
                        for m in range(4):
                            sp.wait_ge(part3_ready, b * 8 + 4 * u + m + 1)
                            dst = (c.q_parts, c.k_parts)[m // 2]
                            sp.dma_start(
                                dst[bass.ds(b * H + (m % 2) * 8, 8), :, :, u * CH:(u + 1) * CH]
                                .rearrange("h r s t -> (h r) s t"), part[m][:, :, :]).then_inc(stored[m], 16)
                peeled(sp, B, store)
                for m in range(4):
                    sp.wait_ge(stored[m], 16 * 2 * B)

            @block.tensor
            def _(pe):
                pe.wait_ge(loaded_w, 48)

                def products(b):
                    for u in range(2):
                        pe.wait_ge(loaded_x[u], b * 16 + 16)
                        for m in range(4):
                            wait_from(pe, part1_ready, b * 8 + 4 * u + m - 3)
                            for k in range(KC):
                                mm = nc.tensor.matmul(pq[m][:, :], w[:, k, m * P:(m + 1) * P], xt[u][:, k, :],
                                                      start=(k == 0), stop=(k == KC - 1))
                            mm.then_inc(qk_ready, 1)
                        for t in range(4):
                            wait_from(pe, v_done, b * 8 + 4 * u + t - 3)
                            for k in range(KC):
                                mm = nc.tensor.matmul(pv[t][:, 0:D], xt[u][:, k, t * P:(t + 1) * P],
                                                      w[:, k, 2 * D:3 * D], start=(k == 0), stop=(k == KC - 1))
                            mm.then_inc(v_ready, 1)
                peeled(pe, B, products)

            @block.scalar
            def _(act):
                def evacuate(b):
                    for u in range(2):
                        wait_from(act, v_ready, b * 8 + 4 * u - 4)
                        act.dma_start(xt[u][:, :, :], a.xt[:, bass.ds(b * S + u * CH, CH)]
                                      .rearrange("(c p) n -> p c n", p=P)).then_inc(loaded_x[u], 16)
                        for m in range(4):
                            i = b * 8 + 4 * u + m
                            act.wait_ge(qk_ready, i + 1)
                            wait_from(act, rest_ready, i - 1)
                            nc.scalar.activation(full[m % 2][:, :], pq[m][:, :], ACT.Identity,
                                                 bias=bias[:, m // 2, m % 2:m % 2 + 1]).then_inc(full_ready, 1)
                            wait_from(act, stored[m], b * 32 + 16 * u)
                            nc.scalar.activation(part[m][:, 0, :], pq[m][:, :], ACT.Identity,
                                                 bias=bias[:, m // 2, m % 2:m % 2 + 1]).then_inc(part1_ready, 1)
                act.wait_ge(loaded_w, 48)
                peeled(act, B, evacuate)

            @block.gpsimd
            def _(pool):
                def second(b):
                    for u in range(2):
                        for m in range(4):
                            wait_apart(pool, spare_p, rest_ready, b * 8 + 4 * u + m + 1)
                            nc.gpsimd.tensor_copy(part[m][:, 1, :], rest[m % 2][:, :]).then_inc(part2_ready, 1)
                peeled(pool, B, second)

            @block.vector
            def _(dve):
                def split(b):
                    for u in range(2):
                        for m in range(4):
                            i = b * 8 + 4 * u + m
                            dve.wait_ge(part1_ready, i + 1)
                            nc.vector.tensor_tensor(rest[m % 2][:, :], full[m % 2][:, :], part[m][:, 0, :],
                                                    ALU.subtract).then_inc(rest_ready, 1)
                            dve.wait_ge(part2_ready, i + 1)
                            nc.vector.tensor_tensor(part[m][:, 2, :], rest[m % 2][:, :], part[m][:, 1, :],
                                                    ALU.subtract).then_inc(part3_ready, 1)
                        for t in range(4):
                            dve.wait_ge(v_ready, b * 8 + 4 * u + t + 1)
                            nc.vector.tensor_tensor(
                                c.v[:, bass.ds(b * H, H), u * 4 + t, :],
                                pv[t][:, 0:D].rearrange("p (h r) -> p h r", h=H),
                                bv[:, :].rearrange("p (h r) -> p h r", h=H), ALU.add).then_inc(v_done, 1)
                dve.wait_ge(loaded_w, 48)
                peeled(dve, B, split)
        mem.clear()


def stage_attention(nc, outer, a, c):
    KT = TB
    with ExitStack() as stack:
        mem = Mem(nc, stack)
        qs = mem.sb("q_stack", [STACK + MAXROWS, SLOTS, S], BF16)
        ks = mem.sb("k_stack", [STACK + MAXROWS, SLOTS, S], BF16)
        pt = c.probs
        vpad = [mem.sb(f"v_padded{u}", [P, KT, 32]) for u in range(2)]
        o_sb = mem.sb("o_transposed", [P, HALF])
        unit_max = mem.sb("unit_max", [P, 2, 2, KT])
        best = [mem.sb(f"row_max{u}", [P, KT]) for u in range(2)]
        neg = mem.sb("neg_max", [P, KT])
        negp = [mem.sb(f"neg_parts{u}", [P, MAXROWS, KT], BF16) for u in range(2)]
        negt = [mem.sb(f"neg_rows{u}", [MAXROWS * KT, P], BF16) for u in range(2)]
        rec = mem.sb("o_reciprocal", [P, 2, 4])
        p_s = [mem.ps(f"ps_scores{u}", (P, S)) for u in range(2)]
        ring = [mem.ps(f"ps_ring{u}") for u in range(RING)]
        p_o = mem.ps("ps_o")
        slot_loaded = [mem.sem(f"b_slot{u}") for u in range(SLOTS)]
        LOADS, ROWS = 6 * 16, 7 * 16
        spare_p = mem.sem("b_spare")
        init = mem.sem("b_init")
        scores_ready, exp_done = mem.sem("b_scores"), mem.sem("b_exp")
        ring_ready, ring_used = mem.sem("b_ring_ready"), mem.sem("b_ring_used")
        best_done = mem.sem("b_best_done")
        neg_order, parts_done = mem.sem("b_neg_order"), mem.sem("b_parts")
        v_copied, pv_done, o_copied = mem.sem("b_v"), mem.sem("b_pv"), mem.sem("b_o")
        rec_done = mem.sem("b_rec")
        GROUPS = NH // SLOTS
        FOLD_AT, ROWS_AT = 4, 2

        def units(first, last, u):
            for kt in range(KT):
                if not (last and u >= 2):
                    yield kt, "max0"
                if kt == ROWS_AT and not (last and u == SLOTS - 1):
                    yield kt, "rows"
                if not (last and u >= 2):
                    yield kt, "max1"
                if kt == FOLD_AT and not (first and u == 0):
                    yield kt, "fold"

        PROLOGUE = 2 * 2 * KT + 1
        PER_GROUP = SLOTS * (2 * KT + 2)
        assert PER_GROUP % RING == 0

        def count_before(g, first, last, u):
            inside = sum(len(list(units(first, last, w))) for w in range(u))
            if first:
                return PROLOGUE + inside
            return g * PER_GROUP + (PROLOGUE - 1 + inside)

        def bank(g, first, last, u, j):
            base = PROLOGUE if first else PROLOGUE - 1
            return ring[(base + sum(len(list(units(first, last, w))) for w in range(u)) + j) % RING]


        def groups(eng, body):
            peeled_ends(eng, GROUPS, body)

        with nc.Block() as block:
            @block.sync
            def _(sp):
                def load(g, u):
                    for dst, src, deep in ((qs, c.q_parts, True), (ks, c.k_parts, False)):
                        at = 0
                        for n in (3, 2, 1):
                            if deep:
                                rows = src[bass.ds(g * SLOTS + u, 1), :, 0:n, :]
                                rows = rows.rearrange("h r s t -> (h r) s t")
                            else:
                                rows = src[bass.ds(g * SLOTS + u, 1), :, 3 - n:4 - n, :]
                                rows = rows.rearrange("h r s t -> (h r) s t").to_broadcast([HD, n, S])
                            sp.dma_start(dst[at:at + n * HD, u, :], rows).then_inc(slot_loaded[u], 16)
                            at += n * HD
                for u in range(3):
                    load(0, u)

                def rows(u, at):
                    sp.wait_ge(ring_used, at + 1)
                    sp.dma_start(qs[STACK:STACK + MAXROWS, u, :].rearrange("s (t q) -> s t q", t=KT),
                                 negt[u % 2][:, :]).then_inc(slot_loaded[u], 16)

                def body(g, first, last):
                    for u in range(SLOTS):
                        if first and u == 0:
                            rows(0, PROLOGUE - 1)
                        if not (last and u > 0):
                            wait_from(sp, scores_ready, (g * SLOTS + u) * KT)
                            load(g + (1 if u > 0 else 0), (u + 3) % SLOTS)
                        for j, (_, kind) in enumerate(units(first, last, u)):
                            if kind == "rows":
                                rows((u + 1) % SLOTS, count_before(g, first, last, u) + j)
                groups(sp, body)

            @block.gpsimd
            def _(pool):
                nc.gpsimd.memset(ks[STACK:STACK + MAXROWS, :, :], 1.0).then_inc(init, 1)
                for j, v in enumerate(vpad):
                    pool.wait_ge(init, 2 * j + 1)
                    nc.gpsimd.memset(v[:, :, HD:HD + 1], 1.0).then_inc(init, 1)
                    pool.wait_ge(init, 2 * j + 2)
                    nc.gpsimd.memset(v[:, :, HD + 1:32], 0.0).then_inc(init, 1)
                pool.wait_ge(init, 5)

                def negate(n, u):
                    wait_apart(pool, spare_p, parts_done, n)
                    wait_apart(pool, spare_p, best_done, n + 1)
                    nc.gpsimd.tensor_scalar(neg[:, :], best[u % 2][:, :], -1.0, None, ALU.mult).then_inc(neg_order, 1)
                    wait_apart(pool, spare_p, neg_order, n * 2 + 1)
                    nc.gpsimd.tensor_copy(negp[u % 2][:, 0, :], neg[:, :]).then_inc(neg_order, 1)
                    wait_apart(pool, spare_p, neg_order, n * 2 + 2)
                    nc.gpsimd.tensor_tensor(negp[u % 2][:, 1, :], neg[:, :], negp[u % 2][:, 0, :],
                                            ALU.subtract).then_inc(parts_done, 1)

                for u in range(2):
                    negate(u, u)

                def body(g, first, last):
                    for u in range(SLOTS):
                        n = g * SLOTS + u
                        wait_apart(pool, spare_p, pv_done, (n - 1) * 4)
                        nc.gpsimd.tensor_copy(vpad[u % 2][:, :, 0:HD], c.v[:, bass.ds(n, 1), :, :]
                                              .rearrange("p h t r -> p (h t) r")).then_inc(v_copied, 1)
                        if not (last and u >= 2):
                            negate(n + 2, u)
                groups(pool, body)

            @block.tensor
            def _(pe):
                def claim(at):
                    wait_from(pe, ring_used, at - RING + 1)

                def max_unit(u, qt, half, at, out):
                    claim(at)
                    nc.tensor.matmul(out[:, :], qs[0:STACK, u, qt * P:(qt + 1) * P],
                                     ks[0:STACK, u, half * HALF:(half + 1) * HALF],
                                     start=True, stop=True).then_inc(ring_ready, 1)

                def rows_unit(n, u, at, out):
                    pe.wait_ge(parts_done, n + 1)
                    claim(at)
                    nc.tensor.transpose(out[0:MAXROWS * KT, 0:P // 2].bitcast(BF16),
                                        negp[u % 2][:, :, :].rearrange("p s t -> p (s t)"),
                                        c.identb[:, :]).then_inc(ring_ready, 1)

                def pv(n, u, i):
                    pe.wait_ge(exp_done, n * KT + 2 * i + 2)
                    if i == 0:
                        pe.wait_ge(v_copied, n + 1)
                        wait_from(pe, o_copied, n)
                    for kh in range(2):
                        for qh in range(2):
                            j = 2 * qh + kh
                            mm = nc.tensor.matmul(p_o[32 * j:32 * j + 32, :], vpad[u % 2][:, 2 * i + kh, :],
                                                  pt[:, 2 * i + kh, qh * HALF:(qh + 1) * HALF],
                                                  start=(i == 0), stop=(i == KT // 2 - 1))
                    mm.then_inc(pv_done, 1)

                def fold_unit(n, at, out):
                    pe.wait_ge(o_copied, n + 1)
                    claim(at)
                    for blk in range(4):
                        mm = nc.tensor.matmul(out[:, blk * 64:(blk + 1) * 64], o_sb[:, blk * P:(blk + 1) * P],
                                              c.fold[:, :], start=True, stop=True)
                    mm.then_inc(ring_ready, 1)

                pe.wait_ge(init, 5)
                for u in range(2):
                    pe.wait_ge(slot_loaded[u], LOADS)
                    for m in range(2 * KT):
                        at = u * 2 * KT + m
                        max_unit(u, m // 2, m % 2, at, ring[at % RING])
                rows_unit(0, 0, PROLOGUE - 1, ring[(PROLOGUE - 1) % RING])

                def body(g, first, last):
                    for u in range(SLOTS):
                        n = g * SLOTS + u
                        ahead = not (last and u >= 2)
                        before = count_before(g, first, last, u)
                        todo = list(enumerate(units(first, last, u)))

                        def emit(kt, kinds):
                            for j, (step, kind) in todo:
                                if step != kt or kind not in kinds:
                                    continue
                                at, out = before + j, bank(g, first, last, u, j)
                                if kind == "rows":
                                    rows_unit(n + 1, u + 1, at, out)
                                elif kind == "fold":
                                    fold_unit(n - 1, at, out)
                                else:
                                    max_unit((u + 2) % SLOTS, kt, int(kind[3]), at, out)
                        for kt in range(KT):
                            if kt == 0:
                                pe.wait_ge(slot_loaded[u], g * ROWS + ROWS)
                                if ahead:
                                    pe.wait_ge(slot_loaded[(u + 2) % SLOTS], (g + (u >= 2)) * ROWS + LOADS)
                            emit(kt, ("max0",))
                            wait_from(pe, exp_done, n * KT + kt - 1)
                            for half in range(2):
                                mm = nc.tensor.matmul(p_s[kt % 2][:, half * HALF:(half + 1) * HALF],
                                                      ks[:, u, kt * P:(kt + 1) * P],
                                                      qs[:, u, half * HALF:(half + 1) * HALF],
                                                      start=True, stop=True)
                            mm.then_inc(scores_ready, 1)
                            emit(kt, ("rows", "max1"))
                            if kt == 1 and not (first and u == 0):
                                pv(n - 1, u + 1, KT // 2 - 1)
                            if kt in (3, 5, 7):
                                pv(n, u, (kt - 3) // 2)
                            emit(kt, ("fold",))
                groups(pe, body)
                pv(NH - 1, SLOTS - 1, KT // 2 - 1)
                end = count_before(GROUPS - 1, False, True, SLOTS)
                fold_unit(NH - 1, end, bank(GROUPS - 1, False, True, SLOTS, 0))

            @block.scalar
            def _(act):
                def copy_o(n, units_before):
                    act.wait_ge(pv_done, (n + 1) * (KT // 2))
                    act.wait_ge(ring_ready, units_before)
                    nc.scalar.activation(o_sb[:, :], p_o[:, :], ACT.Copy).then_inc(o_copied, 1)

                def body(g, first, last):
                    for u in range(SLOTS):
                        n = g * SLOTS + u
                        for kt in range(KT):
                            act.wait_ge(scores_ready, n * KT + kt + 1)
                            if kt % 2 == 0:
                                wait_from(act, pv_done, (n - 1) * (KT // 2) + kt // 2 + 1)
                            nc.scalar.activation(pt[:, kt, :], p_s[kt % 2][:, :], ACT.Exp, scale=SCALE)\
                                .then_inc(exp_done, 1)
                            if kt == 1 and not (first and u == 0):
                                copy_o(n - 1, count_before(g, first, last, u))
                groups(act, body)
                copy_o(NH - 1, count_before(GROUPS - 1, False, True, SLOTS))

            @block.vector
            def _(dve):
                def reduce_unit(n, u, qt, half, at, src):
                    if half == 0 and qt == 0:
                        wait_from(dve, best_done, n - 1)
                    dve.wait_ge(ring_ready, at + 1)
                    nc.vector.tensor_reduce(unit_max[:, u % 2, half, qt:qt + 1], src[:, :], axis=AX.X,
                                            op=ALU.max).then_inc(ring_used, 1)

                def combine(n, u, at):
                    dve.wait_ge(ring_used, at + 1)
                    wait_from(dve, parts_done, n - 1)
                    nc.vector.tensor_tensor(best[u % 2][:, :], unit_max[:, u % 2, 0, :], unit_max[:, u % 2, 1, :],
                                            ALU.max).then_inc(best_done, 1)

                def copy_rows(u, at, src):
                    dve.wait_ge(ring_ready, at + 1)
                    nc.vector.tensor_copy(negt[u % 2][:, :], src[0:MAXROWS * KT, 0:P // 2].bitcast(BF16))\
                        .then_inc(ring_used, 1)

                def normalise(n, at, src):
                    dve.wait_ge(ring_ready, at + 1)
                    wait_from(dve, ring_used, at)
                    o = src[:, 0:256].rearrange("p (b q r) -> p q b r", b=4, q=2)
                    nc.vector.reciprocal(rec[:, :, :], o[:, :, :, HD]).then_inc(rec_done, 1)
                    dve.wait_ge(rec_done, n + 1)
                    nc.vector.tensor_tensor(
                        c.ao[:, bass.ds(n, 1), :, :].rearrange("p h (q b) r -> p (h q) b r", q=2),
                        o[:, :, :, 0:HD], rec[:, :, :].unsqueeze(3).to_broadcast([P, 2, 4, HD]),
                        ALU.mult).then_inc(ring_used, 1)

                for u in range(2):
                    for m in range(2 * KT):
                        at = u * 2 * KT + m
                        reduce_unit(u, u, m // 2, m % 2, at, ring[at % RING])
                    combine(u, u, at)
                copy_rows(0, PROLOGUE - 1, ring[(PROLOGUE - 1) % RING])

                def body(g, first, last):
                    for u in range(SLOTS):
                        n = g * SLOTS + u
                        before = count_before(g, first, last, u)
                        for j, (kt, kind) in enumerate(units(first, last, u)):
                            at, src = before + j, bank(g, first, last, u, j)
                            if kind == "rows":
                                copy_rows(u + 1, at, src)
                            elif kind == "fold":
                                normalise(n - 1, at, src)
                            else:
                                reduce_unit(n + 2, u, kt, int(kind[3]), at, src)
                                if kt == KT - 1 and kind == "max1":
                                    combine(n + 2, u, at)
                groups(dve, body)
                end = count_before(GROUPS - 1, False, True, SLOTS)
                normalise(NH - 1, end, bank(GROUPS - 1, False, True, SLOTS, 0))
        mem.clear()


class Chain:

    def __init__(self, eng, sem):
        self.eng, self.sem, self.count = eng, sem, 0

    def __call__(self, instruction):
        instruction.then_inc(self.sem, 1)
        self.count += 1
        self.eng.wait_ge(self.sem, self.count)


def bcast(ap, shape):
    return ap.to_broadcast(shape)


def stage_output(nc, outer, a, c):
    with ExitStack() as stack:
        mem = Mem(nc, stack)
        wo = mem.sb("w_o", [P, KC, D])
        bo = mem.sb("bo_all", [P, D])
        xin = [mem.sb(f"c_x{u}", [P, D]) for u in range(2)]
        at = [mem.sb(f"c_attn{u}", [P, D]) for u in range(2)]
        ot = [mem.sb(f"c_attn_t{u}", [P, KC, P]) for u in range(2)]
        p_tr = [mem.ps(f"c_ps_t{u}") for u in range(2)]
        p_y = [mem.ps(f"c_ps_y{u}") for u in range(2)]
        loaded_w = mem.sem("c_weights")
        loaded_x = [mem.sem(f"c_loaded_x{u}") for u in range(2)]
        staged, bias_added = mem.sem("c_staged"), mem.sem("c_bias")
        turned, copied, made = mem.sem("c_turned"), mem.sem("c_copied"), mem.sem("c_made")
        summed, spare, spare_p = mem.sem("c_summed"), mem.sem("c_spare"), mem.sem("c_spare_pool")
        ao = c.ao.rearrange("p (b h) t r -> p b h t r", b=B)
        with nc.Block() as block:
            @block.sync
            def _(sp):
                sp.dma_start(wo[:, :, :], a.wo.rearrange("(c p) n -> p c n", p=P)).then_inc(loaded_w, 16)
                sp.dma_start(bo[:, :], a.bo.partition_broadcast(P)).then_inc(loaded_w, 16)

                def load(b):
                    for t in range(TB):
                        wait_from(sp, summed, b * TB + t - 1)
                        sp.dma_start(xin[t % 2][:, :], a.x[bass.ds(b * S + t * P, P), :]).then_inc(loaded_x[t % 2], 16)
                peeled(sp, B, load)

            @block.gpsimd
            def _(pool):
                def stage(b):
                    for t in range(TB):
                        wait_apart(pool, spare_p, turned, b * TB + t - 1)
                        nc.gpsimd.tensor_copy(at[t % 2][:, :].rearrange("p (h r) -> p h r", h=H),
                                              ao[:, bass.ds(b, 1), :, t, :].rearrange("p b h r -> p (b h) r"))\
                            .then_inc(staged, 1)
                        wait_apart(pool, spare_p, loaded_x[t % 2], b * 64 + (t // 2) * 16 + 16)
                        nc.gpsimd.tensor_tensor(xin[t % 2][:, :], xin[t % 2][:, :], bo[:, :], ALU.add)\
                            .then_inc(bias_added, 1)
                pool.wait_ge(loaded_w, 32)
                peeled(pool, B, stage)

            @block.tensor
            def _(pe):
                def turn(b, t):
                    pe.wait_ge(staged, b * TB + t + 1)
                    wait_from(pe, copied, b * TB + t - 1)
                    for k in range(KC):
                        mm = nc.tensor.transpose(p_tr[t % 2][:, k * P:(k + 1) * P], at[t % 2][:, k * P:(k + 1) * P],
                                                 c.ident[:, :])
                    mm.then_inc(turned, 1)

                def product(b, t):
                    pe.wait_ge(copied, b * TB + t + 1)
                    wait_from(pe, summed, b * TB + t - 1)
                    for k in range(KC):
                        mm = nc.tensor.matmul(p_y[t % 2][:, 0:D], ot[t % 2][:, k, :], wo[:, k, :],
                                              start=(k == 0), stop=(k == KC - 1))
                    mm.then_inc(made, 1)

                def tiles(b):
                    turn(b, 0)
                    for t in range(TB):
                        if t + 1 < TB:
                            turn(b, t + 1)
                        product(b, t)
                pe.wait_ge(loaded_w, 32)
                peeled(pe, B, tiles)

            @block.scalar
            def _(act):
                def copy(b):
                    for t in range(TB):
                        act.wait_ge(turned, b * TB + t + 1)
                        wait_from(act, made, b * TB + t - 1)
                        nc.scalar.activation(ot[t % 2][:, :, :].rearrange("p c n -> p (c n)"),
                                             p_tr[t % 2][:, 0:D], ACT.Copy).then_inc(copied, 1)
                peeled(act, B, copy)

            @block.vector
            def _(dve):
                def add(b):
                    for t in range(TB):
                        i = b * TB + t
                        dve.wait_ge(made, i + 1)
                        dve.wait_ge(bias_added, i + 1)
                        nc.vector.tensor_tensor(c.y[:, bass.ds(i, 1), :].rearrange("p a d -> p (a d)"),
                                                p_y[t % 2][:, 0:D], xin[t % 2][:, :], ALU.add).then_inc(summed, 1)
                        wait_apart(dve, spare, summed, i + 1)
                        row_stats(nc, c, i)
                peeled(dve, B, add)
        mem.clear()


def stage_load_stats(nc, outer, c, src):
    with ExitStack() as stack:
        mem = Mem(nc, stack)
        loaded = [mem.sem(f"l_loaded{b}") for b in range(B)]
        rows = src.rearrange("(i p) d -> p i d", p=P)
        with nc.Block() as block:
            @block.sync
            def _(sp):
                for b in range(B):
                    sp.dma_start(c.y[:, b * TB:(b + 1) * TB, :], rows[:, b * TB:(b + 1) * TB, :])\
                        .then_inc(loaded[b], 16)

            @block.vector
            def _(dve):
                for b in range(B):
                    dve.wait_ge(loaded[b], 16)
                with dve.Fori(0, B) as b:
                    for t in range(TB):
                        i = b * TB + t
                        row_stats(nc, c, i)
        mem.clear()


def stage_rstd(nc, outer, c):
    with ExitStack() as stack:
        mem = Mem(nc, stack)
        var = mem.sb("r_var", [P, NT])
        root = mem.sb("r_root", [P, NT])
        tmp = mem.sb("r_tmp", [P, NT])
        mean = mem.sb("r_mean", [P, NT])
        var_ready, root_ready, order = mem.sem("r_var_ready"), mem.sem("r_root_ready"), mem.sem("r_order")
        with nc.Block() as block:
            @block.vector
            def _(dve):
                link = Chain(dve, order)
                even, odd = c.six[:, :, 1], c.six[:, :, 4]
                link(nc.vector.tensor_tensor(mean[:, :], even, odd, ALU.add))
                link(nc.vector.tensor_scalar(mean[:, :], mean[:, :], 0.5, None, ALU.mult))
                link(nc.vector.tensor_tensor(tmp[:, :], even, mean[:, :], ALU.subtract))
                link(nc.vector.tensor_tensor(tmp[:, :], tmp[:, :], tmp[:, :], ALU.mult))
                link(nc.vector.tensor_tensor(var[:, :], c.six[:, :, 2], c.six[:, :, 5], ALU.add))
                link(nc.vector.scalar_tensor_tensor(out=var[:, :], in0=var[:, :], scalar=1.0 / D, in1=tmp[:, :],
                                                    op0=ALU.mult, op1=ALU.add))
                nc.vector.tensor_scalar(var[:, :], var[:, :], 1e-5, None, ALU.add).then_inc(var_ready, 1)
                dve.wait_ge(root_ready, 1)
                link(nc.vector.reciprocal(c.rstd[:, :], root[:, :]))
                link(nc.vector.tensor_tensor(tmp[:, :], c.rstd[:, :], c.rstd[:, :], ALU.mult))
                link(nc.vector.tensor_tensor(tmp[:, :], tmp[:, :], var[:, :], ALU.mult))
                link(nc.vector.tensor_scalar(tmp[:, :], tmp[:, :], -0.5, 1.5, ALU.mult, ALU.add))
                link(nc.vector.tensor_tensor(c.rstd[:, :], c.rstd[:, :], tmp[:, :], ALU.mult))
                link(nc.vector.scalar_tensor_tensor(out=c.nmr[:, :], in0=mean[:, :], scalar=-1.0,
                                                    in1=c.rstd[:, :], op0=ALU.mult, op1=ALU.mult))

            @block.scalar
            def _(act):
                act.wait_ge(var_ready, 1)
                nc.scalar.activation(root[:, :], var[:, :], ACT.Sqrt).then_inc(root_ready, 1)
        mem.clear()


def normalised(nc, c, out, i):
    return nc.vector.tensor_scalar(out, c.y[:, bass.ds(i, 1), :].rearrange("p a d -> p (a d)"),
                                   c.rstd[:, bass.ds(i, 1)], c.nmr[:, bass.ds(i, 1)], ALU.mult, ALU.add)


def stage_gate(nc, outer, c, wgate, rows, sums):
    with ExitStack() as stack:
        mem = Mem(nc, stack)
        wg = mem.sb("g_w", [P, KC, E])
        st = [mem.sb(f"g_tile{u}", [P, D]) for u in range(2)]
        xt = [mem.sb(f"g_tile_t{u}", [P, KC, P]) for u in range(2)]
        p_tr = [mem.ps(f"g_ps_t{u}") for u in range(2)]
        p_g = mem.ps("g_ps_logits")
        loaded_w = mem.sem("g_weights")
        ready, turned, copied, gated = mem.sem("g_ready"), mem.sem("g_turned"), mem.sem("g_copied"), mem.sem("g_gated")
        stored = [mem.sem(f"g_stored{u}") for u in range(2)]
        done = mem.sem("g_done")
        with nc.Block() as block:
            @block.sync
            def _(sp):
                sp.dma_start(wg[:, :, :], wgate.rearrange("(c p) e -> p c e", p=P)).then_inc(loaded_w, 16)

                def store(b):
                    for t in range(TB):
                        sp.wait_ge(ready, b * TB + t + 1)
                        for dst in (rows, sums):
                            sp.dma_start(dst[bass.ds(b * S + t * P, P), :], st[t % 2][:, :]).then_inc(stored[t % 2], 16)
                peeled(sp, B, store)
                for u in range(2):
                    sp.wait_ge(stored[u], 16 * NT)

            @block.vector
            def _(dve):
                def norm(b):
                    for t in range(TB):
                        wait_from(dve, turned, b * TB + t - 1)
                        wait_from(dve, stored[t % 2], b * 128 + (t // 2) * 32)
                        normalised(nc, c, st[t % 2][:, :], b * TB + t).then_inc(ready, 1)
                peeled(dve, B, norm)
                dve.wait_ge(gated, NT)
                nc.vector.tensor_copy(c.logits[:, :], p_g[:, 0:NT * E]).then_inc(done, 1)

            @block.tensor
            def _(pe):
                def turn(b, t):
                    pe.wait_ge(ready, b * TB + t + 1)
                    wait_from(pe, copied, b * TB + t - 1)
                    for k in range(KC):
                        mm = nc.tensor.transpose(p_tr[t % 2][:, k * P:(k + 1) * P], st[t % 2][:, k * P:(k + 1) * P],
                                                 c.ident[:, :])
                    mm.then_inc(turned, 1)

                def gate(b, t):
                    pe.wait_ge(copied, b * TB + t + 1)
                    for k in range(KC):
                        mm = nc.tensor.matmul(p_g[:, bass.ds((b * TB + t) * E, E)], xt[t % 2][:, k, :], wg[:, k, :],
                                              start=(k == 0), stop=(k == KC - 1))
                    mm.then_inc(gated, 1)

                def tiles(b):
                    turn(b, 0)
                    for t in range(TB):
                        if t + 1 < TB:
                            turn(b, t + 1)
                        gate(b, t)
                pe.wait_ge(loaded_w, 16)
                peeled(pe, B, tiles)

            @block.scalar
            def _(act):
                def copy(b):
                    for t in range(TB):
                        act.wait_ge(turned, b * TB + t + 1)
                        wait_from(act, gated, b * TB + t - 1)
                        nc.scalar.activation(xt[t % 2][:, :, :].rearrange("p c n -> p (c n)"),
                                             p_tr[t % 2][:, 0:D], ACT.Copy).then_inc(copied, 1)
                peeled(act, B, copy)
        mem.clear()


def stage_route(nc, outer, c, tiles, fixed):
    with ExitStack() as stack:
        mem = Mem(nc, stack)
        G = NT * E
        names = ("ex", "pr", "pr2", "eq", "cand", "oh1", "oh2", "mask", "incl", "pos", "prod")
        t = {n: mem.sb(f"e_{n}", [P, NT, E]) for n in names}
        maskb = mem.sb("e_maskb", [P, G], BF16)
        tri = mem.sb("e_tri", [P, P], BF16)
        ones = mem.sb("e_ones", [P, P], BF16)
        totals = mem.sb("e_totals", [P, NT, E])
        unit = mem.sb("e_unit", [P, NT])
        iota_e = mem.sb("e_iota_e", [P, E])
        iota_p = mem.sb("e_iota_p", [P, P])
        iota_t = mem.sb("e_iota_t", [P, tiles])
        token = mem.sb("e_token", [P, NT])
        small = {n: mem.sb(f"e_{n}", [P, NT]) for n in ("mx", "sm", "rc", "w1", "w2", "cm", "slot")}
        sloti = mem.sb("e_sloti", [P, NT], I32)
        hi_i = mem.sb("e_hi_i", [P, NT], I32)
        hi = mem.sb("e_hi", [P, 2, NT])
        lo = mem.sb("e_lo", [P, 2, NT])
        cnt = {n: mem.sb(f"e_{n}", [P, E]) for n in ("need", "endt", "start", "drop")}
        need_i = mem.sb("e_need_i", [P, E], I32)
        own = mem.sb("e_own", [P, tiles, E - 1])
        ownf = mem.sb("e_ownf", [P, tiles])
        oh_lo = [mem.sb(f"e_oh_lo{u}", [P, P]) for u in range(4)]
        oh_hi = [mem.sb(f"e_oh_hi{u}", [P, 2, tiles]) for u in range(4)]
        table = mem.sb("e_table", [P, 2, tiles])
        p_r, p_n, p_m = mem.ps("e_ps_rank"), mem.ps("e_ps_totals"), mem.ps("e_ps_map")
        made, shifted, ex_done = mem.sem("e_made"), mem.sem("e_shifted"), mem.sem("e_ex")
        mask_done, ranked, order = mem.sem("e_mask_done"), mem.sem("e_ranked"), mem.sem("e_order")
        hi_done, mapped = mem.sem("e_hi_done"), mem.sem("e_mapped")
        GE = [P, NT, E]
        with nc.Block() as block:
            @block.gpsimd
            def _(pool):
                imprecise = dict(allow_small_or_imprecise_dtypes=True)
                nc.gpsimd.iota(iota_e[:, :], pattern=[[1, E]], base=0, channel_multiplier=0, **imprecise).then_inc(made, 1)
                nc.gpsimd.iota(iota_p[:, :], pattern=[[1, P]], base=0, channel_multiplier=0, **imprecise).then_inc(made, 1)
                nc.gpsimd.iota(iota_t[:, :], pattern=[[1, tiles]], base=0, channel_multiplier=0, **imprecise)\
                    .then_inc(made, 1)
                nc.gpsimd.iota(token[:, :], pattern=[[P, NT]], base=-N, channel_multiplier=1, **imprecise)\
                    .then_inc(made, 1)
                nc.gpsimd.memset(ones[:, :], 1.0).then_inc(made, 1)
                nc.gpsimd.memset(tri[:, :], 1.0).then_inc(made, 1)
                pool.wait_ge(made, 6)
                nc.gpsimd.affine_select(out=tri[:, :], in_=tri[:, :], compare_op=ALU.is_gt, fill=0.0, base=0,
                                        pattern=[[1, P]], channel_multiplier=-1).then_inc(made, 1)

            @block.scalar
            def _(act):
                act.wait_ge(shifted, 1)
                nc.scalar.activation(t["ex"][:, :, :], t["ex"][:, :, :], ACT.Exp).then_inc(ex_done, 1)

            @block.vector
            def _(dve):
                v = nc.vector
                link = Chain(dve, order)
                lg = c.logits[:, :].rearrange("p (i e) -> p i e", e=E)

                def wide(x):
                    return bcast(x[:, :].unsqueeze(2), GE)

                def per_expert(x):
                    return bcast(x[:, :].unsqueeze(1), GE)

                def first_of(values, best, onehot):
                    link(v.tensor_tensor(t["eq"][:, :, :], values, wide(best), ALU.is_equal))
                    link(v.scalar_tensor_tensor(out=t["cand"][:, :, :], in0=t["eq"][:, :, :], scalar=-float(E),
                                                in1=per_expert(iota_e), op0=ALU.mult, op1=ALU.add))
                    link(v.tensor_reduce(small["cm"][:, :], t["cand"][:, :, :], axis=AX.X, op=ALU.min))
                    link(v.tensor_tensor(onehot[:, :, :], t["cand"][:, :, :], wide(small["cm"]), ALU.is_equal))

                link(v.memset(unit[:, :], 1.0))
                link(v.tensor_reduce(small["mx"][:, :], lg, axis=AX.X, op=ALU.max))
                v.tensor_tensor(t["ex"][:, :, :], lg, wide(small["mx"]), ALU.subtract).then_inc(shifted, 1)
                dve.wait_ge(ex_done, 1)
                link(v.tensor_reduce(small["sm"][:, :], t["ex"][:, :, :], axis=AX.X, op=ALU.add))
                link(v.reciprocal(small["rc"][:, :], small["sm"][:, :]))
                link(v.tensor_tensor(t["pr"][:, :, :], t["ex"][:, :, :], wide(small["rc"]), ALU.mult))
                dve.wait_ge(made, 7)
                link(v.tensor_reduce(small["w1"][:, :], t["pr"][:, :, :], axis=AX.X, op=ALU.max))
                first_of(t["pr"][:, :, :], small["w1"], t["oh1"])
                link(v.scalar_tensor_tensor(out=t["pr2"][:, :, :], in0=t["oh1"][:, :, :], scalar=-2.0,
                                            in1=t["pr"][:, :, :], op0=ALU.mult, op1=ALU.add))
                link(v.tensor_reduce(small["w2"][:, :], t["pr2"][:, :, :], axis=AX.X, op=ALU.max))
                first_of(t["pr2"][:, :, :], small["w2"], t["oh2"])
                link(v.tensor_tensor(t["mask"][:, :, :], t["oh1"][:, :, :], t["oh2"][:, :, :], ALU.add))
                v.tensor_copy(maskb[:, :], t["mask"][:, :, :].rearrange("p i e -> p (i e)")).then_inc(mask_done, 1)
                dve.wait_ge(ranked, 1)
                link(v.tensor_copy(totals[:, :, :].rearrange("p i e -> p (i e)"), p_n[:, 0:G]))
                for e in range(E):
                    scan = v.tensor_tensor_scan(out=t["incl"][:, :, e], data0=unit[:, :], data1=totals[:, :, e],
                                                initial=0.0, op0=ALU.mult, op1=ALU.add)
                    link(scan)
                link(v.tensor_tensor(t["pos"][:, :, :].rearrange("p i e -> p (i e)"), p_r[:, 0:G],
                                     t["incl"][:, :, :].rearrange("p i e -> p (i e)"), ALU.add))
                link(v.tensor_tensor(t["pos"][:, :, :], t["pos"][:, :, :], totals[:, :, :], ALU.subtract))
                count = t["incl"][:, NT - 1, :]
                if fixed is None:
                    link(v.tensor_scalar(need_i[:, :], count, float(P - 1), None, ALU.add))
                    link(v.tensor_scalar(need_i[:, :], need_i[:, :], 7, None, ALU.arith_shift_right))
                    link(v.tensor_copy(cnt["need"][:, :], need_i[:, :]))
                    link(v.tensor_tensor_scan(out=cnt["endt"][:, :], data0=unit[:, 0:E], data1=cnt["need"][:, :],
                                              initial=0.0, op0=ALU.mult, op1=ALU.add))
                    link(v.tensor_tensor(cnt["start"][:, :], cnt["endt"][:, :], cnt["need"][:, :], ALU.subtract))
                    link(v.tensor_scalar(cnt["drop"][:, :], cnt["start"][:, :], float(P), None, ALU.mult))
                else:
                    link(v.tensor_scalar(cnt["start"][:, :], iota_e[:, :], float(fixed), None, ALU.mult))
                    link(v.tensor_scalar(cnt["drop"][:, :], count, float(fixed * P), float(4 * N), ALU.is_gt, ALU.mult))
                    link(v.scalar_tensor_tensor(out=cnt["drop"][:, :], in0=cnt["start"][:, :], scalar=float(P),
                                                in1=cnt["drop"][:, :], op0=ALU.mult, op1=ALU.add))
                link(v.tensor_tensor(t["pos"][:, :, :], t["pos"][:, :, :], per_expert(cnt["drop"]), ALU.add))
                for k, onehot in enumerate((t["oh1"], t["oh2"])):
                    link(v.tensor_tensor(t["prod"][:, :, :], t["pos"][:, :, :], onehot[:, :, :], ALU.mult))
                    link(v.tensor_reduce(small["slot"][:, :], t["prod"][:, :, :], axis=AX.X, op=ALU.add))
                    link(v.tensor_copy(sloti[:, :], small["slot"][:, :]))
                    link(v.tensor_scalar(hi_i[:, :], sloti[:, :], 7, None, ALU.arith_shift_right))
                    link(v.tensor_copy(hi[:, k, :], hi_i[:, :]))
                    link(v.scalar_tensor_tensor(out=lo[:, k, :], in0=hi[:, k, :], scalar=-float(P),
                                                in1=small["slot"][:, :], op0=ALU.mult, op1=ALU.add))
                link(v.tensor_tensor(own[:, :, :], bcast(iota_t[:, :].unsqueeze(2), [P, tiles, E - 1]),
                                     bcast(cnt["start"][:, 1:E].unsqueeze(1), [P, tiles, E - 1]), ALU.is_ge))
                link(v.tensor_reduce(ownf[:, :], own[:, :, :], axis=AX.X, op=ALU.add))
                link(v.tensor_copy(c.owner[:, 0:tiles], ownf[:, :]))
                gains = (small["w1"], small["w2"])

                def outer_products(g, first, last):
                    for u in range(4):
                        i, k = g * 2 + u // 2, u % 2
                        wait_from(dve, mapped, g * 4 + u - 3)
                        v.tensor_scalar(oh_lo[u][:, :], iota_p[:, :], lo[:, k, bass.ds(i, 1)], None, ALU.is_equal)
                        v.tensor_scalar(oh_hi[u][:, 0, :], iota_t[:, :], hi[:, k, bass.ds(i, 1)],
                                        token[:, bass.ds(i, 1)], ALU.is_equal, ALU.mult)
                        v.tensor_scalar(oh_hi[u][:, 1, :], iota_t[:, :], hi[:, k, bass.ds(i, 1)],
                                        gains[k][:, bass.ds(i, 1)], ALU.is_equal, ALU.mult).then_inc(hi_done, 1)
                peeled_ends(dve, NT // 2, outer_products)
                dve.wait_ge(mapped, 2 * NT)
                link(v.tensor_copy(table[:, :, :].rearrange("p a t -> p (a t)"), p_m[:, 0:2 * tiles]))
                link(v.tensor_scalar(c.scatter[:, 0:tiles], table[:, 0, :], float(N), None, ALU.add))
                link(v.tensor_scalar(c.gather[:, 0:tiles], table[:, 0, :], float(N), float(N - 1), ALU.add, ALU.min))
                link(v.tensor_copy(c.gains[:, 0:tiles], table[:, 1, :]))

            @block.tensor
            def _(pe):
                pe.wait_ge(mask_done, 1)
                pe.wait_ge(made, 7)
                nc.tensor.matmul(p_r[:, 0:G], tri[:, :], maskb[:, :], start=True, stop=True)
                nc.tensor.matmul(p_n[:, 0:G], ones[:, :], maskb[:, :], start=True, stop=True).then_inc(ranked, 1)

                def outer_products(g, first, last):
                    for u in range(4):
                        pe.wait_ge(hi_done, g * 4 + u + 1)
                        nc.tensor.matmul(p_m[:, 0:2 * tiles], oh_lo[u][:, :],
                                         oh_hi[u][:, :, :].rearrange("p a t -> p (a t)"),
                                         start=(first and u == 0), stop=(last and u == 3)).then_inc(mapped, 1)
                peeled_ends(pe, NT // 2, outer_products)
        mem.clear()


def stage_experts(nc, outer, c, tiles, F, w1, w2, b1, b2, func, rows, sums):
    FC = F // P
    HW = min(F, HALF)
    with ExitStack() as stack:
        mem = Mem(nc, stack)
        ig = [mem.sb(f"m_ig{u}", [P, 1], I32) for u in range(2)]
        isc = [mem.sb(f"m_is{u}", [P, 1], I32) for u in range(2)]
        xg = [mem.sb(f"m_x{u}", [P, D]) for u in range(2)]
        xt = [mem.sb(f"m_xt{u}", [P, KC, P]) for u in range(2)]
        hs = [mem.sb(f"m_h{u}", [P, F]) for u in range(2)]
        ht = [mem.sb(f"m_ht{u}", [P, FC, P]) for u in range(2)]
        ys = [mem.sb(f"m_y{u}", [P, D]) for u in range(2)]
        p_x, p_y = mem.ps("m_ps_x"), mem.ps("m_ps_y")
        p_h = mem.ps("m_ps_h", (P, max(F, HALF)))
        p_t = mem.ps("m_ps_t", (P, max(F, HALF)))
        idx_g, idx_s = mem.sem("m_idx_g"), mem.sem("m_idx_s")
        gathered = [mem.sem(f"m_gathered{u}") for u in range(2)]
        added = mem.sem("m_added")
        x_turned, x_copied = mem.sem("m_x_turned"), mem.sem("m_x_copied")
        h_made, biased, act_done = mem.sem("m_h_made"), mem.sem("m_biased"), mem.sem("m_act_done")
        h_turned, h_copied = mem.sem("m_h_turned"), mem.sem("m_h_copied")
        y_made, y_biased, y_scaled = mem.sem("m_y_made"), mem.sem("m_y_biased"), mem.sem("m_y_scaled")
        spare_p = mem.sem("m_spare")
        halves = F // HW
        with nc.Block() as block:
            def pairs(eng, body):
                body(0, True, False)
                with eng.Fori(1, tiles // 2 - 1) as g:
                    body(g * 2, False, False)
                body(tiles - 2, False, True)

            @block.gpsimd
            def _(pool):
                def gather(t, u):
                    wait_apart(pool, spare_p, x_turned, t - 1)
                    nc.gpsimd.tensor_copy(ig[u][:, :], c.gather[:, bass.ds(t, 1)]).then_inc(idx_g, 1)
                    wait_apart(pool, spare_p, idx_g, t + 1)
                    pool.indirect_dma_start(out=xg[u][:, :], out_offset=None, in_=rows,
                                            in_offset=bass.IndirectOffsetOnAxis(ap=ig[u][:, :], axis=0))\
                        .then_inc(gathered[u], 16)

                def add(t, u):
                    nc.gpsimd.tensor_copy(isc[u][:, :], c.scatter[:, bass.ds(t, 1)]).then_inc(idx_s, 1)
                    wait_apart(pool, spare_p, idx_s, t + 1)
                    wait_apart(pool, spare_p, y_scaled, t + 1)
                    wait_apart(pool, spare_p, added, t * 16)
                    pool.indirect_dma_start(out=sums, out_offset=bass.IndirectOffsetOnAxis(ap=isc[u][:, :], axis=0),
                                            in_=ys[u][:, :], in_offset=None, bounds_check=N - 1, oob_is_err=False,
                                            compute_op=ALU.add).then_inc(added, 16)

                def body(t, first, last):
                    for u in range(2):
                        if not last:
                            gather(t + u + 2, u)
                        if not (first and u == 0):
                            add(t + u - 1, 1 - u)
                gather(0, 0)
                gather(1, 1)
                pairs(pool, body)
                add(tiles - 1, 1)
                pool.wait_ge(added, 16 * tiles)

            @block.tensor
            def _(pe):
                def turn_x(t, u):
                    pe.wait_ge(gathered[u], (t - u) * 8 + 16)
                    wait_from(pe, x_copied, t)
                    for k in range(KC):
                        mm = nc.tensor.transpose(p_x[:, k * P:(k + 1) * P], xg[u][:, k * P:(k + 1) * P], c.ident[:, :])
                    mm.then_inc(x_turned, 1)

                owner = [pe.alloc_register(Mem.label("owner_pe")) for u in range(2)]

                def load_owner(t, u):
                    pe.reg_load(owner[u], c.owner[0:1, bass.ds(t, 1)])

                def expert(u):
                    return pe.snap(owner[u], min_val=0, max_val=E - 1)

                def first_product(t, u):
                    e = expert(u)
                    pe.wait_ge(x_copied, t + 1)
                    for half in range(halves):
                        wait_from(pe, biased, t * halves + half - halves + 1)
                        for k in range(KC):
                            mm = nc.tensor.matmul(p_h[:, half * HW:(half + 1) * HW], xt[u][:, k, :],
                                                  w1[:, bass.ds(e * KC + k, 1), half * HW:(half + 1) * HW]
                                                  .rearrange("p a f -> p (a f)"),
                                                  start=(k == 0), stop=(k == KC - 1))
                        mm.then_inc(h_made, 1)

                def turn_h(t, u):
                    for half in range(halves):
                        pe.wait_ge(act_done, t * halves + half + 1)
                        wait_from(pe, h_copied, t * halves + half - halves + 1)
                        for j in range(HW // P):
                            at = half * HW + j * P
                            mm = nc.tensor.transpose(p_t[:, at:at + P], hs[u][:, at:at + P], c.ident[:, :])
                        mm.then_inc(h_turned, 1)

                def second_product(t, u):
                    e = expert(u)
                    wait_from(pe, y_biased, t)
                    for f in range(FC):
                        if f % (HW // P) == 0:
                            pe.wait_ge(h_copied, t * halves + f // (HW // P) + 1)
                        mm = nc.tensor.matmul(p_y[:, 0:D], ht[u][:, f, :],
                                              w2[:, bass.ds(e * FC + f, 1), :].rearrange("p a d -> p (a d)"),
                                              start=(f == 0), stop=(f == FC - 1))
                    mm.then_inc(y_made, 1)

                def body(t, first, last):
                    for u in range(2):
                        first_product(t + u, u)
                        if not (last and u == 1):
                            turn_x(t + u + 1, 1 - u)
                        if not (first and u == 0):
                            second_product(t + u - 1, 1 - u)
                        if not (last and u == 1):
                            load_owner(t + u + 1, 1 - u)
                        turn_h(t + u, u)
                load_owner(0, 0)
                turn_x(0, 0)
                pairs(pe, body)
                second_product(tiles - 1, 1)

            @block.scalar
            def _(act):
                def copy_x(t, u):
                    act.wait_ge(x_turned, t + 1)
                    wait_from(act, h_made, (t - 1) * halves)
                    nc.scalar.activation(xt[u][:, :, :].rearrange("p c n -> p (c n)"), p_x[:, 0:D], ACT.Identity)\
                        .then_inc(x_copied, 1)

                def body(t, first, last):
                    for u in range(2):
                        for half in range(halves):
                            act.wait_ge(biased, (t + u) * halves + half + 1)
                            span = hs[u][:, half * HW:(half + 1) * HW]
                            nc.scalar.activation(span, span, func).then_inc(act_done, 1)
                        if not (last and u == 1):
                            copy_x(t + u + 1, 1 - u)
                copy_x(0, 0)
                pairs(act, body)

            @block.vector
            def _(dve):
                owner = [dve.alloc_register(Mem.label("owner_dve")) for u in range(2)]

                def load_owner(t, u):
                    dve.reg_load(owner[u], c.owner[0:1, bass.ds(t, 1)])

                def expert(u):
                    return dve.snap(owner[u], min_val=0, max_val=E - 1)

                def bias_h(t, u):
                    e = expert(u)
                    wait_from(dve, h_turned, (t - 1) * halves)
                    for half in range(halves):
                        dve.wait_ge(h_made, t * halves + half + 1)
                        nc.vector.tensor_tensor(hs[u][:, half * HW:(half + 1) * HW], p_h[:, half * HW:(half + 1) * HW],
                                                b1[:, bass.ds(e, 1), half * HW:(half + 1) * HW]
                                                .rearrange("p a f -> p (a f)"), ALU.add).then_inc(biased, 1)

                def copy_h(t, u):
                    wait_from(dve, y_made, t - 1)
                    for half in range(halves):
                        dve.wait_ge(h_turned, t * halves + half + 1)
                        nc.vector.tensor_copy(ht[u][:, :, :].rearrange("p f n -> p (f n)")[:, half * HW:(half + 1) * HW],
                                              p_t[:, half * HW:(half + 1) * HW]).then_inc(h_copied, 1)

                def scale_y(t, u):
                    e = expert(u)
                    dve.wait_ge(y_made, t + 1)
                    wait_from(dve, added, (t - 1) * 16)
                    nc.vector.tensor_tensor(ys[u][:, :], p_y[:, 0:D], b2[:, bass.ds(e, 1), :]
                                            .rearrange("p a d -> p (a d)"), ALU.add).then_inc(y_biased, 1)
                    dve.wait_ge(y_biased, t + 1)
                    nc.vector.tensor_scalar(ys[u][:, :], ys[u][:, :], c.gains[:, bass.ds(t, 1)], None, ALU.mult)\
                        .then_inc(y_scaled, 1)

                def body(t, first, last):
                    for u in range(2):
                        bias_h(t + u, u)
                        if not (first and u == 0):
                            scale_y(t + u - 1, 1 - u)
                        if not (last and u == 1):
                            load_owner(t + u + 1, 1 - u)
                        copy_h(t + u, u)
                load_owner(0, 0)
                pairs(dve, body)
                scale_y(tiles - 1, 1)
        mem.clear()


def stage_to_channels(nc, outer, a, c):
    with ExitStack() as stack:
        mem = Mem(nc, stack)
        st = [mem.sb(f"t_tile{u}", [P, D]) for u in range(2)]
        p_tr = [mem.ps(f"t_ps{u}") for u in range(2)]
        ready, kept, turned, copied = mem.sem("t_ready"), mem.sem("t_kept"), mem.sem("t_turned"), mem.sem("t_copied")
        spare_p = mem.sem("t_spare")
        with nc.Block() as block:
            @block.vector
            def _(dve):
                nc.vector.memset(c.xe[:, :, :, L1:L1 + 2], 0.0)
                nc.vector.memset(c.xo[:, :, :, 0:1], 0.0)

                def norm(b):
                    for t in range(TB):
                        wait_from(dve, turned, b * TB + t - 1)
                        wait_from(dve, kept, b * TB + t - 1)
                        normalised(nc, c, st[t % 2][:, :], b * TB + t).then_inc(ready, 1)
                peeled(dve, B, norm)

            @block.gpsimd
            def _(pool):
                def keep(b):
                    for t in range(TB):
                        wait_apart(pool, spare_p, ready, b * TB + t + 1)
                        nc.gpsimd.tensor_copy(c.x2[:, bass.ds(b * TB + t, 1), :].rearrange("p a d -> p (a d)"),
                                              st[t % 2][:, :]).then_inc(kept, 1)
                peeled(pool, B, keep)

            @block.tensor
            def _(pe):
                def turn(b):
                    for t in range(TB):
                        pe.wait_ge(ready, b * TB + t + 1)
                        wait_from(pe, copied, b * TB + t - 1)
                        for k in range(KC):
                            mm = nc.tensor.transpose(p_tr[t % 2][:, k * P:(k + 1) * P], st[t % 2][:, k * P:(k + 1) * P],
                                                     c.ident[:, :])
                        mm.then_inc(turned, 1)
                peeled(pe, B, turn)

            @block.scalar
            def _(act):
                def copy(b):
                    for t in range(TB):
                        act.wait_ge(turned, b * TB + t + 1)
                        dst, at = (c.xe, 0) if t % 2 == 0 else (c.xo, 1)
                        at += (t // 2) * P
                        nc.scalar.activation(
                            dst[:, :, bass.ds(b, 1), at:at + P].rearrange("p c b n -> p (c b) n"),
                            p_tr[t % 2][:, 0:D].rearrange("p (c n) -> p c n", c=KC), ACT.Copy).then_inc(copied, 1)
                peeled(act, B, copy)
        mem.clear()


def stage_wavelet(nc, outer, a, c):
    with ExitStack() as stack:
        mem = Mem(nc, stack)
        fil = mem.sb("w_filters", [P, KC, 4, 4])
        fs = mem.sb("w_sums", [P, KC, 2, 5])
        diag = mem.sb("w_diag", [P, KC, 9, P])
        blocks = mem.sb("w_blocks", [P, P])
        low1 = mem.sb("w_low1", [P, KC, B, L1 + 2])
        high1 = mem.sb("w_high1", [P, KC, B, L1 + 2])
        low2 = mem.sb("w_low2", [P, KC, B, L2])
        high2 = mem.sb("w_high2", [P, KC, B, L2 + 2])
        q = mem.sb("w_q", [P, KC, B, L2])
        z = mem.sb("w_z", [P, KC, B])
        al = mem.sb("w_attn", [P, KC, B, L2 + 2])
        qt = mem.sb("w_qt", [P, B, KC, 2, P])
        kvm = mem.sb("w_kv", [P, B, KC, P])
        zm = mem.sb("w_zm", [P, B, KC, P])
        den = mem.sb("w_den", [P, KC, L2])
        htt = mem.sb("w_ht", [P, B, KC, 2, P])
        se, so = c.xe, c.xo
        banks = [mem.ps(f"w_ps{n}") for n in range(8)]
        loaded, order, made = mem.sem("w_loaded"), mem.sem("w_order"), mem.sem("w_made")
        diag_ready = mem.sem("w_diag_ready")
        high_made, high_copied = mem.sem("w_high_made"), mem.sem("w_high_copied")
        min_ready, exp_ready, q_ready = mem.sem("w_min"), mem.sem("w_exp"), mem.sem("w_q_ready")
        turned, qt_copied, ht_copied = mem.sem("w_turned"), mem.sem("w_qt_copied"), mem.sem("w_ht_copied")
        kv_made, kv_ready, nd_made, nd_used = mem.sem("w_kv_made"), mem.sem("w_kv_ready"), mem.sem("w_nd"), mem.sem("w_nd_used")
        syn_ready, tile_made, tile_used = mem.sem("w_syn_ready"), mem.sem("w_tile_made"), mem.sem("w_tile_used")
        with nc.Block() as block:
            @block.sync
            def _(sp):
                sp.dma_start(fil[:, :, :, :], a.filters).then_inc(loaded, 16)

            @block.gpsimd
            def _(pool):
                nc.gpsimd.memset(blocks[:, :], 1.0).then_inc(made, 1)
                pool.wait_ge(made, 1)
                bl = blocks[:, :].rearrange("p (h r) -> p h r", r=HD)
                nc.gpsimd.affine_select(out=bl, in_=bl, compare_op=ALU.is_ge, fill=0.0, base=0,
                                        pattern=[[-HD, P // HD], [0, HD]], channel_multiplier=1).then_inc(made, 1)
                pool.wait_ge(made, 2)
                nc.gpsimd.affine_select(out=bl, in_=bl, compare_op=ALU.is_ge, fill=0.0, base=HD - 1,
                                        pattern=[[HD, P // HD], [0, HD]], channel_multiplier=-1).then_inc(made, 1)

            @block.vector
            def _(dve):
                v = nc.vector
                link = Chain(dve, order)
                for x in (low1, high1, high2, al):
                    v.memset(x[:, :, :, 0:1], 0.0)
                    n = x.shape[3]
                    v.memset(x[:, :, :, n - 1:n], 0.0)
                dve.wait_ge(loaded, 16)
                for f in range(2):
                    for n, taps in enumerate(((0,), (1, 2), (3,), (0, 1), (2, 3))):
                        for k in range(KC):
                            src = fil[:, k, 2 + f, taps[0]:taps[0] + 1]
                            dst = fs[:, k, f, n:n + 1]
                            last = (v.tensor_copy(dst, src) if len(taps) == 1 else
                                    v.tensor_tensor(dst, src, fil[:, k, 2 + f, taps[1]:taps[1] + 1], ALU.add))
                link(last)
                for k in range(KC):
                    for n in range(4):
                        last = v.tensor_scalar(diag[:, k, n, :], c.ident[:, :], fil[:, k, 1, n:n + 1], None, ALU.mult)
                last.then_inc(diag_ready, 1)
                for k in range(KC):
                    for n in range(5):
                        last = v.tensor_scalar(diag[:, k, 4 + n, :], c.ident[:, :], fs[:, k, 1, n:n + 1], None, ALU.mult)
                last.then_inc(diag_ready, 1)

                def taps(dst, terms, begin=True):
                    for n, (src, scalar) in enumerate(terms):
                        for k in range(KC):
                            if n == 0 and begin:
                                last = v.tensor_scalar(dst(k), src(k), scalar(k), None, ALU.mult)
                            else:
                                last = v.scalar_tensor_tensor(out=dst(k), in0=src(k), scalar=scalar(k), in1=dst(k),
                                                              op0=ALU.mult, op1=ALU.add)
                        link(last)

                def part(x, at, n, step=1):
                    return lambda k: x[:, k, :, at:at + (n - 1) * step + 1:step]

                def tap(f, n):
                    return lambda k: fil[:, k, f, n:n + 1]

                def total(f, n):
                    return lambda k: fs[:, k, f, n:n + 1]

                taps(part(low1, 1, L1), [(part(c.xo, 0, L1), tap(0, 0)), (part(c.xe, 0, L1), tap(0, 1)),
                                         (part(c.xo, 1, L1), tap(0, 2)), (part(c.xe, 1, L1), tap(0, 3))])
                taps(lambda k: low2[:, k, :, :], [(part(low1, n, L2, 2), tap(0, n)) for n in range(4)])
                flat = low2[:, :, :, :].rearrange("p c b n -> p (c b n)")
                qf = q[:, :, :, :].rearrange("p c b n -> p (c b n)")
                v.tensor_scalar(qf, flat, 0.0, None, ALU.min).then_inc(min_ready, 1)
                taps(part(high2, 1, L2), [(part(low1, n, L2, 2), tap(1, n)) for n in range(4)])
                dve.wait_ge(exp_ready, 1)
                v.scalar_tensor_tensor(out=qf, in0=flat, scalar=0.0, in1=qf, op0=ALU.max, op1=ALU.add)\
                    .then_inc(q_ready, 1)
                dve.wait_ge(q_ready, 1)
                link(v.tensor_reduce(z[:, :, :], q[:, :, :, :], axis=AX.X, op=ALU.add))
                dve.wait_ge(made, 3)
                for b in range(B):
                    for k in range(KC):
                        v.tensor_scalar(zm[:, b, k, :], blocks[:, :], z[:, k, b:b + 1], None, ALU.mult)
                    dve.wait_ge(turned, 2 * b + 1)
                    v.tensor_copy(qt[:, b, :, :, :].rearrange("p c j n -> p (c j n)"), banks[2 * b][:, :])\
                        .then_inc(qt_copied, 1)
                even, odd = part(low1, 1, L2, 2), part(low1, 2, L2, 2)

                def doubled(dst_even, dst_odd, src, f, n, begin):
                    taps(dst_even, [(part(src, 0, n), total(f, 0)), (part(src, 1, n), total(f, 1)),
                                    (part(src, 2, n), total(f, 2))], begin)
                    taps(dst_odd, [(part(src, 1, n), total(f, 3)), (part(src, 2, n), total(f, 4))], begin)
                doubled(even, odd, high2, 1, L2, True)
                for b in range(B):
                    dve.wait_ge(kv_made, b + 1)
                    for k in range(KC):
                        last = v.tensor_tensor(kvm[:, b, k, :], banks[b][:, k * P:(k + 1) * P], blocks[:, :], ALU.mult)
                    last.then_inc(kv_ready, 1)
                for b in range(B):
                    dve.wait_ge(nd_made, b + 1)
                    wait_from(dve, nd_used, b)
                    n, d = 2 * (b % 2) + 4, 2 * (b % 2) + 5
                    dn = den[:, :, :].rearrange("p c n -> p (c n)")
                    link(v.tensor_scalar(dn, banks[d][:, :], 1e-6, None, ALU.add))
                    link(v.reciprocal(dn, dn))
                    v.tensor_tensor(al[:, :, b, 1:1 + L2], banks[n][:, :].rearrange("p (c n) -> p c n", c=KC),
                                    den[:, :, :], ALU.mult).then_inc(nd_used, 1)
                dve.wait_ge(nd_used, B)
                doubled(even, odd, al, 0, L2, False)
                dve.wait_ge(high_copied, B * KC)
                doubled(part(se, 0, L1), part(so, 1, L1), low1, 0, L1, True)
                v.drain().then_inc(syn_ready, 1)
                for i in range(NT):
                    dve.wait_ge(tile_made, i + 1)
                    v.tensor_tensor(c.y[:, i, :], banks[i % 4][:, 0:D], c.x2[:, i, :], ALU.add).then_inc(tile_used, 1)
                    dve.wait_ge(tile_used, i + 1)
                    row_stats(nc, c, i)

            @block.scalar
            def _(act):
                for b in range(B):
                    for k in range(KC):
                        n = b * KC + k
                        act.wait_ge(high_made, n + 1)
                        nc.scalar.activation(high1[:, k, b, 1:1 + L1], banks[n % 2][:, :], ACT.Copy)\
                            .then_inc(high_copied, 1)
                act.wait_ge(min_ready, 1)
                qf = q[:, :, :, :].rearrange("p c b n -> p (c b n)")
                nc.scalar.activation(qf, qf, ACT.Exp).then_inc(exp_ready, 1)
                for b in range(B):
                    act.wait_ge(turned, 2 * b + 2)
                    nc.scalar.activation(htt[:, b, :, :, :].rearrange("p c j n -> p (c j n)"),
                                         banks[2 * b + 1][:, :], ACT.Copy).then_inc(ht_copied, 1)

            @block.tensor
            def _(pe):
                pe.wait_ge(diag_ready, 1)
                for b in range(B):
                    for k in range(KC):
                        n = b * KC + k
                        wait_from(pe, high_copied, n - 1)
                        for j, (src, at) in enumerate(((c.xo, 0), (c.xe, 0), (c.xo, 1), (c.xe, 1))):
                            mm = nc.tensor.matmul(banks[n % 2][:, :], diag[:, k, j, :], src[:, k, b, at:at + L1],
                                                  start=(j == 0), stop=(j == 3))
                        mm.then_inc(high_made, 1)
                pe.wait_ge(high_copied, B * KC)
                pe.wait_ge(q_ready, 1)
                for b in range(B):
                    for m, src in enumerate((q, low2)):
                        for k in range(KC):
                            for j in range(2):
                                at = (k * 2 + j) * P
                                mm = nc.tensor.transpose(banks[2 * b + m][:, at:at + P], src[:, k, b, j * P:(j + 1) * P],
                                                         c.ident[:, :])
                        mm.then_inc(turned, 1)
                pe.wait_ge(qt_copied, B)
                pe.wait_ge(ht_copied, B)
                for b in range(B):
                    for k in range(KC):
                        for j in range(2):
                            mm = nc.tensor.matmul(banks[b][:, k * P:(k + 1) * P], qt[:, b, k, j, :], htt[:, b, k, j, :],
                                                  start=(j == 0), stop=(j == 1))
                    mm.then_inc(kv_made, 1)
                for b in range(B):
                    pe.wait_ge(kv_ready, b + 1)
                    wait_from(pe, nd_used, b - 1)
                    for m, w in enumerate((kvm, zm)):
                        for k in range(KC):
                            mm = nc.tensor.matmul(banks[2 * (b % 2) + 4 + m][:, k * L2:(k + 1) * L2], w[:, b, k, :],
                                                  q[:, k, b, :], start=True, stop=True)
                    mm.then_inc(nd_made, 1)
                pe.wait_ge(diag_ready, 2)
                pe.wait_ge(syn_ready, 1)
                pe.wait_ge(nd_used, B)
                for i in range(NT):
                    b, t = i // TB, i % TB
                    at = (t // 2) * P
                    wait_from(pe, tile_used, i - 3)
                    for k in range(KC):
                        low, high = ((se[:, k, b, at:at + P], ((0, 0), (1, 1), (2, 2))) if t % 2 == 0 else
                                     (so[:, k, b, at + 1:at + 1 + P], ((1, 3), (2, 4))))
                        dst = banks[i % 4][:, k * P:(k + 1) * P]
                        mm = nc.tensor.matmul(dst, low, c.ident[:, :], start=True, stop=False)
                        for off, n in high:
                            mm = nc.tensor.matmul(dst, high1[:, k, b, at + off:at + off + P], diag[:, k, 4 + n, :],
                                                  start=False, stop=(n == high[-1][1]))
                    mm.then_inc(tile_made, 1)
        mem.clear()


def stage_affine(nc, outer, a, c):
    with ExitStack() as stack:
        mem = Mem(nc, stack)
        gamma = mem.sb("n_gamma", [P, D])
        beta = mem.sb("n_beta", [P, D])
        st = [mem.sb(f"n_tile{u}", [P, D]) for u in range(4)]
        loaded, ready, scaled, moved = mem.sem("n_loaded"), mem.sem("n_ready"), mem.sem("n_scaled"), mem.sem("n_moved")
        summed, spare = mem.sem("n_summed"), mem.sem("n_spare")
        spare_p = mem.sem("n_spare_pool")
        with nc.Block() as block:
            @block.sync
            def _(sp):
                sp.dma_start(gamma[:, :], a.gamma.partition_broadcast(P)).then_inc(loaded, 16)
                sp.dma_start(beta[:, :], a.beta.partition_broadcast(P)).then_inc(loaded, 16)

            @block.gpsimd
            def _(pool):
                def scale(b):
                    for t in range(TB):
                        i = b * TB + t
                        wait_apart(pool, spare_p, ready, i + 1)
                        nc.gpsimd.tensor_tensor(st[t % 4][:, :], st[t % 4][:, :], gamma[:, :], ALU.mult).then_inc(scaled, 1)
                        wait_apart(pool, spare_p, scaled, i + 1)
                        nc.gpsimd.tensor_tensor(st[t % 4][:, :], st[t % 4][:, :], beta[:, :], ALU.add).then_inc(moved, 1)
                pool.wait_ge(loaded, 32)
                peeled(pool, B, scale)

            @block.vector
            def _(dve):
                def finish(i, t):
                    dve.wait_ge(moved, i + 1)
                    yi = c.y[:, bass.ds(i, 1), :].rearrange("p a d -> p (a d)")
                    nc.vector.tensor_tensor(yi, st[t % 4][:, :], c.x2[:, bass.ds(i, 1), :]
                                            .rearrange("p a d -> p (a d)"), ALU.add).then_inc(summed, 1)
                    wait_apart(dve, spare, summed, i + 1)
                    row_stats(nc, c, i)

                def tiles(b):
                    for t in range(TB):
                        wait_from(dve, summed, b * TB + t - 3)
                        normalised(nc, c, st[t % 4][:, :], b * TB + t).then_inc(ready, 1)
                        if t >= 2:
                            finish(b * TB + t - 2, t - 2)
                    for t in (TB - 2, TB - 1):
                        finish(b * TB + t, t)
                peeled(dve, B, tiles)
        mem.clear()


def stage_store(nc, outer, c, out):
    with ExitStack() as stack:
        mem = Mem(nc, stack)
        st = [mem.sb(f"s_batch{u}", [P, TB, D]) for u in range(2)]
        ready = mem.sem("s_ready")
        stored = [mem.sem(f"s_stored{u}") for u in range(2)]
        rows = out.rearrange("(i p) d -> p i d", p=P)
        with nc.Block() as block:
            @block.vector
            def _(dve):
                for b in range(B):
                    wait_from(dve, stored[b % 2], 16 * (b // 2))
                    for t in range(TB):
                        last = normalised(nc, c, st[b % 2][:, t, :], b * TB + t)
                    last.then_inc(ready, 1)

            @block.sync
            def _(sp):
                for b in range(B):
                    sp.wait_ge(ready, b + 1)
                    sp.dma_start(rows[:, b * TB:(b + 1) * TB, :], st[b % 2][:, :, :]).then_inc(stored[b % 2], 16)
                for u in range(2):
                    sp.wait_ge(stored[u], 32)


class Names:
    pass


def build(nc, a, out):
    Mem.uses = {}
    c = Names()

    def dram(name, shape, dt=FP32):
        return nc.dram_tensor(name, shape, dt).ap()
    c.q_parts, c.k_parts = dram("q_parts", [NH, HD, PARTS, S], BF16), dram("k_parts", [NH, HD, PARTS, S], BF16)
    rows = [dram(f"rows{n}", [N, D]) for n in range(2)]
    sums = [dram(f"sums{n}", [N, D]) for n in range(2)]
    F0 = 4 * D
    most = N * 2 // P + E - 1
    most += most % 2
    CAP = int(1.25 * N / E) // P
    with ExitStack() as stack:
        mem = Mem(nc, stack)
        stage_constants(nc, mem, c)
        c.six = mem.sb("six", [P, NT, 6])
        c.rstd = mem.sb("rstd", [P, NT])
        c.nmr = mem.sb("nmr", [P, NT])
        c.logits = mem.sb("logits", [P, NT * E])
        c.gather = mem.sb("gather", [P, most], I32)
        c.scatter = mem.sb("scatter", [P, most], I32)
        c.gains = mem.sb("gains", [P, most])
        c.owner = mem.sb("owner", [P, most], I32)
        with ExitStack() as inner:
            m = Mem(nc, inner)
            w1 = m.sb("w1", [P, E * KC, F0])
            w2 = m.sb("w2", [P, E * (F0 // P), D])
            late = m.sb("biases", [P, E * (F0 + D)])
            w1_loaded, w2_loaded, b_loaded = m.sem("w1_loaded"), m.sem("w2_loaded"), m.sem("b_loaded")
            flat = w2[:, :, :].rearrange("p f d -> p (f d)")
            half = E * (F0 // P) * D // 2
            c.v = flat[:, 0:half].rearrange("p (n t r) -> p n t r", n=NH, t=TB)
            c.probs = flat[:, half:2 * half].rearrange("p (t s) -> p t s", t=TB)
            c.y = flat[:, half:2 * half].rearrange("p (i d) -> p i d", d=D)
            c.ao = late[:, 0:NH * TB * HD].rearrange("p (n t r) -> p n t r", n=NH, t=TB)
            stage_project(nc, m, a, c)
            with nc.Block() as block:
                @block.scalar
                def _(act):
                    for e in range(E):
                        act.dma_start(w1[:, e * KC:(e + 1) * KC, :], a.w1_0[e].rearrange("(c p) f -> p c f", p=P))\
                            .then_inc(w1_loaded, 16)
            stage_attention(nc, m, a, c)
            FC = F0 // P

            def load_w2(act, experts):
                for e in experts:
                    act.dma_start(w2[:, e * FC:(e + 1) * FC, :], a.w2_0[e].rearrange("(f p) d -> p f d", p=P))\
                        .then_inc(w2_loaded, 16)
            with nc.Block() as block:
                @block.scalar
                def _(act):
                    load_w2(act, range(E // 2))
            stage_output(nc, m, a, c)
            stage_rstd(nc, m, c)
            b1 = late[:, 0:E * F0].rearrange("p (e f) -> p e f", e=E)
            b2 = late[:, E * F0:E * (F0 + D)].rearrange("p (e d) -> p e d", e=E)
            with nc.Block() as block:
                @block.scalar
                def _(act):
                    act.dma_start(b1, a.b1_0.partition_broadcast(P)).then_inc(b_loaded, 16)
                    act.dma_start(b2, a.b2_0.partition_broadcast(P)).then_inc(b_loaded, 16)
            stage_gate(nc, m, c, a.gate_0, rows[0], sums[0])
            with nc.Block() as block:
                @block.scalar
                def _(act):
                    load_w2(act, range(E // 2, E))
            stage_route(nc, m, c, most, None)
            with nc.Block() as block:
                @block.tensor
                def _(pe):
                    pe.wait_ge(w1_loaded, 16 * E)
                    pe.wait_ge(w2_loaded, 16 * E)

                @block.vector
                def _(dve):
                    dve.wait_ge(b_loaded, 32)
            stage_experts(nc, m, c, most, F0, w1, w2, b1, b2, ACT.Gelu, rows[0], sums[0])
        with ExitStack() as inner:
            m = Mem(nc, inner)
            c.y = m.sb("y", [P, NT, D])
            c.x2 = m.sb("x2", [P, NT, D])
            with ExitStack() as inner2:
                m2 = Mem(nc, inner2)
                c.xe = m2.sb("x_even", [P, KC, B, L1 + 2])
                c.xo = m2.sb("x_odd", [P, KC, B, L1 + 2])
                stage_load_stats(nc, m, c, sums[0])
                stage_rstd(nc, m, c)
                stage_to_channels(nc, m, a, c)
                stage_wavelet(nc, m, a, c)
            stage_rstd(nc, m, c)
            w1 = m.sb("w1_1", [P, E * KC, D])
            w2 = m.sb("w2_1", [P, E * KC, D])
            b1 = m.sb("b1_1", [P, E, D])
            b2 = m.sb("b2_1", [P, E, D])
            loaded = m.sem("loaded_1")
            with nc.Block() as block:
                @block.scalar
                def _(act):
                    act.dma_start(w1[:, :, :], a.w1_1.rearrange("e (c p) f -> p (e c) f", p=P)).then_inc(loaded, 16)
                    act.dma_start(w2[:, :, :], a.w2_1.rearrange("e (c p) f -> p (e c) f", p=P)).then_inc(loaded, 16)
                    act.dma_start(b1[:, :, :], a.b1_1.partition_broadcast(P)).then_inc(loaded, 16)
                    act.dma_start(b2[:, :, :], a.b2_1.partition_broadcast(P)).then_inc(loaded, 16)
            stage_affine(nc, m, a, c)
            stage_rstd(nc, m, c)
            stage_gate(nc, m, c, a.gate_1, rows[1], sums[1])
            stage_route(nc, m, c, CAP * E, CAP)
            with nc.Block() as block:
                @block.tensor
                def _(pe):
                    pe.wait_ge(loaded, 64)

                @block.vector
                def _(dve):
                    dve.wait_ge(loaded, 64)
            stage_experts(nc, m, c, CAP * E, D, w1, w2, b1, b2, ACT.Silu, rows[1], sums[1])
            stage_load_stats(nc, m, c, sums[1])
            stage_rstd(nc, m, c)
            stage_store(nc, m, c, out)


def kernel(**inputs):
    import numpy as np
    import concourse.bacc as bacc
    from concourse.bass_utils import run_bass_kernel_spmd

    g = {k: np.asarray(v) for k, v in inputs.items()}
    J = S // (2 * P)
    x = g["L0_attn_x"].reshape(B, J, P, 2, D).transpose(0, 1, 3, 2, 4).reshape(N, D)
    taps = np.stack([g["L1_attn_" + n] for n in ("h_filter", "g_filter", "h_synth", "g_synth")])
    arrays = {
        "x": x, "xt": x.T,
        "wqkv": np.concatenate([g["L0_attn_W" + n].T for n in "qkv"], axis=1),
        "bqk": np.stack([g["L0_attn_b" + n].reshape(KC, P) for n in "qk"]).transpose(2, 0, 1),
        "bv": g["L0_attn_bv"], "wo": g["L0_attn_Wo"].T, "bo": g["L0_attn_bo"],
        "gate_0": g["L0_ffn_w_gate"].T, "w1_0": g["L0_ffn_W1"], "b1_0": g["L0_ffn_b1"],
        "w2_0": g["L0_ffn_W2"], "b2_0": g["L0_ffn_b2"],
        "filters": taps.reshape(4, 4, KC, P).transpose(3, 2, 0, 1),
        "gamma": g["L1_attn_norm_gamma"], "beta": g["L1_attn_norm_beta"],
        "gate_1": g["L1_ffn_gate_w"].T, "w1_1": g["L1_ffn_w1"].transpose(0, 2, 1), "b1_1": g["L1_ffn_b1"],
        "w2_1": g["L1_ffn_w2"].transpose(0, 2, 1), "b2_1": g["L1_ffn_b2"],
    }
    nc = bacc.Bacc("TRN2", target_bir_lowering=False, num_devices=1)
    a = Names()
    feed = {}
    for name, array in arrays.items():
        feed["in_" + name] = np.ascontiguousarray(array)
        handle = nc.dram_tensor("in_" + name, array.shape, mybir.dt.from_np(array.dtype), kind="ExternalInput")
        a.__dict__[name] = handle.ap()
    out = nc.dram_tensor("out_rows", [N, D], FP32, kind="ExternalOutput").ap()
    build(nc, a, out)
    r = run_bass_kernel_spmd(nc, [feed], core_ids=[0])
    rows = r.results[0]["out_rows"]
    return rows.reshape(B, J, 2, P, D).transpose(0, 1, 3, 2, 4).reshape(B, S, D)
```

```python
from contextlib import ExitStack

import concourse.bass as bass
from concourse import mybir

FP32 = mybir.dt.float32
BF16 = mybir.dt.bfloat16
I32 = mybir.dt.int32
ALU = mybir.AluOpType
ACT = mybir.ActivationFunctionType
AX = mybir.AxisListType

P = 128
B, S, D = 4, 1024, 256
N = B * S
H, HD = 16, 16
KC = D // P
NT = N // P
TB = S // P
E = 8
NH = B * H
L1, L2 = S // 2, S // 4
HALF = 512
SCALE = float(HD) ** -0.5
PARTS = 3
STACK = 6 * HD
RING = 3
MAXROWS = 2
SLOTS = 4


class Mem:

    uses = {}

    def __init__(self, nc, stack):
        self.nc, self.stack, self.sems = nc, stack, []

    def clear(self):
        for sem in self.sems:
            self.nc.gpsimd.sem_clear(sem)

    @staticmethod
    def label(name):
        n = Mem.uses[name] = Mem.uses.get(name, -1) + 1
        return f"{name}_{n}" if n else name

    def sb(self, name, shape, dt=FP32):
        return self.stack.enter_context(self.nc.sbuf_tensor(self.label(name), shape, dt))

    def ps(self, name, shape=(P, HALF), dt=FP32):
        return self.stack.enter_context(self.nc.psum_tensor(self.label(name), list(shape), dt))

    def sem(self, name):
        self.sems.append(self.stack.enter_context(self.nc.semaphore(self.label(name))))
        return self.sems[-1]


def wait_from(eng, sem, value):
    if not isinstance(value, int) or value > 0:
        eng.wait_ge(sem, value)


def wait_apart(eng, spare, sem, value):
    if not isinstance(value, int) or value > 0:
        eng.wait_ge(sem, value)
        eng.sem_inc(spare, 1)


def row_stats(nc, c, i):
    nc.vector.bn_stats(c.six[:, bass.ds(i, 1), :].rearrange("p a d -> p (a d)"),
                       c.y[:, bass.ds(i, 1), :].rearrange("p a d -> p (a d)"))


def peeled(eng, count, body):
    body(0)
    with eng.Fori(1, count) as i:
        body(i)


def peeled_ends(eng, count, body):
    body(0, True, False)
    with eng.Fori(1, count - 1) as i:
        body(i, False, False)
    body(count - 1, False, True)


def stage_constants(nc, mem, c):
    c.ident = mem.sb("ident", [P, P])
    c.identb = mem.sb("identb", [P, P], BF16)
    c.fold = mem.sb("fold", [P, 2 * 32])
    zeroed, made = mem.sem("consts_zeroed"), mem.sem("consts_made")
    with nc.Block() as block:
        @block.gpsimd
        def _(pool):
            nc.gpsimd.memset(c.ident[:, :], 0.0).then_inc(zeroed, 1)
            nc.gpsimd.memset(c.identb[:, :], 0.0).then_inc(zeroed, 1)
            nc.gpsimd.memset(c.fold[:, :], 0.0).then_inc(zeroed, 1)
            pool.wait_ge(zeroed, 3)
            for m in (c.ident, c.identb):
                nc.gpsimd.affine_select(out=m[:, :], in_=m[:, :], compare_op=ALU.not_equal, fill=1.0, base=0,
                                        pattern=[[-1, P]], channel_multiplier=1).then_inc(made, 1)
            fold = c.fold[:, :].rearrange("p (q r) -> p q r", q=2)
            for kh in range(2):
                pool.wait_ge(made, 2 + kh)
                nc.gpsimd.affine_select(out=fold, in_=fold, compare_op=ALU.not_equal, fill=1.0, base=-32 * kh,
                                        pattern=[[-64, 2], [-1, 32]], channel_multiplier=1).then_inc(made, 1)


def stage_project(nc, outer, a, c):
    CH = HALF
    with ExitStack() as stack:
        mem = Mem(nc, stack)
        w = mem.sb("w_qkv", [P, KC, 3 * D])
        bias = mem.sb("b_qk", [P, 2, KC])
        bv = mem.sb("bv_all", [P, D])
        xt = [mem.sb(f"xt{u}", [P, KC, CH]) for u in range(2)]
        full = [mem.sb(f"qk_full{u}", [P, CH]) for u in range(2)]
        part = [mem.sb(f"qk_part{u}", [P, PARTS, CH], BF16) for u in range(4)]
        rest = [mem.sb(f"qk_rest{u}", [P, CH]) for u in range(2)]
        pq = [mem.ps(f"ps_qk{u}") for u in range(4)]
        pv = [mem.ps(f"ps_v{u}") for u in range(4)]
        loaded_w = mem.sem("a_weights")
        loaded_x = [mem.sem(f"a_x{u}") for u in range(2)]
        qk_ready, v_ready = mem.sem("a_qk_ready"), mem.sem("a_v_ready")
        full_ready, part1_ready = mem.sem("a_full"), mem.sem("a_part1")
        rest_ready, part2_ready, part3_ready = mem.sem("a_rest"), mem.sem("a_part2"), mem.sem("a_part3")
        v_done = mem.sem("a_v_done")
        spare_p = mem.sem("a_spare")
        stored = [mem.sem(f"a_stored{u}") for u in range(4)]
        with nc.Block() as block:
            @block.sync
            def _(sp):
                sp.dma_start(w[:, :, :], a.wqkv.rearrange("(c p) n -> p c n", p=P)).then_inc(loaded_w, 16)
                sp.dma_start(bias[:, :, :], a.bqk).then_inc(loaded_w, 16)
                sp.dma_start(bv[:, :], a.bv.partition_broadcast(P)).then_inc(loaded_w, 16)

                def store(b):
                    for u in range(2):
                        for m in range(4):
                            sp.wait_ge(part3_ready, b * 8 + 4 * u + m + 1)
                            dst = (c.q_parts, c.k_parts)[m // 2]
                            sp.dma_start(
                                dst[bass.ds(b * H + (m % 2) * 8, 8), :, :, u * CH:(u + 1) * CH]
                                .rearrange("h r s t -> (h r) s t"), part[m][:, :, :]).then_inc(stored[m], 16)
                peeled(sp, B, store)
                for m in range(4):
                    sp.wait_ge(stored[m], 16 * 2 * B)

            @block.tensor
            def _(pe):
                pe.wait_ge(loaded_w, 48)

                def products(b):
                    for u in range(2):
                        pe.wait_ge(loaded_x[u], b * 16 + 16)
                        for m in range(4):
                            wait_from(pe, part1_ready, b * 8 + 4 * u + m - 3)
                            for k in range(KC):
                                mm = nc.tensor.matmul(pq[m][:, :], w[:, k, m * P:(m + 1) * P], xt[u][:, k, :],
                                                      start=(k == 0), stop=(k == KC - 1))
                            mm.then_inc(qk_ready, 1)
                        for t in range(4):
                            wait_from(pe, v_done, b * 8 + 4 * u + t - 3)
                            for k in range(KC):
                                mm = nc.tensor.matmul(pv[t][:, 0:D], xt[u][:, k, t * P:(t + 1) * P],
                                                      w[:, k, 2 * D:3 * D], start=(k == 0), stop=(k == KC - 1))
                            mm.then_inc(v_ready, 1)
                peeled(pe, B, products)

            @block.scalar
            def _(act):
                def evacuate(b):
                    for u in range(2):
                        wait_from(act, v_ready, b * 8 + 4 * u - 4)
                        act.dma_start(xt[u][:, :, :], a.xt[:, bass.ds(b * S + u * CH, CH)]
                                      .rearrange("(c p) n -> p c n", p=P)).then_inc(loaded_x[u], 16)
                        for m in range(4):
                            i = b * 8 + 4 * u + m
                            act.wait_ge(qk_ready, i + 1)
                            wait_from(act, rest_ready, i - 1)
                            nc.scalar.activation(full[m % 2][:, :], pq[m][:, :], ACT.Identity,
                                                 bias=bias[:, m // 2, m % 2:m % 2 + 1]).then_inc(full_ready, 1)
                            wait_from(act, stored[m], b * 32 + 16 * u)
                            nc.scalar.activation(part[m][:, 0, :], pq[m][:, :], ACT.Identity,
                                                 bias=bias[:, m // 2, m % 2:m % 2 + 1]).then_inc(part1_ready, 1)
                act.wait_ge(loaded_w, 48)
                peeled(act, B, evacuate)

            @block.gpsimd
            def _(pool):
                def second(b):
                    for u in range(2):
                        for m in range(4):
                            wait_apart(pool, spare_p, rest_ready, b * 8 + 4 * u + m + 1)
                            nc.gpsimd.tensor_copy(part[m][:, 1, :], rest[m % 2][:, :]).then_inc(part2_ready, 1)
                peeled(pool, B, second)

            @block.vector
            def _(dve):
                def left_over(i, m):
                    dve.wait_ge(part1_ready, i + 1)
                    wait_from(dve, part3_ready, i - 1)
                    nc.vector.tensor_tensor(rest[m % 2][:, :], full[m % 2][:, :], part[m][:, 0, :],
                                            ALU.subtract).then_inc(rest_ready, 1)

                def third(i, m):
                    dve.wait_ge(part2_ready, i + 1)
                    nc.vector.tensor_tensor(part[m][:, 2, :], rest[m % 2][:, :], part[m][:, 1, :],
                                            ALU.subtract).then_inc(part3_ready, 1)

                def split(b):
                    for u in range(2):
                        at = b * 8 + 4 * u
                        left_over(at, 0)
                        for m in range(4):
                            if m < 3:
                                left_over(at + m + 1, m + 1)
                            third(at + m, m)
                        for t in range(4):
                            dve.wait_ge(v_ready, b * 8 + 4 * u + t + 1)
                            nc.vector.tensor_tensor(
                                c.v[:, bass.ds(b * H, H), u * 4 + t, :],
                                pv[t][:, 0:D].rearrange("p (h r) -> p h r", h=H),
                                bv[:, :].rearrange("p (h r) -> p h r", h=H), ALU.add).then_inc(v_done, 1)
                dve.wait_ge(loaded_w, 48)
                peeled(dve, B, split)
        mem.clear()


def stage_attention(nc, outer, a, c):
    KT = TB
    with ExitStack() as stack:
        mem = Mem(nc, stack)
        qs = mem.sb("q_stack", [STACK + MAXROWS, SLOTS, S], BF16)
        ks = mem.sb("k_stack", [STACK + MAXROWS, SLOTS, S], BF16)
        pt = c.probs
        vpad = [mem.sb(f"v_padded{u}", [P, KT, 32]) for u in range(2)]
        o_sb = mem.sb("o_transposed", [P, HALF])
        unit_max = mem.sb("unit_max", [P, 2, 2, KT])
        best = [mem.sb(f"row_max{u}", [P, KT]) for u in range(2)]
        neg = mem.sb("neg_max", [P, KT])
        negp = [mem.sb(f"neg_parts{u}", [P, MAXROWS, KT], BF16) for u in range(2)]
        negt = [mem.sb(f"neg_rows{u}", [MAXROWS * KT, P], BF16) for u in range(2)]
        rec = mem.sb("o_reciprocal", [P, 2, 4])
        p_s = [mem.ps(f"ps_scores{u}", (P, S)) for u in range(2)]
        ring = [mem.ps(f"ps_ring{u}") for u in range(RING)]
        p_o = mem.ps("ps_o")
        slot_loaded = [mem.sem(f"b_slot{u}") for u in range(SLOTS)]
        LOADS, ROWS = 6 * 16, 7 * 16
        spare_p = mem.sem("b_spare")
        init = mem.sem("b_init")
        scores_ready, exp_done = mem.sem("b_scores"), mem.sem("b_exp")
        ring_ready, ring_used = mem.sem("b_ring_ready"), mem.sem("b_ring_used")
        best_done = mem.sem("b_best_done")
        neg_order, parts_done = mem.sem("b_neg_order"), mem.sem("b_parts")
        v_copied, pv_done, o_copied = mem.sem("b_v"), mem.sem("b_pv"), mem.sem("b_o")
        rec_done = mem.sem("b_rec")
        GROUPS = NH // SLOTS
        FOLD_AT, ROWS_AT = 4, 2

        def units(first, last, u):
            for kt in range(KT):
                if not (last and u >= 2):
                    yield kt, "max0"
                if kt == ROWS_AT and not (last and u == SLOTS - 1):
                    yield kt, "rows"
                if not (last and u >= 2):
                    yield kt, "max1"
                if kt == FOLD_AT and not (first and u == 0):
                    yield kt, "fold"

        PROLOGUE = 2 * 2 * KT + 1
        PER_GROUP = SLOTS * (2 * KT + 2)
        assert PER_GROUP % RING == 0

        def count_before(g, first, last, u):
            inside = sum(len(list(units(first, last, w))) for w in range(u))
            if first:
                return PROLOGUE + inside
            return g * PER_GROUP + (PROLOGUE - 1 + inside)

        def bank(g, first, last, u, j):
            base = PROLOGUE if first else PROLOGUE - 1
            return ring[(base + sum(len(list(units(first, last, w))) for w in range(u)) + j) % RING]


        def groups(eng, body):
            peeled_ends(eng, GROUPS, body)

        with nc.Block() as block:
            @block.sync
            def _(sp):
                def load(g, u):
                    for dst, src, deep in ((qs, c.q_parts, True), (ks, c.k_parts, False)):
                        at = 0
                        for n in (3, 2, 1):
                            if deep:
                                rows = src[bass.ds(g * SLOTS + u, 1), :, 0:n, :]
                                rows = rows.rearrange("h r s t -> (h r) s t")
                            else:
                                rows = src[bass.ds(g * SLOTS + u, 1), :, 3 - n:4 - n, :]
                                rows = rows.rearrange("h r s t -> (h r) s t").to_broadcast([HD, n, S])
                            sp.dma_start(dst[at:at + n * HD, u, :], rows).then_inc(slot_loaded[u], 16)
                            at += n * HD
                for u in range(3):
                    load(0, u)

                def rows(u, at):
                    sp.wait_ge(ring_used, at + 1)
                    sp.dma_start(qs[STACK:STACK + MAXROWS, u, :].rearrange("s (t q) -> s t q", t=KT),
                                 negt[u % 2][:, :]).then_inc(slot_loaded[u], 16)

                def body(g, first, last):
                    for u in range(SLOTS):
                        if first and u == 0:
                            rows(0, PROLOGUE - 1)
                        if not (last and u > 0):
                            wait_from(sp, scores_ready, (g * SLOTS + u) * KT)
                            load(g + (1 if u > 0 else 0), (u + 3) % SLOTS)
                        for j, (_, kind) in enumerate(units(first, last, u)):
                            if kind == "rows":
                                rows((u + 1) % SLOTS, count_before(g, first, last, u) + j)
                groups(sp, body)

            @block.gpsimd
            def _(pool):
                nc.gpsimd.memset(ks[STACK:STACK + MAXROWS, :, :], 1.0).then_inc(init, 1)
                for j, v in enumerate(vpad):
                    pool.wait_ge(init, 2 * j + 1)
                    nc.gpsimd.memset(v[:, :, HD:HD + 1], 1.0).then_inc(init, 1)
                    pool.wait_ge(init, 2 * j + 2)
                    nc.gpsimd.memset(v[:, :, HD + 1:32], 0.0).then_inc(init, 1)
                pool.wait_ge(init, 5)

                def negate(n, u):
                    wait_apart(pool, spare_p, parts_done, n)
                    wait_apart(pool, spare_p, best_done, n + 1)
                    nc.gpsimd.tensor_scalar(neg[:, :], best[u % 2][:, :], -1.0, None, ALU.mult).then_inc(neg_order, 1)
                    wait_apart(pool, spare_p, neg_order, n * 2 + 1)
                    nc.gpsimd.tensor_copy(negp[u % 2][:, 0, :], neg[:, :]).then_inc(neg_order, 1)
                    wait_apart(pool, spare_p, neg_order, n * 2 + 2)
                    nc.gpsimd.tensor_tensor(negp[u % 2][:, 1, :], neg[:, :], negp[u % 2][:, 0, :],
                                            ALU.subtract).then_inc(parts_done, 1)

                for u in range(2):
                    negate(u, u)

                def body(g, first, last):
                    for u in range(SLOTS):
                        n = g * SLOTS + u
                        wait_apart(pool, spare_p, pv_done, (n - 1) * 4)
                        nc.gpsimd.tensor_copy(vpad[u % 2][:, :, 0:HD], c.v[:, bass.ds(n, 1), :, :]
                                              .rearrange("p h t r -> p (h t) r")).then_inc(v_copied, 1)
                        if not (last and u >= 2):
                            negate(n + 2, u)
                groups(pool, body)

            @block.tensor
            def _(pe):
                def claim(at):
                    wait_from(pe, ring_used, at - RING + 1)

                def max_unit(u, qt, half, at, out):
                    claim(at)
                    nc.tensor.matmul(out[:, :], qs[0:STACK, u, qt * P:(qt + 1) * P],
                                     ks[0:STACK, u, half * HALF:(half + 1) * HALF],
                                     start=True, stop=True).then_inc(ring_ready, 1)

                def rows_unit(n, u, at, out):
                    pe.wait_ge(parts_done, n + 1)
                    claim(at)
                    nc.tensor.transpose(out[0:MAXROWS * KT, 0:P // 2].bitcast(BF16),
                                        negp[u % 2][:, :, :].rearrange("p s t -> p (s t)"),
                                        c.identb[:, :]).then_inc(ring_ready, 1)

                def pv(n, u, i):
                    pe.wait_ge(exp_done, n * KT + 2 * i + 2)
                    if i == 0:
                        pe.wait_ge(v_copied, n + 1)
                        wait_from(pe, o_copied, n)
                    for kh in range(2):
                        for qh in range(2):
                            j = 2 * qh + kh
                            mm = nc.tensor.matmul(p_o[32 * j:32 * j + 32, :], vpad[u % 2][:, 2 * i + kh, :],
                                                  pt[:, 2 * i + kh, qh * HALF:(qh + 1) * HALF],
                                                  start=(i == 0), stop=(i == KT // 2 - 1))
                    mm.then_inc(pv_done, 1)

                def fold_unit(n, at, out):
                    pe.wait_ge(o_copied, n + 1)
                    claim(at)
                    for blk in range(4):
                        mm = nc.tensor.matmul(out[:, blk * 64:(blk + 1) * 64], o_sb[:, blk * P:(blk + 1) * P],
                                              c.fold[:, :], start=True, stop=True)
                    mm.then_inc(ring_ready, 1)

                pe.wait_ge(init, 5)
                for u in range(2):
                    pe.wait_ge(slot_loaded[u], LOADS)
                    for m in range(2 * KT):
                        at = u * 2 * KT + m
                        max_unit(u, m // 2, m % 2, at, ring[at % RING])
                rows_unit(0, 0, PROLOGUE - 1, ring[(PROLOGUE - 1) % RING])

                def body(g, first, last):
                    for u in range(SLOTS):
                        n = g * SLOTS + u
                        ahead = not (last and u >= 2)
                        before = count_before(g, first, last, u)
                        todo = list(enumerate(units(first, last, u)))

                        def emit(kt, kinds):
                            for j, (step, kind) in todo:
                                if step != kt or kind not in kinds:
                                    continue
                                at, out = before + j, bank(g, first, last, u, j)
                                if kind == "rows":
                                    rows_unit(n + 1, u + 1, at, out)
                                elif kind == "fold":
                                    fold_unit(n - 1, at, out)
                                else:
                                    max_unit((u + 2) % SLOTS, kt, int(kind[3]), at, out)
                        for kt in range(KT):
                            if kt == 0:
                                pe.wait_ge(slot_loaded[u], g * ROWS + ROWS)
                                if ahead:
                                    pe.wait_ge(slot_loaded[(u + 2) % SLOTS], (g + (u >= 2)) * ROWS + LOADS)
                            emit(kt, ("max0",))
                            wait_from(pe, exp_done, n * KT + kt - 1)
                            for half in range(2):
                                mm = nc.tensor.matmul(p_s[kt % 2][:, half * HALF:(half + 1) * HALF],
                                                      ks[:, u, kt * P:(kt + 1) * P],
                                                      qs[:, u, half * HALF:(half + 1) * HALF],
                                                      start=True, stop=True)
                            mm.then_inc(scores_ready, 1)
                            emit(kt, ("rows", "max1"))
                            if kt == 1 and not (first and u == 0):
                                pv(n - 1, u + 1, KT // 2 - 1)
                            if kt in (3, 5, 7):
                                pv(n, u, (kt - 3) // 2)
                            emit(kt, ("fold",))
                groups(pe, body)
                pv(NH - 1, SLOTS - 1, KT // 2 - 1)
                end = count_before(GROUPS - 1, False, True, SLOTS)
                fold_unit(NH - 1, end, bank(GROUPS - 1, False, True, SLOTS, 0))

            @block.scalar
            def _(act):
                def copy_o(n, units_before):
                    act.wait_ge(pv_done, (n + 1) * (KT // 2))
                    act.wait_ge(ring_ready, units_before)
                    nc.scalar.activation(o_sb[:, :], p_o[:, :], ACT.Copy).then_inc(o_copied, 1)

                def body(g, first, last):
                    for u in range(SLOTS):
                        n = g * SLOTS + u
                        for kt in range(KT):
                            act.wait_ge(scores_ready, n * KT + kt + 1)
                            if kt % 2 == 0:
                                wait_from(act, pv_done, (n - 1) * (KT // 2) + kt // 2 + 1)
                            nc.scalar.activation(pt[:, kt, :], p_s[kt % 2][:, :], ACT.Exp, scale=SCALE)\
                                .then_inc(exp_done, 1)
                            if kt == 1 and not (first and u == 0):
                                copy_o(n - 1, count_before(g, first, last, u))
                groups(act, body)
                copy_o(NH - 1, count_before(GROUPS - 1, False, True, SLOTS))

            @block.vector
            def _(dve):
                def reduce_unit(n, u, qt, half, at, src):
                    if half == 0 and qt == 0:
                        wait_from(dve, best_done, n - 1)
                    dve.wait_ge(ring_ready, at + 1)
                    nc.vector.tensor_reduce(unit_max[:, u % 2, half, qt:qt + 1], src[:, :], axis=AX.X,
                                            op=ALU.max).then_inc(ring_used, 1)

                def combine(n, u, at):
                    dve.wait_ge(ring_used, at + 1)
                    wait_from(dve, parts_done, n - 1)
                    nc.vector.tensor_tensor(best[u % 2][:, :], unit_max[:, u % 2, 0, :], unit_max[:, u % 2, 1, :],
                                            ALU.max).then_inc(best_done, 1)

                def copy_rows(u, at, src):
                    dve.wait_ge(ring_ready, at + 1)
                    nc.vector.tensor_copy(negt[u % 2][:, :], src[0:MAXROWS * KT, 0:P // 2].bitcast(BF16))\
                        .then_inc(ring_used, 1)

                def normalise(n, at, src):
                    dve.wait_ge(ring_ready, at + 1)
                    wait_from(dve, ring_used, at)
                    o = src[:, 0:256].rearrange("p (b q r) -> p q b r", b=4, q=2)
                    nc.vector.reciprocal(rec[:, :, :], o[:, :, :, HD]).then_inc(rec_done, 1)
                    dve.wait_ge(rec_done, n + 1)
                    nc.vector.tensor_tensor(
                        c.ao[:, bass.ds(n, 1), :, :].rearrange("p h (q b) r -> p (h q) b r", q=2),
                        o[:, :, :, 0:HD], rec[:, :, :].unsqueeze(3).to_broadcast([P, 2, 4, HD]),
                        ALU.mult).then_inc(ring_used, 1)

                for u in range(2):
                    for m in range(2 * KT):
                        at = u * 2 * KT + m
                        reduce_unit(u, u, m // 2, m % 2, at, ring[at % RING])
                    combine(u, u, at)
                copy_rows(0, PROLOGUE - 1, ring[(PROLOGUE - 1) % RING])

                def body(g, first, last):
                    for u in range(SLOTS):
                        n = g * SLOTS + u
                        before = count_before(g, first, last, u)
                        for j, (kt, kind) in enumerate(units(first, last, u)):
                            at, src = before + j, bank(g, first, last, u, j)
                            if kind == "rows":
                                copy_rows(u + 1, at, src)
                            elif kind == "fold":
                                normalise(n - 1, at, src)
                            else:
                                reduce_unit(n + 2, u, kt, int(kind[3]), at, src)
                                if kt == KT - 1 and kind == "max1":
                                    combine(n + 2, u, at)
                groups(dve, body)
                end = count_before(GROUPS - 1, False, True, SLOTS)
                normalise(NH - 1, end, bank(GROUPS - 1, False, True, SLOTS, 0))
        mem.clear()


class Chain:

    def __init__(self, eng, sem):
        self.eng, self.sem, self.count = eng, sem, 0

    def __call__(self, instruction):
        instruction.then_inc(self.sem, 1)
        self.count += 1
        self.eng.wait_ge(self.sem, self.count)


def bcast(ap, shape):
    return ap.to_broadcast(shape)


def stage_output(nc, outer, a, c):
    PAIRS, HB = TB // 2, TB // 2
    with ExitStack() as stack:
        mem = Mem(nc, stack)
        wo = mem.sb("w_o", [P, KC, D])
        bo = mem.sb("bo_all", [P, D])
        xin = [mem.sb(f"c_x{u}", [P, HB, D]) for u in range(2)]
        at = [mem.sb(f"c_attn{u}", [P, 2, D]) for u in range(2)]
        ot = [mem.sb(f"c_attn_t{u}", [P, 2, KC, P]) for u in range(2)]
        p_tr = [mem.ps(f"c_ps_t{u}") for u in range(2)]
        p_y = [mem.ps(f"c_ps_y{u}") for u in range(2)]
        loaded_w, loaded_b = mem.sem("c_weights"), mem.sem("c_loaded_bias")
        loaded_x = [mem.sem(f"c_loaded_x{u}") for u in range(2)]
        staged, bias_added = mem.sem("c_staged"), mem.sem("c_bias")
        turned, copied, made = mem.sem("c_turned"), mem.sem("c_copied"), mem.sem("c_made")
        summed, spare, spare_p = mem.sem("c_summed"), mem.sem("c_spare"), mem.sem("c_spare_pool")
        ao = c.ao.rearrange("p (b h) t r -> p b h t r", b=B)
        tokens = a.x.rearrange("(b h t p) d -> b h p t d", b=B, h=2, p=P)
        with nc.Block() as block:
            @block.sync
            def _(sp):
                sp.dma_start(wo[:, :, :], a.wo.rearrange("(c p) n -> p c n", p=P)).then_inc(loaded_w, 16)
                sp.dma_start(bo[:, :], a.bo.partition_broadcast(P)).then_inc(loaded_b, 16)

                def load(b):
                    for h in range(2):
                        wait_from(sp, summed, b * PAIRS + 2 * h - 2)
                        sp.dma_start(xin[h][:, :, :], tokens[bass.ds(b, 1), h, :, :, :]
                                     .rearrange("b p t d -> (b p) t d")).then_inc(loaded_x[h], 16)
                peeled(sp, B, load)

            @block.gpsimd
            def _(pool):
                def add_bias(b):
                    for h in range(2):
                        wait_apart(pool, spare_p, loaded_x[h], b * 16 + 16)
                        nc.gpsimd.tensor_tensor(xin[h][:, :, :], xin[h][:, :, :],
                                                bcast(bo[:, :].unsqueeze(1), [P, HB, D]), ALU.add)\
                            .then_inc(bias_added, 1)
                pool.wait_ge(loaded_b, 16)
                peeled(pool, B, add_bias)

            @block.tensor
            def _(pe):
                def turn(i, s):
                    pe.wait_ge(staged, i + 1)
                    wait_from(pe, copied, i - 1)
                    for j in range(2):
                        for k in range(KC):
                            col = (j * KC + k) * P
                            mm = nc.tensor.transpose(p_tr[s % 2][:, col:col + P],
                                                     at[s % 2][:, j, k * P:(k + 1) * P], c.ident[:, :])
                    mm.then_inc(turned, 1)

                def product(i, s):
                    pe.wait_ge(copied, i + 1)
                    wait_from(pe, summed, i - 1)
                    for j in range(2):
                        for k in range(KC):
                            mm = nc.tensor.matmul(p_y[s % 2][:, j * D:(j + 1) * D], ot[s % 2][:, j, k, :],
                                                  wo[:, k, :], start=(k == 0), stop=(k == KC - 1))
                    mm.then_inc(made, 1)

                def pairs(b, first, last):
                    for s in range(PAIRS):
                        if not (last and s == PAIRS - 1):
                            turn(b * PAIRS + s + 1, s + 1)
                        product(b * PAIRS + s, s)
                pe.wait_ge(loaded_w, 16)
                turn(0, 0)
                peeled_ends(pe, B, pairs)

            @block.scalar
            def _(act):
                def stage(b, s):
                    wait_from(act, turned, b * PAIRS + s - 1)
                    nc.scalar.activation(at[s % 2][:, :, :].rearrange("p j (h r) -> p h j r", h=H),
                                         ao[:, bass.ds(b + s // PAIRS, 1), :, s % PAIRS * 2:s % PAIRS * 2 + 2, :]
                                         .rearrange("p b h t r -> p (b h) t r"), ACT.Copy).then_inc(staged, 1)

                def copies(b, first, last):
                    for s in range(PAIRS):
                        if not (last and s == PAIRS - 1):
                            stage(b, s + 1)
                        act.wait_ge(turned, b * PAIRS + s + 1)
                        wait_from(act, made, b * PAIRS + s - 1)
                        nc.scalar.activation(ot[s % 2][:, :, :, :].rearrange("p j c n -> p (j c n)"),
                                             p_tr[s % 2][:, :], ACT.Copy).then_inc(copied, 1)
                stage(0, 0)
                peeled_ends(act, B, copies)

            @block.vector
            def _(dve):
                def add(b):
                    for s in range(PAIRS):
                        i = b * PAIRS + s
                        dve.wait_ge(made, i + 1)
                        if s % 2 == 0:
                            dve.wait_ge(bias_added, b * 2 + s // 2 + 1)
                        nc.vector.tensor_tensor(
                            c.y[:, bass.ds(2 * i, 2), :].rearrange("p a d -> p (a d)"), p_y[s % 2][:, :],
                            xin[s // 2][:, s % 2 * 2:s % 2 * 2 + 2, :].rearrange("p a d -> p (a d)"), ALU.add)\
                            .then_inc(summed, 1)
                        wait_apart(dve, spare, summed, i + 1)
                        for j in range(2):
                            row_stats(nc, c, 2 * i + j)
                peeled(dve, B, add)
        mem.clear()


def stage_load_stats(nc, outer, c, src):
    with ExitStack() as stack:
        mem = Mem(nc, stack)
        loaded = [mem.sem(f"l_loaded{b}") for b in range(B)]
        rows = src.rearrange("(i p) d -> p i d", p=P)
        with nc.Block() as block:
            @block.sync
            def _(sp):
                for b in range(B):
                    sp.dma_start(c.y[:, b * TB:(b + 1) * TB, :], rows[:, b * TB:(b + 1) * TB, :])\
                        .then_inc(loaded[b], 16)

            @block.vector
            def _(dve):
                for b in range(B):
                    dve.wait_ge(loaded[b], 16)
                    with dve.Fori(b * TB // 4, (b + 1) * TB // 4) as g:
                        for t in range(4):
                            row_stats(nc, c, g * 4 + t)
        mem.clear()


def stage_rstd(nc, outer, c):
    with ExitStack() as stack:
        mem = Mem(nc, stack)
        var = mem.sb("r_var", [P, NT])
        root = mem.sb("r_root", [P, NT])
        tmp = mem.sb("r_tmp", [P, NT])
        var_ready, root_ready, order = mem.sem("r_var_ready"), mem.sem("r_root_ready"), mem.sem("r_order")
        with nc.Block() as block:
            @block.vector
            def _(dve):
                link = Chain(dve, order)
                even, odd = c.six[:, :, 1], c.six[:, :, 4]
                link(nc.vector.tensor_tensor(c.mean[:, :], even, odd, ALU.add))
                link(nc.vector.tensor_scalar(c.mean[:, :], c.mean[:, :], 0.5, None, ALU.mult))
                link(nc.vector.tensor_tensor(tmp[:, :], even, c.mean[:, :], ALU.subtract))
                link(nc.vector.tensor_tensor(tmp[:, :], tmp[:, :], tmp[:, :], ALU.mult))
                link(nc.vector.tensor_tensor(var[:, :], c.six[:, :, 2], c.six[:, :, 5], ALU.add))
                link(nc.vector.scalar_tensor_tensor(out=var[:, :], in0=var[:, :], scalar=1.0 / D, in1=tmp[:, :],
                                                    op0=ALU.mult, op1=ALU.add))
                nc.vector.tensor_scalar(var[:, :], var[:, :], 1e-5, None, ALU.add).then_inc(var_ready, 1)
                dve.wait_ge(root_ready, 1)
                link(nc.vector.reciprocal(c.rstd[:, :], root[:, :]))
                link(nc.vector.tensor_tensor(tmp[:, :], c.rstd[:, :], c.rstd[:, :], ALU.mult))
                link(nc.vector.tensor_tensor(tmp[:, :], tmp[:, :], var[:, :], ALU.mult))
                link(nc.vector.tensor_scalar(tmp[:, :], tmp[:, :], -0.5, 1.5, ALU.mult, ALU.add))
                link(nc.vector.tensor_tensor(c.rstd[:, :], c.rstd[:, :], tmp[:, :], ALU.mult))
                link(nc.vector.scalar_tensor_tensor(out=c.nmr[:, :], in0=c.mean[:, :], scalar=-1.0,
                                                    in1=c.rstd[:, :], op0=ALU.mult, op1=ALU.mult))

            @block.scalar
            def _(act):
                act.wait_ge(var_ready, 1)
                nc.scalar.activation(root[:, :], var[:, :], ACT.Sqrt).then_inc(root_ready, 1)
        mem.clear()


def normalised(nc, c, out, i):
    return nc.vector.tensor_scalar(out, c.y[:, bass.ds(i, 1), :].rearrange("p a d -> p (a d)"),
                                   c.rstd[:, bass.ds(i, 1)], c.nmr[:, bass.ds(i, 1)], ALU.mult, ALU.add)


def stage_gate(nc, outer, c, wgate, rows):
    PAIRS, HB = TB // 2, TB // 2
    with ExitStack() as stack:
        mem = Mem(nc, stack)
        wg = mem.sb("g_w", [P, KC, E])
        st = [mem.sb(f"g_rows{u}", [P, HB, D]) for u in range(2)]
        xt = [mem.sb(f"g_rows_t{u}", [P, 2, KC, P]) for u in range(2)]
        p_tr = [mem.ps(f"g_ps_t{u}") for u in range(2)]
        p_g = mem.ps("g_ps_logits")
        loaded_w = mem.sem("g_weights")
        ready, turned, copied, gated = mem.sem("g_ready"), mem.sem("g_turned"), mem.sem("g_copied"), mem.sem("g_gated")
        stored = [mem.sem(f"g_stored{u}") for u in range(2)]
        done = mem.sem("g_done")
        halves = rows.rearrange("(b h t p) d -> b h p t d", b=B, h=2, p=P)
        with nc.Block() as block:
            @block.sync
            def _(sp):
                sp.dma_start(wg[:, :, :], wgate.rearrange("(c p) e -> p c e", p=P)).then_inc(loaded_w, 16)

                def store(b):
                    for h in range(2):
                        sp.wait_ge(ready, b * PAIRS + 2 * h + 2)
                        sp.dma_start(halves[bass.ds(b, 1), h, :, :, :].rearrange("b p t d -> (b p) t d"),
                                     st[h][:, :, :]).then_inc(stored[h], 16)
                peeled(sp, B, store)
                for h in range(2):
                    sp.wait_ge(stored[h], 16 * B)

            @block.vector
            def _(dve):
                def norm(b):
                    for s in range(PAIRS):
                        wait_from(dve, turned, (b - 1) * PAIRS + s + 1)
                        if s % 2 == 0:
                            wait_from(dve, stored[s // 2], b * 16)
                        normalised(nc, c, st[s // 2][:, s % 2 * 2, :], b * TB + 2 * s)
                        normalised(nc, c, st[s // 2][:, s % 2 * 2 + 1, :], b * TB + 2 * s + 1).then_inc(ready, 1)
                peeled(dve, B, norm)
                dve.wait_ge(gated, NT // 2)
                nc.vector.tensor_copy(c.logits[:, :], p_g[:, 0:NT * E]).then_inc(done, 1)

            @block.tensor
            def _(pe):
                def turn(i, s):
                    pe.wait_ge(ready, i + 1)
                    wait_from(pe, copied, i - 1)
                    for j in range(2):
                        for k in range(KC):
                            col = (j * KC + k) * P
                            mm = nc.tensor.transpose(p_tr[s % 2][:, col:col + P],
                                                     st[s // 2][:, s % 2 * 2 + j, k * P:(k + 1) * P], c.ident[:, :])
                    mm.then_inc(turned, 1)

                def gate(i, s):
                    pe.wait_ge(copied, i + 1)
                    for j in range(2):
                        for k in range(KC):
                            mm = nc.tensor.matmul(p_g[:, bass.ds((2 * i + j) * E, E)], xt[s % 2][:, j, k, :],
                                                  wg[:, k, :], start=(k == 0), stop=(k == KC - 1))
                    mm.then_inc(gated, 1)

                def pairs(b, first, last):
                    for s in range(PAIRS):
                        if not (last and s == PAIRS - 1):
                            turn(b * PAIRS + s + 1, (s + 1) % PAIRS)
                        gate(b * PAIRS + s, s)
                pe.wait_ge(loaded_w, 16)
                turn(0, 0)
                peeled_ends(pe, B, pairs)

            @block.scalar
            def _(act):
                def copy(b):
                    for s in range(PAIRS):
                        act.wait_ge(turned, b * PAIRS + s + 1)
                        wait_from(act, gated, b * PAIRS + s - 1)
                        nc.scalar.activation(xt[s % 2][:, :, :, :].rearrange("p j c n -> p (j c n)"),
                                             p_tr[s % 2][:, :], ACT.Copy).then_inc(copied, 1)
                peeled(act, B, copy)
        mem.clear()


def stage_route(nc, outer, c, tiles, fixed, rows, sums):
    with ExitStack() as stack:
        mem = Mem(nc, stack)
        G = NT * E
        names = ("ex", "pr", "pr2", "eq", "cand", "oh1", "oh2", "mask", "incl", "pos", "prod")
        t = {n: mem.sb(f"e_{n}", [P, NT, E]) for n in names}
        maskb = mem.sb("e_maskb", [P, G], BF16)
        tri = mem.sb("e_tri", [P, P], BF16)
        ones = mem.sb("e_ones", [P, P], BF16)
        totals = mem.sb("e_totals", [P, NT, E])
        unit = mem.sb("e_unit", [P, NT])
        iota_e = mem.sb("e_iota_e", [P, E])
        iota_p = mem.sb("e_iota_p", [P, P])
        iota_t = mem.sb("e_iota_t", [P, tiles])
        token = mem.sb("e_token", [P, NT])
        small = {n: mem.sb(f"e_{n}", [P, NT]) for n in ("mx", "sm", "rc", "w1", "w2", "cm", "slot")}
        sloti = mem.sb("e_sloti", [P, NT], I32)
        hi_i = mem.sb("e_hi_i", [P, NT], I32)
        hi = mem.sb("e_hi", [P, 2, NT])
        lo = mem.sb("e_lo", [P, 2, NT])
        cnt = {n: mem.sb(f"e_{n}", [P, E]) for n in ("need", "endt", "start", "drop")}
        need_i = mem.sb("e_need_i", [P, E], I32)
        own = mem.sb("e_own", [P, tiles, E - 1])
        ownf = mem.sb("e_ownf", [P, tiles])
        oh_lo = [mem.sb(f"e_oh_lo{u}", [P, P]) for u in range(4)]
        oh_hi = [mem.sb(f"e_oh_hi{u}", [P, 2, tiles]) for u in range(4)]
        table = mem.sb("e_table", [P, 2, tiles])
        p_r, p_n, p_m = mem.ps("e_ps_rank"), mem.ps("e_ps_totals"), mem.ps("e_ps_map")
        made, shifted, ex_done = mem.sem("e_made"), mem.sem("e_shifted"), mem.sem("e_ex")
        mask_done, ranked, order = mem.sem("e_mask_done"), mem.sem("e_ranked"), mem.sem("e_order")
        hi_done, mapped = mem.sem("e_hi_done"), mem.sem("e_mapped")
        sums_copied = mem.sem("e_sums_copied")
        GE = [P, NT, E]
        with nc.Block() as block:
            @block.sync
            def _(sp):
                for b in range(B):
                    sp.dma_start(sums[b * S:(b + 1) * S, :], rows[b * S:(b + 1) * S, :]).then_inc(sums_copied, 16)
                sp.wait_ge(sums_copied, 16 * B)

            @block.gpsimd
            def _(pool):
                imprecise = dict(allow_small_or_imprecise_dtypes=True)
                nc.gpsimd.iota(iota_e[:, :], pattern=[[1, E]], base=0, channel_multiplier=0, **imprecise).then_inc(made, 1)
                nc.gpsimd.iota(iota_p[:, :], pattern=[[1, P]], base=0, channel_multiplier=0, **imprecise).then_inc(made, 1)
                nc.gpsimd.iota(iota_t[:, :], pattern=[[1, tiles]], base=0, channel_multiplier=0, **imprecise)\
                    .then_inc(made, 1)
                nc.gpsimd.iota(token[:, :], pattern=[[P, NT]], base=-N, channel_multiplier=1, **imprecise)\
                    .then_inc(made, 1)
                nc.gpsimd.memset(ones[:, :], 1.0).then_inc(made, 1)
                nc.gpsimd.memset(tri[:, :], 1.0).then_inc(made, 1)
                pool.wait_ge(made, 6)
                nc.gpsimd.affine_select(out=tri[:, :], in_=tri[:, :], compare_op=ALU.is_gt, fill=0.0, base=0,
                                        pattern=[[1, P]], channel_multiplier=-1).then_inc(made, 1)

            @block.scalar
            def _(act):
                act.wait_ge(shifted, 1)
                nc.scalar.activation(t["ex"][:, :, :], t["ex"][:, :, :], ACT.Exp).then_inc(ex_done, 1)

            @block.vector
            def _(dve):
                v = nc.vector
                link = Chain(dve, order)
                lg = c.logits[:, :].rearrange("p (i e) -> p i e", e=E)

                def wide(x):
                    return bcast(x[:, :].unsqueeze(2), GE)

                def per_expert(x):
                    return bcast(x[:, :].unsqueeze(1), GE)

                def first_of(values, best, onehot):
                    link(v.tensor_tensor(t["eq"][:, :, :], values, wide(best), ALU.is_equal))
                    link(v.scalar_tensor_tensor(out=t["cand"][:, :, :], in0=t["eq"][:, :, :], scalar=-float(E),
                                                in1=per_expert(iota_e), op0=ALU.mult, op1=ALU.add))
                    link(v.tensor_reduce(small["cm"][:, :], t["cand"][:, :, :], axis=AX.X, op=ALU.min))
                    link(v.tensor_tensor(onehot[:, :, :], t["cand"][:, :, :], wide(small["cm"]), ALU.is_equal))

                link(v.memset(unit[:, :], 1.0))
                link(v.tensor_reduce(small["mx"][:, :], lg, axis=AX.X, op=ALU.max))
                v.tensor_tensor(t["ex"][:, :, :], lg, wide(small["mx"]), ALU.subtract).then_inc(shifted, 1)
                dve.wait_ge(ex_done, 1)
                link(v.tensor_reduce(small["sm"][:, :], t["ex"][:, :, :], axis=AX.X, op=ALU.add))
                link(v.reciprocal(small["rc"][:, :], small["sm"][:, :]))
                link(v.tensor_tensor(t["pr"][:, :, :], t["ex"][:, :, :], wide(small["rc"]), ALU.mult))
                dve.wait_ge(made, 7)
                link(v.tensor_reduce(small["w1"][:, :], t["pr"][:, :, :], axis=AX.X, op=ALU.max))
                first_of(t["pr"][:, :, :], small["w1"], t["oh1"])
                link(v.scalar_tensor_tensor(out=t["pr2"][:, :, :], in0=t["oh1"][:, :, :], scalar=-2.0,
                                            in1=t["pr"][:, :, :], op0=ALU.mult, op1=ALU.add))
                link(v.tensor_reduce(small["w2"][:, :], t["pr2"][:, :, :], axis=AX.X, op=ALU.max))
                first_of(t["pr2"][:, :, :], small["w2"], t["oh2"])
                link(v.tensor_tensor(t["mask"][:, :, :], t["oh1"][:, :, :], t["oh2"][:, :, :], ALU.add))
                v.tensor_copy(maskb[:, :], t["mask"][:, :, :].rearrange("p i e -> p (i e)")).then_inc(mask_done, 1)
                dve.wait_ge(ranked, 1)
                link(v.tensor_copy(totals[:, :, :].rearrange("p i e -> p (i e)"), p_n[:, 0:G]))
                for e in range(E):
                    scan = v.tensor_tensor_scan(out=t["incl"][:, :, e], data0=unit[:, :], data1=totals[:, :, e],
                                                initial=0.0, op0=ALU.mult, op1=ALU.add)
                    link(scan)
                link(v.tensor_tensor(t["pos"][:, :, :].rearrange("p i e -> p (i e)"), p_r[:, 0:G],
                                     t["incl"][:, :, :].rearrange("p i e -> p (i e)"), ALU.add))
                link(v.tensor_tensor(t["pos"][:, :, :], t["pos"][:, :, :], totals[:, :, :], ALU.subtract))
                count = t["incl"][:, NT - 1, :]
                if fixed is None:
                    link(v.tensor_scalar(need_i[:, :], count, float(P - 1), None, ALU.add))
                    link(v.tensor_scalar(need_i[:, :], need_i[:, :], 7, None, ALU.arith_shift_right))
                    link(v.tensor_copy(cnt["need"][:, :], need_i[:, :]))
                    link(v.tensor_tensor_scan(out=cnt["endt"][:, :], data0=unit[:, 0:E], data1=cnt["need"][:, :],
                                              initial=0.0, op0=ALU.mult, op1=ALU.add))
                    link(v.tensor_tensor(cnt["start"][:, :], cnt["endt"][:, :], cnt["need"][:, :], ALU.subtract))
                    link(v.tensor_scalar(cnt["drop"][:, :], cnt["start"][:, :], float(P), None, ALU.mult))
                else:
                    link(v.tensor_scalar(cnt["start"][:, :], iota_e[:, :], float(fixed), None, ALU.mult))
                    link(v.tensor_scalar(cnt["drop"][:, :], count, float(fixed * P), float(4 * N), ALU.is_gt, ALU.mult))
                    link(v.scalar_tensor_tensor(out=cnt["drop"][:, :], in0=cnt["start"][:, :], scalar=float(P),
                                                in1=cnt["drop"][:, :], op0=ALU.mult, op1=ALU.add))
                link(v.tensor_tensor(t["pos"][:, :, :], t["pos"][:, :, :], per_expert(cnt["drop"]), ALU.add))
                for k, onehot in enumerate((t["oh1"], t["oh2"])):
                    link(v.tensor_tensor(t["prod"][:, :, :], t["pos"][:, :, :], onehot[:, :, :], ALU.mult))
                    link(v.tensor_reduce(small["slot"][:, :], t["prod"][:, :, :], axis=AX.X, op=ALU.add))
                    link(v.tensor_copy(sloti[:, :], small["slot"][:, :]))
                    link(v.tensor_scalar(hi_i[:, :], sloti[:, :], 7, None, ALU.arith_shift_right))
                    link(v.tensor_copy(hi[:, k, :], hi_i[:, :]))
                    link(v.scalar_tensor_tensor(out=lo[:, k, :], in0=hi[:, k, :], scalar=-float(P),
                                                in1=small["slot"][:, :], op0=ALU.mult, op1=ALU.add))
                link(v.tensor_tensor(own[:, :, :], bcast(iota_t[:, :].unsqueeze(2), [P, tiles, E - 1]),
                                     bcast(cnt["start"][:, 1:E].unsqueeze(1), [P, tiles, E - 1]), ALU.is_ge))
                link(v.tensor_reduce(ownf[:, :], own[:, :, :], axis=AX.X, op=ALU.add))
                link(v.tensor_copy(c.owner[:, 0:tiles], ownf[:, :]))
                gains = (small["w1"], small["w2"])

                def outer_products(g, first, last):
                    for u in range(4):
                        i, k = g * 2 + u // 2, u % 2
                        wait_from(dve, mapped, g * 4 + u - 3)
                        v.tensor_scalar(oh_lo[u][:, :], iota_p[:, :], lo[:, k, bass.ds(i, 1)], None, ALU.is_equal)
                        v.tensor_scalar(oh_hi[u][:, 0, :], iota_t[:, :], hi[:, k, bass.ds(i, 1)],
                                        token[:, bass.ds(i, 1)], ALU.is_equal, ALU.mult)
                        v.tensor_scalar(oh_hi[u][:, 1, :], iota_t[:, :], hi[:, k, bass.ds(i, 1)],
                                        gains[k][:, bass.ds(i, 1)], ALU.is_equal, ALU.mult).then_inc(hi_done, 1)
                peeled_ends(dve, NT // 2, outer_products)
                dve.wait_ge(mapped, 2 * NT)
                link(v.tensor_copy(table[:, :, :].rearrange("p a t -> p (a t)"), p_m[:, 0:2 * tiles]))
                link(v.tensor_scalar(c.scatter[:, 0:tiles], table[:, 0, :], float(N), None, ALU.add))
                link(v.tensor_scalar(c.gather[:, 0:tiles], table[:, 0, :], float(N), float(N - 1), ALU.add, ALU.min))
                link(v.tensor_copy(c.gains[:, 0:tiles], table[:, 1, :]))

            @block.tensor
            def _(pe):
                pe.wait_ge(mask_done, 1)
                pe.wait_ge(made, 7)
                nc.tensor.matmul(p_r[:, 0:G], tri[:, :], maskb[:, :], start=True, stop=True)
                nc.tensor.matmul(p_n[:, 0:G], ones[:, :], maskb[:, :], start=True, stop=True).then_inc(ranked, 1)

                def outer_products(g, first, last):
                    for u in range(4):
                        pe.wait_ge(hi_done, g * 4 + u + 1)
                        nc.tensor.matmul(p_m[:, 0:2 * tiles], oh_lo[u][:, :],
                                         oh_hi[u][:, :, :].rearrange("p a t -> p (a t)"),
                                         start=(first and u == 0), stop=(last and u == 3)).then_inc(mapped, 1)
                peeled_ends(pe, NT // 2, outer_products)
        mem.clear()


def stage_experts(nc, outer, c, tiles, fixed, F, w1, w2, b1, b2, func, rows, sums):
    FC = F // P
    HW = min(F, HALF)
    STEP, AHEAD = (2, 2) if fixed is None else (2 * fixed, fixed)
    with ExitStack() as stack:
        mem = Mem(nc, stack)
        ig = [mem.sb(f"m_ig{u}", [P, 1], I32) for u in range(AHEAD)]
        isc = [mem.sb(f"m_is{u}", [P, 1], I32) for u in range(2)]
        xg = [mem.sb(f"m_x{u}", [P, D]) for u in range(AHEAD)]
        xt = [mem.sb(f"m_xt{u}", [P, KC, P]) for u in range(2)]
        hs = [mem.sb(f"m_h{u}", [P, F]) for u in range(2)]
        ht = [mem.sb(f"m_ht{u}", [P, FC, P]) for u in range(2)]
        ys = [mem.sb(f"m_y{u}", [P, D]) for u in range(2)]
        p_x, p_y = mem.ps("m_ps_x"), mem.ps("m_ps_y")
        p_h = mem.ps("m_ps_h", (P, max(F, HALF)))
        p_t = mem.ps("m_ps_t", (P, max(F, HALF)))
        idx_g, idx_s = mem.sem("m_idx_g"), mem.sem("m_idx_s")
        gathered = [mem.sem(f"m_gathered{u}") for u in range(AHEAD)]
        added = [mem.sem(f"m_added{u}") for u in range(2)]
        x_turned, x_copied = mem.sem("m_x_turned"), mem.sem("m_x_copied")
        h_made, biased, act_done = mem.sem("m_h_made"), mem.sem("m_biased"), mem.sem("m_act_done")
        h_turned, h_copied = mem.sem("m_h_turned"), mem.sem("m_h_copied")
        y_made, y_biased, y_scaled = mem.sem("m_y_made"), mem.sem("m_y_biased"), mem.sem("m_y_scaled")
        spare_p = mem.sem("m_spare")
        halves = F // HW
        with nc.Block() as block:
            def steps(eng, body):
                peeled_ends(eng, tiles // STEP, body)

            @block.gpsimd
            def _(pool):
                def gather(t, u):
                    wait_apart(pool, spare_p, x_turned, t - AHEAD + 1)
                    nc.gpsimd.tensor_copy(ig[u][:, :], c.gather[:, bass.ds(t, 1)]).then_inc(idx_g, 1)
                    wait_apart(pool, spare_p, idx_g, t + 1)
                    pool.indirect_dma_start(out=xg[u][:, :], out_offset=None, in_=rows,
                                            in_offset=bass.IndirectOffsetOnAxis(ap=ig[u][:, :], axis=0))\
                        .then_inc(gathered[u], 16)

                def add(t, u):
                    nc.gpsimd.tensor_copy(isc[u][:, :], c.scatter[:, bass.ds(t, 1)]).then_inc(idx_s, 1)
                    wait_apart(pool, spare_p, idx_s, t + 1)
                    wait_apart(pool, spare_p, y_scaled, t + 1)
                    pool.indirect_dma_start(out=sums, out_offset=bass.IndirectOffsetOnAxis(ap=isc[u][:, :], axis=0),
                                            in_=ys[u][:, :], in_offset=None, bounds_check=N - 1, oob_is_err=False,
                                            compute_op=ALU.add).then_inc(added[u], 16)

                for u in range(AHEAD):
                    gather(u, u)

                def body(g, first, last):
                    t = g * STEP
                    for u in range(STEP):
                        if not (last and u >= STEP - AHEAD):
                            gather(t + u + AHEAD, u % AHEAD)
                        if first and u == 0:
                            continue
                        before = [t * 8 + (u // 2) * 16, t * 8 + ((u - 1) // 2) * 16]
                        if fixed is None:
                            wait_apart(pool, spare_p, added[u % 2], before[u % 2])
                        elif u - 1 in (0, fixed):
                            wait_apart(pool, spare_p, added[0], before[0])
                            wait_apart(pool, spare_p, added[1], before[1])
                        else:
                            wait_apart(pool, spare_p, added[(u - 1) % 2], before[(u - 1) % 2])
                        add(t + u - 1, (u - 1) % 2)
                steps(pool, body)
                wait_apart(pool, spare_p, added[0 if fixed is None else 1],
                           8 * tiles if fixed is None else 8 * tiles - 16)
                add(tiles - 1, 1)
                for u in range(2):
                    pool.wait_ge(added[u], 8 * tiles)

            @block.tensor
            def _(pe):
                def turn_x(g, u):
                    t, a = g * STEP + u, u % AHEAD
                    pe.wait_ge(gathered[a], g * (STEP // AHEAD * 16) + (u // AHEAD * 16 + 16))
                    wait_from(pe, x_copied, t)
                    for k in range(KC):
                        mm = nc.tensor.transpose(p_x[:, k * P:(k + 1) * P], xg[a][:, k * P:(k + 1) * P], c.ident[:, :])
                    mm.then_inc(x_turned, 1)

                owner = [pe.alloc_register(Mem.label("owner_pe")) for u in range(2)]

                def load_owner(t, u):
                    pe.reg_load(owner[u], c.owner[0:1, bass.ds(t, 1)])

                def expert(u):
                    return pe.snap(owner[u], min_val=0, max_val=E - 1)

                def first_product(t, u):
                    e = expert(u)
                    pe.wait_ge(x_copied, t + 1)
                    for half in range(halves):
                        wait_from(pe, biased, t * halves + half - halves + 1)
                        for k in range(KC):
                            mm = nc.tensor.matmul(p_h[:, half * HW:(half + 1) * HW], xt[u][:, k, :],
                                                  w1[:, bass.ds(e * KC + k, 1), half * HW:(half + 1) * HW]
                                                  .rearrange("p a f -> p (a f)"),
                                                  start=(k == 0), stop=(k == KC - 1))
                        mm.then_inc(h_made, 1)

                def turn_h(t, u):
                    for half in range(halves):
                        pe.wait_ge(act_done, t * halves + half + 1)
                        wait_from(pe, h_copied, t * halves + half - halves + 1)
                        for j in range(HW // P):
                            at = half * HW + j * P
                            mm = nc.tensor.transpose(p_t[:, at:at + P], hs[u][:, at:at + P], c.ident[:, :])
                        mm.then_inc(h_turned, 1)

                def second_product(t, u):
                    e = expert(u)
                    wait_from(pe, y_biased, t)
                    for f in range(FC):
                        if f % (HW // P) == 0:
                            pe.wait_ge(h_copied, t * halves + f // (HW // P) + 1)
                        mm = nc.tensor.matmul(p_y[:, 0:D], ht[u][:, f, :],
                                              w2[:, bass.ds(e * FC + f, 1), :].rearrange("p a d -> p (a d)"),
                                              start=(f == 0), stop=(f == FC - 1))
                    mm.then_inc(y_made, 1)

                def body(g, first, last):
                    t = g * STEP
                    for u in range(STEP):
                        first_product(t + u, u % 2)
                        if not (last and u == STEP - 1):
                            turn_x(g + (u + 1) // STEP, (u + 1) % STEP)
                        if not (first and u == 0):
                            second_product(t + u - 1, (u + 1) % 2)
                        if not (last and u == STEP - 1):
                            load_owner(t + u + 1, (u + 1) % 2)
                        turn_h(t + u, u % 2)
                load_owner(0, 0)
                turn_x(0, 0)
                steps(pe, body)
                second_product(tiles - 1, 1)

            @block.scalar
            def _(act):
                def copy_x(t, u):
                    act.wait_ge(x_turned, t + 1)
                    wait_from(act, h_made, (t - 1) * halves)
                    nc.scalar.activation(xt[u][:, :, :].rearrange("p c n -> p (c n)"), p_x[:, 0:D], ACT.Identity)\
                        .then_inc(x_copied, 1)

                def body(g, first, last):
                    t = g * STEP
                    for u in range(STEP):
                        for half in range(halves):
                            act.wait_ge(biased, (t + u) * halves + half + 1)
                            span = hs[u % 2][:, half * HW:(half + 1) * HW]
                            nc.scalar.activation(span, span, func).then_inc(act_done, 1)
                        if not (last and u == STEP - 1):
                            copy_x(t + u + 1, (u + 1) % 2)
                copy_x(0, 0)
                steps(act, body)

            @block.vector
            def _(dve):
                owner = [dve.alloc_register(Mem.label("owner_dve")) for u in range(2)]

                def load_owner(t, u):
                    dve.reg_load(owner[u], c.owner[0:1, bass.ds(t, 1)])

                def expert(u):
                    return dve.snap(owner[u], min_val=0, max_val=E - 1)

                def bias_h(t, u):
                    e = expert(u)
                    wait_from(dve, h_turned, (t - 1) * halves)
                    for half in range(halves):
                        dve.wait_ge(h_made, t * halves + half + 1)
                        nc.vector.tensor_tensor(hs[u][:, half * HW:(half + 1) * HW], p_h[:, half * HW:(half + 1) * HW],
                                                b1[:, bass.ds(e, 1), half * HW:(half + 1) * HW]
                                                .rearrange("p a f -> p (a f)"), ALU.add).then_inc(biased, 1)

                def copy_h(t, u):
                    wait_from(dve, y_made, t - 1)
                    for half in range(halves):
                        dve.wait_ge(h_turned, t * halves + half + 1)
                        nc.vector.tensor_copy(ht[u][:, :, :].rearrange("p f n -> p (f n)")[:, half * HW:(half + 1) * HW],
                                              p_t[:, half * HW:(half + 1) * HW]).then_inc(h_copied, 1)

                def scale_y(t, u):
                    e = expert(u)
                    dve.wait_ge(y_made, t + 1)
                    wait_from(dve, added[u], (t - u) * 8)
                    nc.vector.tensor_tensor(ys[u][:, :], p_y[:, 0:D], b2[:, bass.ds(e, 1), :]
                                            .rearrange("p a d -> p (a d)"), ALU.add).then_inc(y_biased, 1)
                    dve.wait_ge(y_biased, t + 1)
                    nc.vector.tensor_scalar(ys[u][:, :], ys[u][:, :], c.gains[:, bass.ds(t, 1)], None, ALU.mult)\
                        .then_inc(y_scaled, 1)

                def body(g, first, last):
                    t = g * STEP
                    for u in range(STEP):
                        bias_h(t + u, u % 2)
                        if not (first and u == 0):
                            scale_y(t + u - 1, (u + 1) % 2)
                        if not (last and u == STEP - 1):
                            load_owner(t + u + 1, (u + 1) % 2)
                        copy_h(t + u, u % 2)
                load_owner(0, 0)
                steps(dve, body)
                scale_y(tiles - 1, 1)
        mem.clear()


def stage_to_channels(nc, outer, a, c):
    with ExitStack() as stack:
        mem = Mem(nc, stack)
        p_tr = [mem.ps(f"t_ps{u}") for u in range(4)]
        ready, turned, copied = mem.sem("t_ready"), mem.sem("t_turned"), mem.sem("t_copied")
        PAIRS = [(0, 2), (1, 3), (4, 6), (5, 7)]
        with nc.Block() as block:
            @block.vector
            def _(dve):
                nc.vector.memset(c.xe[:, :, :, L1:L1 + 2], 0.0)
                nc.vector.memset(c.xo[:, :, :, 0:1], 0.0)
                with dve.Fori(0, B) as b:
                    for t in range(TB):
                        normalised(nc, c, c.x2[:, bass.ds(b * TB + t, 1), :].rearrange("p a d -> p (a d)"),
                                   b * TB + t).then_inc(ready, 1)

            @block.tensor
            def _(pe):
                for b in range(B):
                    for s, pair in enumerate(PAIRS):
                        pe.wait_ge(ready, b * TB + pair[1] + 1)
                        wait_from(pe, copied, (b - 1) * len(PAIRS) + s + 1)
                        for k in range(KC):
                            for j, t in enumerate(pair):
                                at = (k * 2 + j) * P
                                mm = nc.tensor.transpose(p_tr[s][:, at:at + P],
                                                         c.x2[:, b * TB + t, k * P:(k + 1) * P], c.ident[:, :])
                        mm.then_inc(turned, 1)

            @block.scalar
            def _(act):
                with act.Fori(0, B) as b:
                    for s, pair in enumerate(PAIRS):
                        act.wait_ge(turned, b * len(PAIRS) + s + 1)
                        dst, at = (c.xe, 0) if s % 2 == 0 else (c.xo, 1)
                        at += (pair[0] // 2) * P
                        nc.scalar.activation(
                            dst[:, :, bass.ds(b, 1), at:at + 2 * P].rearrange("p c b n -> p (c b) n"),
                            p_tr[s][:, :].rearrange("p (c n) -> p c n", c=KC), ACT.Copy).then_inc(copied, 1)
        mem.clear()


def stage_wavelet(nc, outer, a, c):
    with ExitStack() as stack:
        mem = Mem(nc, stack)
        fil = mem.sb("w_filters", [P, KC, 4, 4])
        fs = mem.sb("w_sums", [P, KC, 2, 5])
        diag = mem.sb("w_diag", [P, KC, 9, P])
        blocks = mem.sb("w_blocks", [P, P])
        low1 = mem.sb("w_low1", [P, KC, B, L1 + 2])
        high1 = mem.sb("w_high1", [P, KC, B, L1 + 2])
        low2 = mem.sb("w_low2", [P, KC, B, L2])
        high2 = mem.sb("w_high2", [P, KC, B, L2 + 2])
        q = mem.sb("w_q", [P, KC, B, L2])
        z = mem.sb("w_z", [P, KC, B])
        al = mem.sb("w_attn", [P, KC, B, L2 + 2])
        qt = mem.sb("w_qt", [P, B, KC, 2, P])
        kvm = mem.sb("w_kv", [P, B, KC, P])
        zm = mem.sb("w_zm", [P, B, KC, P])
        den = mem.sb("w_den", [P, KC, L2])
        htt = mem.sb("w_ht", [P, B, KC, 2, P])
        se, so = c.xe, c.xo
        banks = [mem.ps(f"w_ps{n}") for n in range(8)]
        loaded, order, made = mem.sem("w_loaded"), mem.sem("w_order"), mem.sem("w_made")
        diag_ready = mem.sem("w_diag_ready")
        high_made, high_copied = mem.sem("w_high_made"), mem.sem("w_high_copied")
        min_ready, exp_ready, q_ready = mem.sem("w_min"), mem.sem("w_exp"), mem.sem("w_q_ready")
        turned, qt_copied, ht_copied = mem.sem("w_turned"), mem.sem("w_qt_copied"), mem.sem("w_ht_copied")
        kv_made, kv_ready, nd_made, nd_used = mem.sem("w_kv_made"), mem.sem("w_kv_ready"), mem.sem("w_nd"), mem.sem("w_nd_used")
        syn_ready, tile_made, tile_used = mem.sem("w_syn_ready"), mem.sem("w_tile_made"), mem.sem("w_tile_used")
        with nc.Block() as block:
            @block.sync
            def _(sp):
                sp.dma_start(fil[:, :, :, :], a.filters).then_inc(loaded, 16)

            @block.gpsimd
            def _(pool):
                nc.gpsimd.memset(blocks[:, :], 1.0).then_inc(made, 1)
                pool.wait_ge(made, 1)
                bl = blocks[:, :].rearrange("p (h r) -> p h r", r=HD)
                nc.gpsimd.affine_select(out=bl, in_=bl, compare_op=ALU.is_ge, fill=0.0, base=0,
                                        pattern=[[-HD, P // HD], [0, HD]], channel_multiplier=1).then_inc(made, 1)
                pool.wait_ge(made, 2)
                nc.gpsimd.affine_select(out=bl, in_=bl, compare_op=ALU.is_ge, fill=0.0, base=HD - 1,
                                        pattern=[[HD, P // HD], [0, HD]], channel_multiplier=-1).then_inc(made, 1)

            @block.vector
            def _(dve):
                v = nc.vector
                link = Chain(dve, order)
                for x in (low1, high1, high2, al):
                    v.memset(x[:, :, :, 0:1], 0.0)
                    n = x.shape[3]
                    v.memset(x[:, :, :, n - 1:n], 0.0)
                dve.wait_ge(loaded, 16)
                for f in range(2):
                    for n, taps in enumerate(((0,), (1, 2), (3,), (0, 1), (2, 3))):
                        for k in range(KC):
                            src = fil[:, k, 2 + f, taps[0]:taps[0] + 1]
                            dst = fs[:, k, f, n:n + 1]
                            last = (v.tensor_copy(dst, src) if len(taps) == 1 else
                                    v.tensor_tensor(dst, src, fil[:, k, 2 + f, taps[1]:taps[1] + 1], ALU.add))
                link(last)
                for k in range(KC):
                    for n in range(4):
                        last = v.tensor_scalar(diag[:, k, n, :], c.ident[:, :], fil[:, k, 1, n:n + 1], None, ALU.mult)
                last.then_inc(diag_ready, 1)
                for k in range(KC):
                    for n in range(5):
                        last = v.tensor_scalar(diag[:, k, 4 + n, :], c.ident[:, :], fs[:, k, 1, n:n + 1], None, ALU.mult)
                last.then_inc(diag_ready, 1)

                def taps(dst, terms, begin=True):
                    for n, (src, scalar) in enumerate(terms):
                        for k in range(KC):
                            if n == 0 and begin:
                                last = v.tensor_scalar(dst(k), src(k), scalar(k), None, ALU.mult)
                            else:
                                last = v.scalar_tensor_tensor(out=dst(k), in0=src(k), scalar=scalar(k), in1=dst(k),
                                                              op0=ALU.mult, op1=ALU.add)
                        link(last)

                def part(x, at, n, step=1):
                    return lambda k: x[:, k, :, at:at + (n - 1) * step + 1:step]

                def tap(f, n):
                    return lambda k: fil[:, k, f, n:n + 1]

                def total(f, n):
                    return lambda k: fs[:, k, f, n:n + 1]

                taps(part(low1, 1, L1), [(part(c.xo, 0, L1), tap(0, 0)), (part(c.xe, 0, L1), tap(0, 1)),
                                         (part(c.xo, 1, L1), tap(0, 2)), (part(c.xe, 1, L1), tap(0, 3))])
                taps(lambda k: low2[:, k, :, :], [(part(low1, n, L2, 2), tap(0, n)) for n in range(4)])
                flat = low2[:, :, :, :].rearrange("p c b n -> p (c b n)")
                qf = q[:, :, :, :].rearrange("p c b n -> p (c b n)")
                v.tensor_scalar(qf, flat, 0.0, None, ALU.min).then_inc(min_ready, 1)
                taps(part(high2, 1, L2), [(part(low1, n, L2, 2), tap(1, n)) for n in range(4)])
                dve.wait_ge(exp_ready, 1)
                v.scalar_tensor_tensor(out=qf, in0=flat, scalar=0.0, in1=qf, op0=ALU.max, op1=ALU.add)\
                    .then_inc(q_ready, 1)
                dve.wait_ge(q_ready, 1)
                link(v.tensor_reduce(z[:, :, :], q[:, :, :, :], axis=AX.X, op=ALU.add))
                dve.wait_ge(made, 3)
                for b in range(B):
                    for k in range(KC):
                        v.tensor_scalar(zm[:, b, k, :], blocks[:, :], z[:, k, b:b + 1], None, ALU.mult)
                    dve.wait_ge(turned, 2 * b + 1)
                    v.tensor_copy(qt[:, b, :, :, :].rearrange("p c j n -> p (c j n)"), banks[2 * b][:, :])\
                        .then_inc(qt_copied, 1)
                even, odd = part(low1, 1, L2, 2), part(low1, 2, L2, 2)

                def doubled(dst_even, dst_odd, src, f, n, begin):
                    taps(dst_even, [(part(src, 0, n), total(f, 0)), (part(src, 1, n), total(f, 1)),
                                    (part(src, 2, n), total(f, 2))], begin)
                    taps(dst_odd, [(part(src, 1, n), total(f, 3)), (part(src, 2, n), total(f, 4))], begin)
                doubled(even, odd, high2, 1, L2, True)
                for b in range(B):
                    dve.wait_ge(kv_made, b + 1)
                    for k in range(KC):
                        last = v.tensor_tensor(kvm[:, b, k, :], banks[b][:, k * P:(k + 1) * P], blocks[:, :], ALU.mult)
                    last.then_inc(kv_ready, 1)
                for b in range(B):
                    dve.wait_ge(nd_made, b + 1)
                    wait_from(dve, nd_used, b)
                    n, d = 2 * (b % 2) + 4, 2 * (b % 2) + 5
                    dn = den[:, :, :].rearrange("p c n -> p (c n)")
                    link(v.tensor_scalar(dn, banks[d][:, :], 1e-6, None, ALU.add))
                    link(v.reciprocal(dn, dn))
                    v.tensor_tensor(al[:, :, b, 1:1 + L2], banks[n][:, :].rearrange("p (c n) -> p c n", c=KC),
                                    den[:, :, :], ALU.mult).then_inc(nd_used, 1)
                dve.wait_ge(nd_used, B)
                doubled(even, odd, al, 0, L2, False)
                dve.wait_ge(high_copied, B * KC)
                doubled(part(se, 0, L1), part(so, 1, L1), low1, 0, L1, True)
                v.drain().then_inc(syn_ready, 1)
                for i in range(NT):
                    dve.wait_ge(tile_made, i + 1)
                    v.tensor_tensor(c.y[:, i, :], banks[i % 4][:, 0:D], c.x2[:, i, :], ALU.add).then_inc(tile_used, 1)
                    dve.wait_ge(tile_used, i + 1)
                    row_stats(nc, c, i)

            @block.scalar
            def _(act):
                for b in range(B):
                    for k in range(KC):
                        n = b * KC + k
                        act.wait_ge(high_made, n + 1)
                        nc.scalar.activation(high1[:, k, b, 1:1 + L1], banks[n % 2][:, :], ACT.Copy)\
                            .then_inc(high_copied, 1)
                act.wait_ge(min_ready, 1)
                qf = q[:, :, :, :].rearrange("p c b n -> p (c b n)")
                nc.scalar.activation(qf, qf, ACT.Exp).then_inc(exp_ready, 1)
                for b in range(B):
                    act.wait_ge(turned, 2 * b + 2)
                    nc.scalar.activation(htt[:, b, :, :, :].rearrange("p c j n -> p (c j n)"),
                                         banks[2 * b + 1][:, :], ACT.Copy).then_inc(ht_copied, 1)

            @block.tensor
            def _(pe):
                pe.wait_ge(diag_ready, 1)
                for b in range(B):
                    for k in range(KC):
                        n = b * KC + k
                        wait_from(pe, high_copied, n - 1)
                        for j, (src, at) in enumerate(((c.xo, 0), (c.xe, 0), (c.xo, 1), (c.xe, 1))):
                            mm = nc.tensor.matmul(banks[n % 2][:, :], diag[:, k, j, :], src[:, k, b, at:at + L1],
                                                  start=(j == 0), stop=(j == 3))
                        mm.then_inc(high_made, 1)
                pe.wait_ge(high_copied, B * KC)
                pe.wait_ge(q_ready, 1)
                for b in range(B):
                    for m, src in enumerate((q, low2)):
                        for k in range(KC):
                            for j in range(2):
                                at = (k * 2 + j) * P
                                mm = nc.tensor.transpose(banks[2 * b + m][:, at:at + P], src[:, k, b, j * P:(j + 1) * P],
                                                         c.ident[:, :])
                        mm.then_inc(turned, 1)
                pe.wait_ge(qt_copied, B)
                pe.wait_ge(ht_copied, B)
                for b in range(B):
                    for k in range(KC):
                        for j in range(2):
                            mm = nc.tensor.matmul(banks[b][:, k * P:(k + 1) * P], qt[:, b, k, j, :], htt[:, b, k, j, :],
                                                  start=(j == 0), stop=(j == 1))
                    mm.then_inc(kv_made, 1)
                for b in range(B):
                    pe.wait_ge(kv_ready, b + 1)
                    wait_from(pe, nd_used, b - 1)
                    for m, w in enumerate((kvm, zm)):
                        for k in range(KC):
                            mm = nc.tensor.matmul(banks[2 * (b % 2) + 4 + m][:, k * L2:(k + 1) * L2], w[:, b, k, :],
                                                  q[:, k, b, :], start=True, stop=True)
                    mm.then_inc(nd_made, 1)
                pe.wait_ge(diag_ready, 2)
                pe.wait_ge(syn_ready, 1)
                pe.wait_ge(nd_used, B)
                for i in range(NT):
                    b, t = i // TB, i % TB
                    at = (t // 2) * P
                    wait_from(pe, tile_used, i - 3)
                    for k in range(KC):
                        low, high = ((se[:, k, b, at:at + P], ((0, 0), (1, 1), (2, 2))) if t % 2 == 0 else
                                     (so[:, k, b, at + 1:at + 1 + P], ((1, 3), (2, 4))))
                        dst = banks[i % 4][:, k * P:(k + 1) * P]
                        mm = nc.tensor.matmul(dst, low, c.ident[:, :], start=True, stop=False)
                        for off, n in high:
                            mm = nc.tensor.matmul(dst, high1[:, k, b, at + off:at + off + P], diag[:, k, 4 + n, :],
                                                  start=False, stop=(n == high[-1][1]))
                    mm.then_inc(tile_made, 1)
        mem.clear()


def stage_affine(nc, outer, a, c):
    HB = TB // 2
    with ExitStack() as stack:
        mem = Mem(nc, stack)
        gamma = mem.sb("n_gamma", [P, D])
        beta = mem.sb("n_beta", [P, D])
        loaded, moved, scaled = mem.sem("n_loaded"), mem.sem("n_moved"), mem.sem("n_scaled")
        summed, spare = mem.sem("n_summed"), mem.sem("n_spare")
        loaded_b = mem.sem("n_loaded_beta")
        with nc.Block() as block:
            @block.sync
            def _(sp):
                sp.dma_start(beta[:, :], a.beta.partition_broadcast(P)).then_inc(loaded_b, 16)
                sp.dma_start(gamma[:, :], a.gamma.partition_broadcast(P)).then_inc(loaded, 16)

            @block.gpsimd
            def _(pool):
                pool.wait_ge(loaded_b, 16)
                with pool.Fori(0, B * 2) as h:
                    part = c.x2[:, bass.ds(h * HB, HB), :]
                    nc.gpsimd.tensor_tensor(part, part, bcast(beta[:, :].unsqueeze(1), [P, HB, D]), ALU.add)\
                        .then_inc(moved, 1)

            @block.vector
            def _(dve):
                def flat(x, i):
                    return x[:, bass.ds(i, 1), :].rearrange("p a d -> p (a d)")

                def scale(i):
                    nc.vector.scalar_tensor_tensor(out=flat(c.y, i), in0=flat(c.y, i), scalar=c.mean[:, bass.ds(i, 1)],
                                                   in1=gamma[:, :], op0=ALU.subtract, op1=ALU.mult).then_inc(scaled, 1)

                def add(i):
                    dve.wait_ge(scaled, i + 1)
                    nc.vector.scalar_tensor_tensor(out=flat(c.y, i), in0=flat(c.y, i), scalar=c.rstd[:, bass.ds(i, 1)],
                                                   in1=flat(c.x2, i), op0=ALU.mult, op1=ALU.add).then_inc(summed, 1)

                def stats(i):
                    wait_apart(dve, spare, summed, i + 1)
                    row_stats(nc, c, i)

                dve.wait_ge(loaded, 16)
                with dve.Fori(0, B * 2) as g:
                    for t in range(HB + 2):
                        if t < HB:
                            scale(g * HB + t)
                        if t == 1:
                            dve.wait_ge(moved, g + 1)
                        if 1 <= t <= HB:
                            add(g * HB + t - 1)
                        if t >= 2:
                            stats(g * HB + t - 2)
        mem.clear()


def stage_store(nc, outer, c, out):
    with ExitStack() as stack:
        mem = Mem(nc, stack)
        st = [mem.sb(f"s_batch{u}", [P, TB, D]) for u in range(2)]
        ready = mem.sem("s_ready")
        stored = [mem.sem(f"s_stored{u}") for u in range(2)]
        rows = out.rearrange("(i p) d -> p i d", p=P)
        with nc.Block() as block:
            @block.vector
            def _(dve):
                for b in range(B):
                    wait_from(dve, stored[b % 2], 16 * (b // 2))
                    for t in range(TB):
                        last = normalised(nc, c, st[b % 2][:, t, :], b * TB + t)
                    last.then_inc(ready, 1)

            @block.sync
            def _(sp):
                for b in range(B):
                    sp.wait_ge(ready, b + 1)
                    sp.dma_start(rows[:, b * TB:(b + 1) * TB, :], st[b % 2][:, :, :]).then_inc(stored[b % 2], 16)
                for u in range(2):
                    sp.wait_ge(stored[u], 32)


class Names:
    pass


def build(nc, a, out):
    Mem.uses = {}
    c = Names()

    def dram(name, shape, dt=FP32):
        return nc.dram_tensor(name, shape, dt).ap()
    c.q_parts, c.k_parts = dram("q_parts", [NH, HD, PARTS, S], BF16), dram("k_parts", [NH, HD, PARTS, S], BF16)
    rows = [dram(f"rows{n}", [N, D]) for n in range(2)]
    sums = [dram(f"sums{n}", [N, D]) for n in range(2)]
    F0 = 4 * D
    most = N * 2 // P + E - 1
    most += most % 2
    CAP = int(1.25 * N / E) // P
    with ExitStack() as stack:
        mem = Mem(nc, stack)
        stage_constants(nc, mem, c)
        c.six = mem.sb("six", [P, NT, 6])
        c.rstd = mem.sb("rstd", [P, NT])
        c.mean = mem.sb("mean", [P, NT])
        c.nmr = mem.sb("nmr", [P, NT])
        c.logits = mem.sb("logits", [P, NT * E])
        c.gather = mem.sb("gather", [P, most], I32)
        c.scatter = mem.sb("scatter", [P, most], I32)
        c.gains = mem.sb("gains", [P, most])
        c.owner = mem.sb("owner", [P, most], I32)
        with ExitStack() as inner:
            m = Mem(nc, inner)
            w1 = m.sb("w1", [P, E * KC, F0])
            w2 = m.sb("w2", [P, E * (F0 // P), D])
            late = m.sb("biases", [P, E * (F0 + D)])
            w1_loaded, w2_loaded, b_loaded = m.sem("w1_loaded"), m.sem("w2_loaded"), m.sem("b_loaded")
            flat = w2[:, :, :].rearrange("p f d -> p (f d)")
            half = E * (F0 // P) * D // 2
            c.v = flat[:, 0:half].rearrange("p (n t r) -> p n t r", n=NH, t=TB)
            c.probs = flat[:, half:2 * half].rearrange("p (t s) -> p t s", t=TB)
            c.y = flat[:, half:2 * half].rearrange("p (i d) -> p i d", d=D)
            c.ao = late[:, 0:NH * TB * HD].rearrange("p (n t r) -> p n t r", n=NH, t=TB)
            stage_project(nc, m, a, c)
            with nc.Block() as block:
                @block.scalar
                def _(act):
                    for e in range(E):
                        act.dma_start(w1[:, e * KC:(e + 1) * KC, :], a.w1_0[e].rearrange("(c p) f -> p c f", p=P))\
                            .then_inc(w1_loaded, 16)
            stage_attention(nc, m, a, c)
            FC = F0 // P

            def load_w2(act, experts):
                for e in experts:
                    act.dma_start(w2[:, e * FC:(e + 1) * FC, :], a.w2_0[e].rearrange("(f p) d -> p f d", p=P))\
                        .then_inc(w2_loaded, 16)
            with nc.Block() as block:
                @block.scalar
                def _(act):
                    load_w2(act, range(E // 2))
            stage_output(nc, m, a, c)
            stage_rstd(nc, m, c)
            b1 = late[:, 0:E * F0].rearrange("p (e f) -> p e f", e=E)
            b2 = late[:, E * F0:E * (F0 + D)].rearrange("p (e d) -> p e d", e=E)
            stage_gate(nc, m, c, a.gate_0, rows[0])
            with nc.Block() as block:
                @block.scalar
                def _(act):
                    act.dma_start(b1, a.b1_0.partition_broadcast(P)).then_inc(b_loaded, 16)
                    act.dma_start(b2, a.b2_0.partition_broadcast(P)).then_inc(b_loaded, 16)
                    load_w2(act, range(E // 2, E))
            stage_route(nc, m, c, most, None, rows[0], sums[0])
            with nc.Block() as block:
                @block.tensor
                def _(pe):
                    pe.wait_ge(w1_loaded, 16 * E)
                    pe.wait_ge(w2_loaded, 16 * E)

                @block.vector
                def _(dve):
                    dve.wait_ge(b_loaded, 32)
            stage_experts(nc, m, c, most, None, F0, w1, w2, b1, b2, ACT.Gelu, rows[0], sums[0])
        with ExitStack() as inner:
            m = Mem(nc, inner)
            c.y = m.sb("y", [P, NT, D])
            c.x2 = m.sb("x2", [P, NT, D])
            with ExitStack() as inner2:
                m2 = Mem(nc, inner2)
                c.xe = m2.sb("x_even", [P, KC, B, L1 + 2])
                c.xo = m2.sb("x_odd", [P, KC, B, L1 + 2])
                stage_load_stats(nc, m, c, sums[0])
                stage_rstd(nc, m, c)
                stage_to_channels(nc, m, a, c)
                stage_wavelet(nc, m, a, c)
            stage_rstd(nc, m, c)
            w1 = m.sb("w1_1", [P, E * KC, D])
            w2 = m.sb("w2_1", [P, E * KC, D])
            b1 = m.sb("b1_1", [P, E, D])
            b2 = m.sb("b2_1", [P, E, D])
            loaded = m.sem("loaded_1")
            stage_affine(nc, m, a, c)
            stage_rstd(nc, m, c)
            stage_gate(nc, m, c, a.gate_1, rows[1])
            with nc.Block() as block:
                @block.scalar
                def _(act):
                    act.dma_start(w1[:, :, :], a.w1_1.rearrange("e (c p) f -> p (e c) f", p=P)).then_inc(loaded, 16)
                    act.dma_start(w2[:, :, :], a.w2_1.rearrange("e (c p) f -> p (e c) f", p=P)).then_inc(loaded, 16)
                    act.dma_start(b1[:, :, :], a.b1_1.partition_broadcast(P)).then_inc(loaded, 16)
                    act.dma_start(b2[:, :, :], a.b2_1.partition_broadcast(P)).then_inc(loaded, 16)
            stage_route(nc, m, c, CAP * E, CAP, rows[1], sums[1])
            with nc.Block() as block:
                @block.tensor
                def _(pe):
                    pe.wait_ge(loaded, 64)

                @block.vector
                def _(dve):
                    dve.wait_ge(loaded, 64)
            stage_experts(nc, m, c, CAP * E, CAP, D, w1, w2, b1, b2, ACT.Silu, rows[1], sums[1])
            stage_load_stats(nc, m, c, sums[1])
            stage_rstd(nc, m, c)
            stage_store(nc, m, c, out)


def kernel(**inputs):
    import numpy as np
    import concourse.bacc as bacc
    from concourse.bass_utils import run_bass_kernel_spmd

    g = {k: np.asarray(v) for k, v in inputs.items()}
    J = S // (2 * P)
    x = g["L0_attn_x"].reshape(B, J, P, 2, D).transpose(0, 1, 3, 2, 4).reshape(N, D)
    taps = np.stack([g["L1_attn_" + n] for n in ("h_filter", "g_filter", "h_synth", "g_synth")])
    arrays = {
        "x": x, "xt": x.T,
        "wqkv": np.concatenate([g["L0_attn_W" + n].T for n in "qkv"], axis=1),
        "bqk": np.stack([g["L0_attn_b" + n].reshape(KC, P) for n in "qk"]).transpose(2, 0, 1),
        "bv": g["L0_attn_bv"], "wo": g["L0_attn_Wo"].T, "bo": g["L0_attn_bo"],
        "gate_0": g["L0_ffn_w_gate"].T, "w1_0": g["L0_ffn_W1"], "b1_0": g["L0_ffn_b1"],
        "w2_0": g["L0_ffn_W2"], "b2_0": g["L0_ffn_b2"],
        "filters": taps.reshape(4, 4, KC, P).transpose(3, 2, 0, 1),
        "gamma": g["L1_attn_norm_gamma"], "beta": g["L1_attn_norm_beta"],
        "gate_1": g["L1_ffn_gate_w"].T, "w1_1": g["L1_ffn_w1"].transpose(0, 2, 1), "b1_1": g["L1_ffn_b1"],
        "w2_1": g["L1_ffn_w2"].transpose(0, 2, 1), "b2_1": g["L1_ffn_b2"],
    }
    nc = bacc.Bacc("TRN2", target_bir_lowering=False, num_devices=1)
    a = Names()
    feed = {}
    for name, array in arrays.items():
        feed["in_" + name] = np.ascontiguousarray(array)
        handle = nc.dram_tensor("in_" + name, array.shape, mybir.dt.from_np(array.dtype), kind="ExternalInput")
        a.__dict__[name] = handle.ap()
    out = nc.dram_tensor("out_rows", [N, D], FP32, kind="ExternalOutput").ap()
    build(nc, a, out)
    r = run_bass_kernel_spmd(nc, [feed], core_ids=[0])
    rows = r.results[0]["out_rows"]
    return rows.reshape(B, J, 2, P, D).transpose(0, 1, 3, 2, 4).reshape(B, S, D)
```

```python
from contextlib import ExitStack

import concourse.bass as bass
from concourse import mybir

FP32 = mybir.dt.float32
BF16 = mybir.dt.bfloat16
I32 = mybir.dt.int32
ALU = mybir.AluOpType
ACT = mybir.ActivationFunctionType
AX = mybir.AxisListType

P = 128
B, S, D = 4, 1024, 256
N = B * S
H, HD = 16, 16
KC = D // P
NT = N // P
TB = S // P
E = 8
NH = B * H
L1, L2 = S // 2, S // 4
HALF = 512
SCALE = float(HD) ** -0.5
PARTS = 3
STACK = 6 * HD
RING = 3
MAXROWS = 2
SLOTS = 4


class Mem:

    uses = {}

    def __init__(self, nc, stack):
        self.nc, self.stack, self.sems = nc, stack, []

    def clear(self):
        for sem in self.sems:
            self.nc.gpsimd.sem_clear(sem)

    @staticmethod
    def label(name):
        n = Mem.uses[name] = Mem.uses.get(name, -1) + 1
        return f"{name}_{n}" if n else name

    def sb(self, name, shape, dt=FP32):
        return self.stack.enter_context(self.nc.sbuf_tensor(self.label(name), shape, dt))

    def ps(self, name, shape=(P, HALF), dt=FP32):
        return self.stack.enter_context(self.nc.psum_tensor(self.label(name), list(shape), dt))

    def sem(self, name):
        self.sems.append(self.stack.enter_context(self.nc.semaphore(self.label(name))))
        return self.sems[-1]


def wait_from(eng, sem, value):
    if not isinstance(value, int) or value > 0:
        eng.wait_ge(sem, value)


def wait_apart(eng, spare, sem, value):
    if not isinstance(value, int) or value > 0:
        eng.wait_ge(sem, value)
        eng.sem_inc(spare, 1)


def row_stats(nc, c, i):
    nc.vector.bn_stats(c.six[:, bass.ds(i, 1), :].rearrange("p a d -> p (a d)"),
                       c.y[:, bass.ds(i, 1), :].rearrange("p a d -> p (a d)"))


def peeled(eng, count, body):
    body(0)
    with eng.Fori(1, count) as i:
        body(i)


def peeled_ends(eng, count, body):
    body(0, True, False)
    with eng.Fori(1, count - 1) as i:
        body(i, False, False)
    body(count - 1, False, True)


def stage_constants(nc, mem, c):
    c.ident = mem.sb("ident", [P, P])
    c.identb = mem.sb("identb", [P, P], BF16)
    c.fold = mem.sb("fold", [P, 2 * 32])
    zeroed, made = mem.sem("consts_zeroed"), mem.sem("consts_made")
    with nc.Block() as block:
        @block.gpsimd
        def _(pool):
            nc.gpsimd.memset(c.ident[:, :], 0.0).then_inc(zeroed, 1)
            nc.gpsimd.memset(c.identb[:, :], 0.0).then_inc(zeroed, 1)
            nc.gpsimd.memset(c.fold[:, :], 0.0).then_inc(zeroed, 1)
            pool.wait_ge(zeroed, 3)
            for m in (c.ident, c.identb):
                nc.gpsimd.affine_select(out=m[:, :], in_=m[:, :], compare_op=ALU.not_equal, fill=1.0, base=0,
                                        pattern=[[-1, P]], channel_multiplier=1).then_inc(made, 1)
            fold = c.fold[:, :].rearrange("p (q r) -> p q r", q=2)
            for kh in range(2):
                pool.wait_ge(made, 2 + kh)
                nc.gpsimd.affine_select(out=fold, in_=fold, compare_op=ALU.not_equal, fill=1.0, base=-32 * kh,
                                        pattern=[[-64, 2], [-1, 32]], channel_multiplier=1).then_inc(made, 1)


def stage_project(nc, a, c):
    CH = HALF
    with ExitStack() as stack:
        mem = Mem(nc, stack)
        w = mem.sb("w_qkv", [P, KC, 3 * D])
        bias = mem.sb("b_qk", [P, 2, KC])
        bv = mem.sb("bv_all", [P, D])
        xt = [mem.sb(f"xt{u}", [P, KC, CH]) for u in range(2)]
        full = [mem.sb(f"qk_full{u}", [P, CH]) for u in range(2)]
        part = [mem.sb(f"qk_part{u}", [P, PARTS, CH], BF16) for u in range(4)]
        rest = [mem.sb(f"qk_rest{u}", [P, CH]) for u in range(2)]
        pq = [mem.ps(f"ps_qk{u}") for u in range(4)]
        pv = [mem.ps(f"ps_v{u}") for u in range(4)]
        loaded_w = mem.sem("a_weights")
        loaded_x = [mem.sem(f"a_x{u}") for u in range(2)]
        qk_ready, v_ready = mem.sem("a_qk_ready"), mem.sem("a_v_ready")
        full_ready, part1_ready = mem.sem("a_full"), mem.sem("a_part1")
        rest_ready, part2_ready, part3_ready = mem.sem("a_rest"), mem.sem("a_part2"), mem.sem("a_part3")
        v_done = mem.sem("a_v_done")
        spare_p = mem.sem("a_spare")
        stored = [mem.sem(f"a_stored{u}") for u in range(4)]
        with nc.Block() as block:
            @block.sync
            def _(sp):
                sp.dma_start(w[:, :, :], a.wqkv.rearrange("(c p) n -> p c n", p=P)).then_inc(loaded_w, 16)
                sp.dma_start(bias[:, :, :], a.bqk).then_inc(loaded_w, 16)
                sp.dma_start(bv[:, :], a.bv.partition_broadcast(P)).then_inc(loaded_w, 16)

                def store(b):
                    for u in range(2):
                        for m in range(4):
                            sp.wait_ge(part3_ready, b * 8 + 4 * u + m + 1)
                            dst = (c.q_parts, c.k_parts)[m // 2]
                            sp.dma_start(
                                dst[bass.ds(b * H + (m % 2) * 8, 8), :, :, u * CH:(u + 1) * CH]
                                .rearrange("h r s t -> (h r) s t"), part[m][:, :, :]).then_inc(stored[m], 16)
                peeled(sp, B, store)
                for m in range(4):
                    sp.wait_ge(stored[m], 16 * 2 * B)

            @block.tensor
            def _(pe):
                pe.wait_ge(loaded_w, 48)

                def products(b):
                    for u in range(2):
                        pe.wait_ge(loaded_x[u], b * 16 + 16)
                        for m in range(4):
                            wait_from(pe, part1_ready, b * 8 + 4 * u + m - 3)
                            for k in range(KC):
                                mm = nc.tensor.matmul(pq[m][:, :], w[:, k, m * P:(m + 1) * P], xt[u][:, k, :],
                                                      start=(k == 0), stop=(k == KC - 1))
                            mm.then_inc(qk_ready, 1)
                        for t in range(4):
                            wait_from(pe, v_done, b * 8 + 4 * u + t - 3)
                            for k in range(KC):
                                mm = nc.tensor.matmul(pv[t][:, 0:D], xt[u][:, k, t * P:(t + 1) * P],
                                                      w[:, k, 2 * D:3 * D], start=(k == 0), stop=(k == KC - 1))
                            mm.then_inc(v_ready, 1)
                peeled(pe, B, products)

            @block.scalar
            def _(act):
                def evacuate(b):
                    for u in range(2):
                        wait_from(act, v_ready, b * 8 + 4 * u - 4)
                        act.dma_start(xt[u][:, :, :], a.xt[:, bass.ds(b * S + u * CH, CH)]
                                      .rearrange("(c p) n -> p c n", p=P)).then_inc(loaded_x[u], 16)
                        if isinstance(b, int) and u == 0:
                            act.wait_ge(loaded_w, 48)
                        for m in range(4):
                            i = b * 8 + 4 * u + m
                            act.wait_ge(qk_ready, i + 1)
                            wait_from(act, rest_ready, i - 1)
                            nc.scalar.activation(full[m % 2][:, :], pq[m][:, :], ACT.Identity,
                                                 bias=bias[:, m // 2, m % 2:m % 2 + 1]).then_inc(full_ready, 1)
                            wait_from(act, stored[m], b * 32 + 16 * u)
                            nc.scalar.activation(part[m][:, 0, :], pq[m][:, :], ACT.Identity,
                                                 bias=bias[:, m // 2, m % 2:m % 2 + 1]).then_inc(part1_ready, 1)
                peeled(act, B, evacuate)

            @block.gpsimd
            def _(pool):
                def second(b):
                    for u in range(2):
                        for m in range(4):
                            wait_apart(pool, spare_p, rest_ready, b * 8 + 4 * u + m + 1)
                            nc.gpsimd.tensor_copy(part[m][:, 1, :], rest[m % 2][:, :]).then_inc(part2_ready, 1)
                peeled(pool, B, second)

            @block.vector
            def _(dve):
                def left_over(i, m):
                    dve.wait_ge(part1_ready, i + 1)
                    wait_from(dve, part3_ready, i - 1)
                    nc.vector.tensor_tensor(rest[m % 2][:, :], full[m % 2][:, :], part[m][:, 0, :],
                                            ALU.subtract).then_inc(rest_ready, 1)

                def third(i, m):
                    dve.wait_ge(part2_ready, i + 1)
                    nc.vector.tensor_tensor(part[m][:, 2, :], rest[m % 2][:, :], part[m][:, 1, :],
                                            ALU.subtract).then_inc(part3_ready, 1)

                def split(b):
                    for u in range(2):
                        at = b * 8 + 4 * u
                        left_over(at, 0)
                        for m in range(4):
                            if m < 3:
                                left_over(at + m + 1, m + 1)
                            third(at + m, m)
                        for t in range(4):
                            dve.wait_ge(v_ready, b * 8 + 4 * u + t + 1)
                            nc.vector.tensor_tensor(
                                c.v[:, bass.ds(b * H, H), u * 4 + t, :],
                                pv[t][:, 0:D].rearrange("p (h r) -> p h r", h=H),
                                bv[:, :].rearrange("p (h r) -> p h r", h=H), ALU.add).then_inc(v_done, 1)
                dve.wait_ge(loaded_w, 48)
                peeled(dve, B, split)
        mem.clear()


def stage_attention(nc, a, c, w1, w1_loaded):
    KT = TB
    with ExitStack() as stack:
        mem = Mem(nc, stack)
        qs = mem.sb("q_stack", [STACK + MAXROWS, SLOTS, S], BF16)
        ks = mem.sb("k_stack", [STACK + MAXROWS, SLOTS, S], BF16)
        pt = c.probs
        vpad = [mem.sb(f"v_padded{u}", [P, KT, 32]) for u in range(2)]
        o_sb = mem.sb("o_transposed", [P, HALF])
        unit_max = mem.sb("unit_max", [P, 2, 2, KT])
        best = [mem.sb(f"row_max{u}", [P, KT]) for u in range(2)]
        neg = mem.sb("neg_max", [P, KT])
        negp = [mem.sb(f"neg_parts{u}", [P, MAXROWS, KT], BF16) for u in range(2)]
        negt = [mem.sb(f"neg_rows{u}", [MAXROWS * KT, P], BF16) for u in range(2)]
        rec = mem.sb("o_reciprocal", [P, 2, 4])
        p_s = [mem.ps(f"ps_scores{u}", (P, S)) for u in range(2)]
        ring = [mem.ps(f"ps_ring{u}") for u in range(RING)]
        p_o = mem.ps("ps_o")
        slot_loaded = [mem.sem(f"b_slot{u}") for u in range(SLOTS)]
        LOADS, ROWS = 6 * 16, 7 * 16
        spare_p = mem.sem("b_spare")
        init = mem.sem("b_init")
        scores_ready, exp_done = mem.sem("b_scores"), mem.sem("b_exp")
        ring_ready, ring_used = mem.sem("b_ring_ready"), mem.sem("b_ring_used")
        best_done = mem.sem("b_best_done")
        neg_order, parts_done = mem.sem("b_neg_order"), mem.sem("b_parts")
        v_copied, pv_done, o_copied = mem.sem("b_v"), mem.sem("b_pv"), mem.sem("b_o")
        rec_done = mem.sem("b_rec")
        GROUPS = NH // SLOTS
        w1_chunks = a.w1_0.rearrange("e (c p) f -> (e c) p f", p=P)
        FOLD_AT, ROWS_AT = 4, 2

        def units(first, last, u):
            for kt in range(KT):
                if not (last and u >= 2):
                    yield kt, "max0"
                if kt == ROWS_AT and not (last and u == SLOTS - 1):
                    yield kt, "rows"
                if not (last and u >= 2):
                    yield kt, "max1"
                if kt == FOLD_AT and not (first and u == 0):
                    yield kt, "fold"

        FIRST_ROWS = 2 * KT + 4
        PROLOGUE = 2 * 2 * KT + 1

        def first_units():
            for at in range(PROLOGUE):
                n = at - (at > FIRST_ROWS)
                yield (at, None, 0, 0) if at == FIRST_ROWS else (at, n // (2 * KT), n % (2 * KT) // 2, n % 2)
        PER_GROUP = SLOTS * (2 * KT + 2)
        assert PER_GROUP % RING == 0 and GROUPS == w1.shape[1]

        def count_before(g, first, last, u):
            inside = sum(len(list(units(first, last, w))) for w in range(u))
            if first:
                return PROLOGUE + inside
            return g * PER_GROUP + (PROLOGUE - 1 + inside)

        def bank(g, first, last, u, j):
            base = PROLOGUE if first else PROLOGUE - 1
            return ring[(base + sum(len(list(units(first, last, w))) for w in range(u)) + j) % RING]


        def groups(eng, body):
            peeled_ends(eng, GROUPS, body)

        with nc.Block() as block:
            @block.sync
            def _(sp):
                def load(g, u):
                    for dst, src, deep in ((qs, c.q_parts, True), (ks, c.k_parts, False)):
                        at = 0
                        for n in (3, 2, 1):
                            if deep:
                                rows = src[bass.ds(g * SLOTS + u, 1), :, 0:n, :]
                                rows = rows.rearrange("h r s t -> (h r) s t")
                            else:
                                rows = src[bass.ds(g * SLOTS + u, 1), :, 3 - n:4 - n, :]
                                rows = rows.rearrange("h r s t -> (h r) s t").to_broadcast([HD, n, S])
                            sp.dma_start(dst[at:at + n * HD, u, :], rows).then_inc(slot_loaded[u], 16)
                            at += n * HD
                for u in range(3):
                    load(0, u)

                def rows(u, at):
                    sp.wait_ge(ring_used, at + 1)
                    sp.dma_start(qs[STACK:STACK + MAXROWS, u, :].rearrange("s (t q) -> s t q", t=KT),
                                 negt[u % 2][:, :]).then_inc(slot_loaded[u], 16)

                def body(g, first, last):
                    for u in range(SLOTS):
                        if first and u == 0:
                            rows(0, FIRST_ROWS)
                        if not (last and u > 0):
                            wait_from(sp, scores_ready, (g * SLOTS + u) * KT)
                            load(g + (1 if u > 0 else 0), (u + 3) % SLOTS)
                        for j, (_, kind) in enumerate(units(first, last, u)):
                            if kind == "rows":
                                rows((u + 1) % SLOTS, count_before(g, first, last, u) + j)
                    sp.dma_start(w1[:, bass.ds(g, 1), :], w1_chunks[bass.ds(g, 1), :, :]
                                 .rearrange("n p f -> p n f")).then_inc(w1_loaded, 16)
                groups(sp, body)

            @block.gpsimd
            def _(pool):
                nc.gpsimd.memset(ks[STACK:STACK + MAXROWS, :, :], 1.0).then_inc(init, 1)
                for j, v in enumerate(vpad):
                    pool.wait_ge(init, 2 * j + 1)
                    nc.gpsimd.memset(v[:, :, HD:HD + 1], 1.0).then_inc(init, 1)
                    pool.wait_ge(init, 2 * j + 2)
                    nc.gpsimd.memset(v[:, :, HD + 1:32], 0.0).then_inc(init, 1)
                pool.wait_ge(init, 5)

                def negate(n, u):
                    wait_apart(pool, spare_p, parts_done, n)
                    wait_apart(pool, spare_p, best_done, n + 1)
                    nc.gpsimd.tensor_scalar(neg[:, :], best[u % 2][:, :], -1.0, None, ALU.mult).then_inc(neg_order, 1)
                    wait_apart(pool, spare_p, neg_order, n * 2 + 1)
                    nc.gpsimd.tensor_copy(negp[u % 2][:, 0, :], neg[:, :]).then_inc(neg_order, 1)
                    wait_apart(pool, spare_p, neg_order, n * 2 + 2)
                    nc.gpsimd.tensor_tensor(negp[u % 2][:, 1, :], neg[:, :], negp[u % 2][:, 0, :],
                                            ALU.subtract).then_inc(parts_done, 1)

                for u in range(2):
                    negate(u, u)

                def body(g, first, last):
                    for u in range(SLOTS):
                        n = g * SLOTS + u
                        wait_apart(pool, spare_p, pv_done, (n - 1) * 4)
                        nc.gpsimd.tensor_copy(vpad[u % 2][:, :, 0:HD], c.v[:, bass.ds(n, 1), :, :]
                                              .rearrange("p h t r -> p (h t) r")).then_inc(v_copied, 1)
                        if not (last and u >= 2):
                            negate(n + 2, u)
                groups(pool, body)

            @block.tensor
            def _(pe):
                def claim(at):
                    wait_from(pe, ring_used, at - RING + 1)

                def max_unit(u, qt, half, at, out):
                    claim(at)
                    nc.tensor.matmul(out[:, :], qs[0:STACK, u, qt * P:(qt + 1) * P],
                                     ks[0:STACK, u, half * HALF:(half + 1) * HALF],
                                     start=True, stop=True).then_inc(ring_ready, 1)

                def rows_unit(n, u, at, out):
                    pe.wait_ge(parts_done, n + 1)
                    claim(at)
                    nc.tensor.transpose(out[0:MAXROWS * KT, 0:P // 2].bitcast(BF16),
                                        negp[u % 2][:, :, :].rearrange("p s t -> p (s t)"),
                                        c.identb[:, :]).then_inc(ring_ready, 1)

                def pv(n, u, i):
                    pe.wait_ge(exp_done, n * KT + 2 * i + 2)
                    if i == 0:
                        pe.wait_ge(v_copied, n + 1)
                        wait_from(pe, o_copied, n)
                    for kh in range(2):
                        for qh in range(2):
                            j = 2 * qh + kh
                            mm = nc.tensor.matmul(p_o[32 * j:32 * j + 32, :], vpad[u % 2][:, 2 * i + kh, :],
                                                  pt[:, 2 * i + kh, qh * HALF:(qh + 1) * HALF],
                                                  start=(i == 0), stop=(i == KT // 2 - 1))
                    mm.then_inc(pv_done, 1)

                def fold_unit(n, at, out):
                    pe.wait_ge(o_copied, n + 1)
                    claim(at)
                    for blk in range(4):
                        mm = nc.tensor.matmul(out[:, blk * 64:(blk + 1) * 64], o_sb[:, blk * P:(blk + 1) * P],
                                              c.fold[:, :], start=True, stop=True)
                    mm.then_inc(ring_ready, 1)

                pe.wait_ge(init, 5)
                for at, u, qt, half in first_units():
                    if u is None:
                        rows_unit(0, 0, at, ring[at % RING])
                        continue
                    if qt == 0 and half == 0:
                        pe.wait_ge(slot_loaded[u], LOADS)
                    max_unit(u, qt, half, at, ring[at % RING])

                def body(g, first, last):
                    for u in range(SLOTS):
                        n = g * SLOTS + u
                        ahead = not (last and u >= 2)
                        before = count_before(g, first, last, u)
                        todo = list(enumerate(units(first, last, u)))

                        def emit(kt, kinds):
                            for j, (step, kind) in todo:
                                if step != kt or kind not in kinds:
                                    continue
                                at, out = before + j, bank(g, first, last, u, j)
                                if kind == "rows":
                                    rows_unit(n + 1, u + 1, at, out)
                                elif kind == "fold":
                                    fold_unit(n - 1, at, out)
                                else:
                                    max_unit((u + 2) % SLOTS, kt, int(kind[3]), at, out)
                        for kt in range(KT):
                            if kt == 0:
                                pe.wait_ge(slot_loaded[u], g * ROWS + ROWS)
                                if ahead:
                                    pe.wait_ge(slot_loaded[(u + 2) % SLOTS], (g + (u >= 2)) * ROWS + LOADS)
                            emit(kt, ("max0",))
                            wait_from(pe, exp_done, n * KT + kt - 1)
                            for half in range(2):
                                mm = nc.tensor.matmul(p_s[kt % 2][:, half * HALF:(half + 1) * HALF],
                                                      ks[:, u, kt * P:(kt + 1) * P],
                                                      qs[:, u, half * HALF:(half + 1) * HALF],
                                                      start=True, stop=True)
                            mm.then_inc(scores_ready, 1)
                            emit(kt, ("rows", "max1"))
                            if kt == 1 and not (first and u == 0):
                                pv(n - 1, u + 1, KT // 2 - 1)
                            if kt in (3, 5, 7):
                                pv(n, u, (kt - 3) // 2)
                            emit(kt, ("fold",))
                groups(pe, body)
                pv(NH - 1, SLOTS - 1, KT // 2 - 1)
                end = count_before(GROUPS - 1, False, True, SLOTS)
                fold_unit(NH - 1, end, bank(GROUPS - 1, False, True, SLOTS, 0))

            @block.scalar
            def _(act):
                def copy_o(n, units_before):
                    act.wait_ge(pv_done, (n + 1) * (KT // 2))
                    act.wait_ge(ring_ready, units_before)
                    nc.scalar.activation(o_sb[:, :], p_o[:, :], ACT.Copy).then_inc(o_copied, 1)

                def body(g, first, last):
                    for u in range(SLOTS):
                        n = g * SLOTS + u
                        for kt in range(KT):
                            act.wait_ge(scores_ready, n * KT + kt + 1)
                            if kt % 2 == 0:
                                wait_from(act, pv_done, (n - 1) * (KT // 2) + kt // 2 + 1)
                            nc.scalar.activation(pt[:, kt, :], p_s[kt % 2][:, :], ACT.Exp, scale=SCALE)\
                                .then_inc(exp_done, 1)
                            if kt == 1 and not (first and u == 0):
                                copy_o(n - 1, count_before(g, first, last, u))
                groups(act, body)
                copy_o(NH - 1, count_before(GROUPS - 1, False, True, SLOTS))

            @block.vector
            def _(dve):
                def reduce_unit(n, u, qt, half, at, src):
                    if half == 0 and qt == 0:
                        wait_from(dve, best_done, n - 1)
                    dve.wait_ge(ring_ready, at + 1)
                    nc.vector.tensor_reduce(unit_max[:, u % 2, half, qt:qt + 1], src[:, :], axis=AX.X,
                                            op=ALU.max).then_inc(ring_used, 1)

                def combine(n, u, at):
                    dve.wait_ge(ring_used, at + 1)
                    wait_from(dve, parts_done, n - 1)
                    nc.vector.tensor_tensor(best[u % 2][:, :], unit_max[:, u % 2, 0, :], unit_max[:, u % 2, 1, :],
                                            ALU.max).then_inc(best_done, 1)

                def copy_rows(u, at, src):
                    dve.wait_ge(ring_ready, at + 1)
                    nc.vector.tensor_copy(negt[u % 2][:, :], src[0:MAXROWS * KT, 0:P // 2].bitcast(BF16))\
                        .then_inc(ring_used, 1)

                def normalise(n, at, src):
                    dve.wait_ge(ring_ready, at + 1)
                    wait_from(dve, ring_used, at)
                    o = src[:, 0:256].rearrange("p (b q r) -> p q b r", b=4, q=2)
                    nc.vector.reciprocal(rec[:, :, :], o[:, :, :, HD]).then_inc(rec_done, 1)
                    dve.wait_ge(rec_done, n + 1)
                    nc.vector.tensor_tensor(
                        c.ao[:, bass.ds(n, 1), :, :].rearrange("p h (q b) r -> p (h q) b r", q=2),
                        o[:, :, :, 0:HD], rec[:, :, :].unsqueeze(3).to_broadcast([P, 2, 4, HD]),
                        ALU.mult).then_inc(ring_used, 1)

                for at, u, qt, half in first_units():
                    if u is None:
                        copy_rows(0, at, ring[at % RING])
                        continue
                    reduce_unit(u, u, qt, half, at, ring[at % RING])
                    if qt == KT - 1 and half == 1:
                        combine(u, u, at)

                def body(g, first, last):
                    for u in range(SLOTS):
                        n = g * SLOTS + u
                        before = count_before(g, first, last, u)
                        for j, (kt, kind) in enumerate(units(first, last, u)):
                            at, src = before + j, bank(g, first, last, u, j)
                            if kind == "rows":
                                copy_rows(u + 1, at, src)
                            elif kind == "fold":
                                normalise(n - 1, at, src)
                            else:
                                reduce_unit(n + 2, u, kt, int(kind[3]), at, src)
                                if kt == KT - 1 and kind == "max1":
                                    combine(n + 2, u, at)
                groups(dve, body)
                end = count_before(GROUPS - 1, False, True, SLOTS)
                normalise(NH - 1, end, bank(GROUPS - 1, False, True, SLOTS, 0))
        mem.clear()


class Chain:

    def __init__(self, eng, sem):
        self.eng, self.sem, self.count = eng, sem, 0

    def __call__(self, instruction):
        instruction.then_inc(self.sem, 1)
        self.count += 1
        self.eng.wait_ge(self.sem, self.count)


def bcast(ap, shape):
    return ap.to_broadcast(shape)


def stage_output(nc, a, c, w2, w2_loaded):
    PAIRS, HB = TB // 2, TB // 2
    with ExitStack() as stack:
        mem = Mem(nc, stack)
        wo = mem.sb("w_o", [P, KC, D])
        bo = mem.sb("bo_all", [P, D])
        xin = [mem.sb(f"c_x{u}", [P, HB, D]) for u in range(2)]
        at = [mem.sb(f"c_attn{u}", [P, 2, D]) for u in range(2)]
        ot = [mem.sb(f"c_attn_t{u}", [P, 2, KC, P]) for u in range(2)]
        p_tr = [mem.ps(f"c_ps_t{u}") for u in range(2)]
        p_y = [mem.ps(f"c_ps_y{u}") for u in range(2)]
        loaded_w, loaded_b = mem.sem("c_weights"), mem.sem("c_loaded_bias")
        loaded_x = [mem.sem(f"c_loaded_x{u}") for u in range(2)]
        staged, bias_added = mem.sem("c_staged"), mem.sem("c_bias")
        turned, copied, made = mem.sem("c_turned"), mem.sem("c_copied"), mem.sem("c_made")
        summed, spare, spare_p = mem.sem("c_summed"), mem.sem("c_spare"), mem.sem("c_spare_pool")
        ao = c.ao.rearrange("p (b h) t r -> p b h t r", b=B)
        FC = w2.shape[1] // E
        w2_experts = a.w2_0.rearrange("e (f p) d -> e p f d", p=P)
        tokens = a.x.rearrange("(b h t p) d -> b h p t d", b=B, h=2, p=P)
        with nc.Block() as block:
            @block.sync
            def _(sp):
                sp.dma_start(wo[:, :, :], a.wo.rearrange("(c p) n -> p c n", p=P)).then_inc(loaded_w, 16)
                sp.dma_start(bo[:, :], a.bo.partition_broadcast(P)).then_inc(loaded_b, 16)

                def load(b):
                    for h in range(2):
                        wait_from(sp, summed, b * PAIRS + 2 * h - 2)
                        sp.dma_start(xin[h][:, :, :], tokens[bass.ds(b, 1), h, :, :, :]
                                     .rearrange("b p t d -> (b p) t d")).then_inc(loaded_x[h], 16)
                    sp.dma_start(w2[:, bass.ds(b * FC, FC), :], w2_experts[bass.ds(b, 1), :, :, :]
                                 .rearrange("e p f d -> (e p) f d")).then_inc(w2_loaded, 16)
                peeled(sp, B, load)

            @block.gpsimd
            def _(pool):
                def add_bias(b):
                    for h in range(2):
                        wait_apart(pool, spare_p, loaded_x[h], b * 16 + 16)
                        nc.gpsimd.tensor_tensor(xin[h][:, :, :], xin[h][:, :, :],
                                                bcast(bo[:, :].unsqueeze(1), [P, HB, D]), ALU.add)\
                            .then_inc(bias_added, 1)
                pool.wait_ge(loaded_b, 16)
                peeled(pool, B, add_bias)

            @block.tensor
            def _(pe):
                def turn(i, s):
                    pe.wait_ge(staged, i + 1)
                    wait_from(pe, copied, i - 1)
                    for j in range(2):
                        for k in range(KC):
                            col = (j * KC + k) * P
                            mm = nc.tensor.transpose(p_tr[s % 2][:, col:col + P],
                                                     at[s % 2][:, j, k * P:(k + 1) * P], c.ident[:, :])
                    mm.then_inc(turned, 1)

                def product(i, s):
                    pe.wait_ge(copied, i + 1)
                    wait_from(pe, summed, i - 1)
                    for j in range(2):
                        for k in range(KC):
                            mm = nc.tensor.matmul(p_y[s % 2][:, j * D:(j + 1) * D], ot[s % 2][:, j, k, :],
                                                  wo[:, k, :], start=(k == 0), stop=(k == KC - 1))
                    mm.then_inc(made, 1)

                def pairs(b, first, last):
                    for s in range(PAIRS):
                        if not (last and s == PAIRS - 1):
                            turn(b * PAIRS + s + 1, s + 1)
                        product(b * PAIRS + s, s)
                pe.wait_ge(loaded_w, 16)
                turn(0, 0)
                peeled_ends(pe, B, pairs)

            @block.scalar
            def _(act):
                def stage(b, s):
                    wait_from(act, turned, b * PAIRS + s - 1)
                    nc.scalar.activation(at[s % 2][:, :, :].rearrange("p j (h r) -> p h j r", h=H),
                                         ao[:, bass.ds(b + s // PAIRS, 1), :, s % PAIRS * 2:s % PAIRS * 2 + 2, :]
                                         .rearrange("p b h t r -> p (b h) t r"), ACT.Copy).then_inc(staged, 1)

                def copies(b, first, last):
                    for s in range(PAIRS):
                        if not (last and s == PAIRS - 1):
                            stage(b, s + 1)
                        act.wait_ge(turned, b * PAIRS + s + 1)
                        wait_from(act, made, b * PAIRS + s - 1)
                        nc.scalar.activation(ot[s % 2][:, :, :, :].rearrange("p j c n -> p (j c n)"),
                                             p_tr[s % 2][:, :], ACT.Copy).then_inc(copied, 1)
                stage(0, 0)
                peeled_ends(act, B, copies)

            @block.vector
            def _(dve):
                def add(b):
                    for s in range(PAIRS):
                        i = b * PAIRS + s
                        dve.wait_ge(made, i + 1)
                        if s % 2 == 0:
                            dve.wait_ge(bias_added, b * 2 + s // 2 + 1)
                        nc.vector.tensor_tensor(
                            c.y[:, bass.ds(2 * i, 2), :].rearrange("p a d -> p (a d)"), p_y[s % 2][:, :],
                            xin[s // 2][:, s % 2 * 2:s % 2 * 2 + 2, :].rearrange("p a d -> p (a d)"), ALU.add)\
                            .then_inc(summed, 1)
                        wait_apart(dve, spare, summed, i + 1)
                        for j in range(2):
                            row_stats(nc, c, 2 * i + j)
                peeled(dve, B, add)
        mem.clear()


def stage_load_stats(nc, c, src):
    HB, HALVES = TB // 2, B * 2
    with ExitStack() as stack:
        mem = Mem(nc, stack)
        loaded = [mem.sem(f"l_loaded{h}") for h in range(HALVES)]
        rows = src.rearrange("(i p) d -> p i d", p=P)
        with nc.Block() as block:
            @block.sync
            def _(sp):
                for h in range(HALVES):
                    sp.dma_start(c.y[:, h * HB:(h + 1) * HB, :], rows[:, h * HB:(h + 1) * HB, :])\
                        .then_inc(loaded[h], 16)

            @block.vector
            def _(dve):
                for h in range(HALVES):
                    dve.wait_ge(loaded[h], 16)
                    for i in range(h * HB, (h + 1) * HB):
                        row_stats(nc, c, i)
        mem.clear()


def stage_rstd(nc, c):
    with ExitStack() as stack:
        mem = Mem(nc, stack)
        var = mem.sb("r_var", [P, NT])
        root = mem.sb("r_root", [P, NT])
        tmp = mem.sb("r_tmp", [P, NT])
        var_ready, root_ready, order = mem.sem("r_var_ready"), mem.sem("r_root_ready"), mem.sem("r_order")
        with nc.Block() as block:
            @block.vector
            def _(dve):
                link = Chain(dve, order)
                even, odd = c.six[:, :, 1], c.six[:, :, 4]
                link(nc.vector.tensor_tensor(c.mean[:, :], even, odd, ALU.add))
                link(nc.vector.tensor_scalar(c.mean[:, :], c.mean[:, :], 0.5, None, ALU.mult))
                link(nc.vector.tensor_tensor(tmp[:, :], even, c.mean[:, :], ALU.subtract))
                link(nc.vector.tensor_tensor(tmp[:, :], tmp[:, :], tmp[:, :], ALU.mult))
                link(nc.vector.tensor_tensor(var[:, :], c.six[:, :, 2], c.six[:, :, 5], ALU.add))
                link(nc.vector.scalar_tensor_tensor(out=var[:, :], in0=var[:, :], scalar=1.0 / D, in1=tmp[:, :],
                                                    op0=ALU.mult, op1=ALU.add))
                nc.vector.tensor_scalar(var[:, :], var[:, :], 1e-5, None, ALU.add).then_inc(var_ready, 1)
                dve.wait_ge(root_ready, 1)
                link(nc.vector.reciprocal(c.rstd[:, :], root[:, :]))
                link(nc.vector.tensor_tensor(tmp[:, :], c.rstd[:, :], c.rstd[:, :], ALU.mult))
                link(nc.vector.tensor_tensor(tmp[:, :], tmp[:, :], var[:, :], ALU.mult))
                link(nc.vector.tensor_scalar(tmp[:, :], tmp[:, :], -0.5, 1.5, ALU.mult, ALU.add))
                link(nc.vector.tensor_tensor(c.rstd[:, :], c.rstd[:, :], tmp[:, :], ALU.mult))
                link(nc.vector.scalar_tensor_tensor(out=c.nmr[:, :], in0=c.mean[:, :], scalar=-1.0,
                                                    in1=c.rstd[:, :], op0=ALU.mult, op1=ALU.mult))

            @block.scalar
            def _(act):
                act.wait_ge(var_ready, 1)
                nc.scalar.activation(root[:, :], var[:, :], ACT.Sqrt).then_inc(root_ready, 1)
        mem.clear()


def normalised(nc, c, out, i):
    return nc.vector.tensor_scalar(out, c.y[:, bass.ds(i, 1), :].rearrange("p a d -> p (a d)"),
                                   c.rstd[:, bass.ds(i, 1)], c.nmr[:, bass.ds(i, 1)], ALU.mult, ALU.add)


def stage_gate(nc, c, wgate, rows):
    PAIRS, HB = TB // 2, TB // 2
    with ExitStack() as stack:
        mem = Mem(nc, stack)
        wg = mem.sb("g_w", [P, KC, E])
        st = [mem.sb(f"g_rows{u}", [P, HB, D]) for u in range(2)]
        xt = [mem.sb(f"g_rows_t{u}", [P, 2, KC, P]) for u in range(2)]
        p_tr = [mem.ps(f"g_ps_t{u}") for u in range(2)]
        lt = [mem.sb(f"g_logits_t{u}", [E, 2, P]) for u in range(2)]
        p_lt = [mem.ps(f"g_ps_logits_t{u}") for u in range(2)]
        p_g = mem.ps("g_ps_logits")
        loaded_w = mem.sem("g_weights")
        ready, turned, copied, gated = mem.sem("g_ready"), mem.sem("g_turned"), mem.sem("g_copied"), mem.sem("g_gated")
        stored = [mem.sem(f"g_stored{u}") for u in range(2)]
        lt_copied, logits_turned = mem.sem("g_lt_copied"), mem.sem("g_logits_turned")
        done = mem.sem("g_done")
        halves = rows.rearrange("(b h t p) d -> b h p t d", b=B, h=2, p=P)
        with nc.Block() as block:
            @block.sync
            def _(sp):
                sp.dma_start(wg[:, :, :], wgate.rearrange("(c p) e -> p c e", p=P)).then_inc(loaded_w, 16)

                def store(b):
                    for h in range(2):
                        sp.wait_ge(ready, b * PAIRS + 2 * h + 2)
                        sp.dma_start(halves[bass.ds(b, 1), h, :, :, :].rearrange("b p t d -> (b p) t d"),
                                     st[h][:, :, :]).then_inc(stored[h], 16)
                peeled(sp, B, store)
                for h in range(2):
                    sp.wait_ge(stored[h], 16 * B)

            @block.vector
            def _(dve):
                def norm(b):
                    for s in range(PAIRS):
                        wait_from(dve, turned, (b - 1) * PAIRS + s + 1)
                        if s % 2 == 0:
                            wait_from(dve, stored[s // 2], b * 16)
                        normalised(nc, c, st[s // 2][:, s % 2 * 2, :], b * TB + 2 * s)
                        normalised(nc, c, st[s // 2][:, s % 2 * 2 + 1, :], b * TB + 2 * s + 1).then_inc(ready, 1)
                peeled(dve, B, norm)
                dve.wait_ge(logits_turned, NT // 2)
                nc.vector.tensor_copy(c.logits[:, :], p_g[:, 0:NT * E]).then_inc(done, 1)

            @block.tensor
            def _(pe):
                def turn(i, s):
                    pe.wait_ge(ready, i + 1)
                    wait_from(pe, copied, i - 1)
                    for j in range(2):
                        for k in range(KC):
                            col = (j * KC + k) * P
                            mm = nc.tensor.transpose(p_tr[s % 2][:, col:col + P],
                                                     st[s // 2][:, s % 2 * 2 + j, k * P:(k + 1) * P], c.ident[:, :])
                    mm.then_inc(turned, 1)

                def gate(i, s):
                    pe.wait_ge(copied, i + 1)
                    wait_from(pe, lt_copied, i - 1)
                    for k in range(KC):
                        mm = nc.tensor.matmul(p_lt[s % 2][0:E, 0:2 * P], wg[:, k, :], xt[s % 2][:, :, k, :],
                                              start=(k == 0), stop=(k == KC - 1))
                    mm.then_inc(gated, 1)

                def turn_logits(i, s):
                    pe.wait_ge(lt_copied, i + 1)
                    for j in range(2):
                        mm = nc.tensor.matmul(p_g[:, bass.ds((2 * i + j) * E, E)], lt[s % 2][:, j, :],
                                              c.ident[0:E, 0:E], start=True, stop=True)
                    mm.then_inc(logits_turned, 1)

                def pairs(b, first, last):
                    for s in range(PAIRS):
                        if not (last and s == PAIRS - 1):
                            turn(b * PAIRS + s + 1, (s + 1) % PAIRS)
                        gate(b * PAIRS + s, s)
                        if not (first and s == 0):
                            turn_logits(b * PAIRS + s - 1, (s - 1) % 2)
                pe.wait_ge(loaded_w, 16)
                turn(0, 0)
                peeled_ends(pe, B, pairs)
                turn_logits(NT // 2 - 1, (NT // 2 - 1) % 2)

            @block.scalar
            def _(act):
                def copy_logits(i, s):
                    act.wait_ge(gated, i + 1)
                    wait_from(act, logits_turned, i - 1)
                    nc.scalar.activation(lt[s % 2][:, :, :].rearrange("e j n -> e (j n)"), p_lt[s % 2][0:E, 0:2 * P],
                                         ACT.Copy).then_inc(lt_copied, 1)

                def copy(b, first, last):
                    for s in range(PAIRS):
                        act.wait_ge(turned, b * PAIRS + s + 1)
                        wait_from(act, gated, b * PAIRS + s - 1)
                        nc.scalar.activation(xt[s % 2][:, :, :, :].rearrange("p j c n -> p (j c n)"),
                                             p_tr[s % 2][:, :], ACT.Copy).then_inc(copied, 1)
                        if not (first and s == 0):
                            copy_logits(b * PAIRS + s - 1, (s - 1) % 2)
                peeled_ends(act, B, copy)
                copy_logits(NT // 2 - 1, (NT // 2 - 1) % 2)
        mem.clear()


def stage_route(nc, c, tiles, fixed, rows, sums):
    with ExitStack() as stack:
        mem = Mem(nc, stack)
        G = NT * E
        DEEP = 8
        names = ("ex", "pr", "pr2", "eq", "cand", "oh1", "oh2", "mask", "incl", "pos", "prod")
        t = {n: mem.sb(f"e_{n}", [P, NT, E]) for n in names}
        maskb = mem.sb("e_maskb", [P, G], BF16)
        tri = mem.sb("e_tri", [P, P], BF16)
        ones = mem.sb("e_ones", [P, P], BF16)
        totals = mem.sb("e_totals", [P, NT, E])
        unit = mem.sb("e_unit", [P, NT])
        iota_e = mem.sb("e_iota_e", [P, E])
        iota_p = mem.sb("e_iota_p", [P, P])
        iota_t = mem.sb("e_iota_t", [P, tiles])
        token = mem.sb("e_token", [P, NT])
        small = {n: mem.sb(f"e_{n}", [P, NT]) for n in ("mx", "sm", "rc", "w1", "w2", "cm", "slot")}
        sloti = mem.sb("e_sloti", [P, NT], I32)
        hi_i = mem.sb("e_hi_i", [P, NT], I32)
        hi = mem.sb("e_hi", [P, 2, NT])
        value = mem.sb("e_value", [P, 2, NT, 2])
        lo = mem.sb("e_lo", [P, 2, NT])
        cnt = {n: mem.sb(f"e_{n}", [P, E]) for n in ("need", "endt", "start", "drop")}
        need_i = mem.sb("e_need_i", [P, E], I32)
        own = mem.sb("e_own", [P, tiles, E - 1])
        ownf = mem.sb("e_ownf", [P, tiles])
        oh_lo = [mem.sb(f"e_oh_lo{u}", [P, P]) for u in range(DEEP)]
        oh_hi = [mem.sb(f"e_oh_hi{u}", [P, 2, tiles]) for u in range(DEEP)]
        table = mem.sb("e_table", [P, 2, tiles])
        p_r, p_n, p_m = mem.ps("e_ps_rank"), mem.ps("e_ps_totals"), mem.ps("e_ps_map")
        made, shifted, ex_done = mem.sem("e_made"), mem.sem("e_shifted"), mem.sem("e_ex")
        mask_done, ranked, order = mem.sem("e_mask_done"), mem.sem("e_ranked"), mem.sem("e_order")
        hi_done, mapped = mem.sem("e_hi_done"), mem.sem("e_mapped")
        sums_copied = mem.sem("e_sums_copied")
        GE = [P, NT, E]
        with nc.Block() as block:
            @block.sync
            def _(sp):
                for b in range(B):
                    sp.dma_start(sums[b * S:(b + 1) * S, :], rows[b * S:(b + 1) * S, :]).then_inc(sums_copied, 16)
                sp.wait_ge(sums_copied, 16 * B)

            @block.gpsimd
            def _(pool):
                imprecise = dict(allow_small_or_imprecise_dtypes=True)
                nc.gpsimd.iota(iota_e[:, :], pattern=[[1, E]], base=0, channel_multiplier=0, **imprecise).then_inc(made, 1)
                nc.gpsimd.iota(iota_p[:, :], pattern=[[1, P]], base=0, channel_multiplier=0, **imprecise).then_inc(made, 1)
                nc.gpsimd.iota(iota_t[:, :], pattern=[[1, tiles]], base=0, channel_multiplier=0, **imprecise)\
                    .then_inc(made, 1)
                nc.gpsimd.iota(token[:, :], pattern=[[P, NT]], base=-N, channel_multiplier=1, **imprecise)\
                    .then_inc(made, 1)
                nc.gpsimd.memset(ones[:, :], 1.0).then_inc(made, 1)
                nc.gpsimd.memset(tri[:, :], 1.0).then_inc(made, 1)
                pool.wait_ge(made, 6)
                nc.gpsimd.affine_select(out=tri[:, :], in_=tri[:, :], compare_op=ALU.is_gt, fill=0.0, base=0,
                                        pattern=[[1, P]], channel_multiplier=-1).then_inc(made, 1)

            @block.scalar
            def _(act):
                act.wait_ge(shifted, 1)
                nc.scalar.activation(t["ex"][:, :, :], t["ex"][:, :, :], ACT.Exp).then_inc(ex_done, 1)

            @block.vector
            def _(dve):
                v = nc.vector
                link = Chain(dve, order)
                lg = c.logits[:, :].rearrange("p (i e) -> p i e", e=E)

                def wide(x):
                    return bcast(x[:, :].unsqueeze(2), GE)

                def per_expert(x):
                    return bcast(x[:, :].unsqueeze(1), GE)

                def first_of(values, best, onehot):
                    link(v.tensor_tensor(t["eq"][:, :, :], values, wide(best), ALU.is_equal))
                    link(v.scalar_tensor_tensor(out=t["cand"][:, :, :], in0=t["eq"][:, :, :], scalar=-float(E),
                                                in1=per_expert(iota_e), op0=ALU.mult, op1=ALU.add))
                    link(v.tensor_reduce(small["cm"][:, :], t["cand"][:, :, :], axis=AX.X, op=ALU.min))
                    link(v.tensor_tensor(onehot[:, :, :], t["cand"][:, :, :], wide(small["cm"]), ALU.is_equal))

                link(v.memset(unit[:, :], 1.0))
                link(v.tensor_reduce(small["mx"][:, :], lg, axis=AX.X, op=ALU.max))
                v.tensor_tensor(t["ex"][:, :, :], lg, wide(small["mx"]), ALU.subtract).then_inc(shifted, 1)
                dve.wait_ge(ex_done, 1)
                link(v.tensor_reduce(small["sm"][:, :], t["ex"][:, :, :], axis=AX.X, op=ALU.add))
                link(v.reciprocal(small["rc"][:, :], small["sm"][:, :]))
                link(v.tensor_tensor(t["pr"][:, :, :], t["ex"][:, :, :], wide(small["rc"]), ALU.mult))
                dve.wait_ge(made, 7)
                link(v.tensor_reduce(small["w1"][:, :], t["pr"][:, :, :], axis=AX.X, op=ALU.max))
                first_of(t["pr"][:, :, :], small["w1"], t["oh1"])
                link(v.scalar_tensor_tensor(out=t["pr2"][:, :, :], in0=t["oh1"][:, :, :], scalar=-2.0,
                                            in1=t["pr"][:, :, :], op0=ALU.mult, op1=ALU.add))
                link(v.tensor_reduce(small["w2"][:, :], t["pr2"][:, :, :], axis=AX.X, op=ALU.max))
                first_of(t["pr2"][:, :, :], small["w2"], t["oh2"])
                link(v.tensor_tensor(t["mask"][:, :, :], t["oh1"][:, :, :], t["oh2"][:, :, :], ALU.add))
                v.tensor_copy(maskb[:, :], t["mask"][:, :, :].rearrange("p i e -> p (i e)")).then_inc(mask_done, 1)
                dve.wait_ge(ranked, 1)
                link(v.tensor_copy(totals[:, :, :].rearrange("p i e -> p (i e)"), p_n[:, 0:G]))
                for e in range(E):
                    scan = v.tensor_tensor_scan(out=t["incl"][:, :, e], data0=unit[:, :], data1=totals[:, :, e],
                                                initial=0.0, op0=ALU.mult, op1=ALU.add)
                    link(scan)
                link(v.tensor_tensor(t["pos"][:, :, :].rearrange("p i e -> p (i e)"), p_r[:, 0:G],
                                     t["incl"][:, :, :].rearrange("p i e -> p (i e)"), ALU.add))
                link(v.tensor_tensor(t["pos"][:, :, :], t["pos"][:, :, :], totals[:, :, :], ALU.subtract))
                count = t["incl"][:, NT - 1, :]
                if fixed is None:
                    link(v.tensor_scalar(need_i[:, :], count, float(P - 1), None, ALU.add))
                    link(v.tensor_scalar(need_i[:, :], need_i[:, :], 7, None, ALU.arith_shift_right))
                    link(v.tensor_copy(cnt["need"][:, :], need_i[:, :]))
                    link(v.tensor_tensor_scan(out=cnt["endt"][:, :], data0=unit[:, 0:E], data1=cnt["need"][:, :],
                                              initial=0.0, op0=ALU.mult, op1=ALU.add))
                    link(v.tensor_tensor(cnt["start"][:, :], cnt["endt"][:, :], cnt["need"][:, :], ALU.subtract))
                    link(v.tensor_scalar(cnt["drop"][:, :], cnt["start"][:, :], float(P), None, ALU.mult))
                else:
                    link(v.tensor_scalar(cnt["start"][:, :], iota_e[:, :], float(fixed), None, ALU.mult))
                    link(v.tensor_scalar(cnt["drop"][:, :], count, float(fixed * P), float(4 * N), ALU.is_gt, ALU.mult))
                    link(v.scalar_tensor_tensor(out=cnt["drop"][:, :], in0=cnt["start"][:, :], scalar=float(P),
                                                in1=cnt["drop"][:, :], op0=ALU.mult, op1=ALU.add))
                link(v.tensor_tensor(t["pos"][:, :, :], t["pos"][:, :, :], per_expert(cnt["drop"]), ALU.add))
                for k, onehot in enumerate((t["oh1"], t["oh2"])):
                    link(v.tensor_tensor(t["prod"][:, :, :], t["pos"][:, :, :], onehot[:, :, :], ALU.mult))
                    link(v.tensor_reduce(small["slot"][:, :], t["prod"][:, :, :], axis=AX.X, op=ALU.add))
                    link(v.tensor_copy(sloti[:, :], small["slot"][:, :]))
                    link(v.tensor_scalar(hi_i[:, :], sloti[:, :], 7, None, ALU.arith_shift_right))
                    link(v.tensor_copy(hi[:, k, :], hi_i[:, :]))
                    link(v.scalar_tensor_tensor(out=lo[:, k, :], in0=hi[:, k, :], scalar=-float(P),
                                                in1=small["slot"][:, :], op0=ALU.mult, op1=ALU.add))
                link(v.tensor_tensor(own[:, :, :], bcast(iota_t[:, :].unsqueeze(2), [P, tiles, E - 1]),
                                     bcast(cnt["start"][:, 1:E].unsqueeze(1), [P, tiles, E - 1]), ALU.is_ge))
                link(v.tensor_reduce(ownf[:, :], own[:, :, :], axis=AX.X, op=ALU.add))
                link(v.tensor_copy(c.owner[:, 0:tiles], ownf[:, :]))
                for k, gain in enumerate((small["w1"], small["w2"])):
                    link(v.tensor_copy(value[:, k, :, 0], token[:, :]))
                    link(v.tensor_copy(value[:, k, :, 1], gain[:, :]))

                def outer_products(g, first, last):
                    for u in range(DEEP):
                        i, k = g * (DEEP // 2) + u // 2, u % 2
                        wait_from(dve, mapped, g * DEEP + u - (DEEP - 1))
                        v.tensor_scalar(oh_lo[u][:, :], iota_p[:, :], lo[:, k, bass.ds(i, 1)], None, ALU.is_equal)
                        v.scalar_tensor_tensor(
                            out=oh_hi[u][:, :, :], in0=bcast(iota_t[:, :].unsqueeze(1), [P, 2, tiles]),
                            scalar=hi[:, k, bass.ds(i, 1)],
                            in1=bcast(value[:, k, bass.ds(i, 1), :].rearrange("p i a -> p (i a)").unsqueeze(2),
                                      [P, 2, tiles]),
                            op0=ALU.is_equal, op1=ALU.mult).then_inc(hi_done, 1)
                peeled_ends(dve, 2 * NT // DEEP, outer_products)
                dve.wait_ge(mapped, 2 * NT)
                link(v.tensor_copy(table[:, :, :].rearrange("p a t -> p (a t)"), p_m[:, 0:2 * tiles]))
                link(v.tensor_scalar(c.scatter[:, 0:tiles], table[:, 0, :], float(N), None, ALU.add))
                link(v.tensor_scalar(c.gather[:, 0:tiles], table[:, 0, :], float(N), float(N - 1), ALU.add, ALU.min))
                link(v.tensor_copy(c.gains[:, 0:tiles], table[:, 1, :]))

            @block.tensor
            def _(pe):
                pe.wait_ge(mask_done, 1)
                pe.wait_ge(made, 7)
                nc.tensor.matmul(p_r[:, 0:G], tri[:, :], maskb[:, :], start=True, stop=True)
                nc.tensor.matmul(p_n[:, 0:G], ones[:, :], maskb[:, :], start=True, stop=True).then_inc(ranked, 1)

                def outer_products(g, first, last):
                    for u in range(DEEP):
                        pe.wait_ge(hi_done, g * DEEP + u + 1)
                        nc.tensor.matmul(p_m[:, 0:2 * tiles], oh_lo[u][:, :],
                                         oh_hi[u][:, :, :].rearrange("p a t -> p (a t)"),
                                         start=(first and u == 0), stop=(last and u == DEEP - 1)).then_inc(mapped, 1)
                peeled_ends(pe, 2 * NT // DEEP, outer_products)
        mem.clear()


def stage_experts(nc, c, tiles, fixed, F, w1, w2, b1, b2, func, rows, sums):
    FC = F // P
    HW = min(F, HALF)
    STEP, AHEAD = (2, 2) if fixed is None else (2 * fixed, fixed)
    with ExitStack() as stack:
        mem = Mem(nc, stack)
        ig = [mem.sb(f"m_ig{u}", [P, 1], I32) for u in range(AHEAD)]
        isc = [mem.sb(f"m_is{u}", [P, 1], I32) for u in range(2)]
        xg = [mem.sb(f"m_x{u}", [P, D]) for u in range(AHEAD)]
        xt = [mem.sb(f"m_xt{u}", [P, KC, P]) for u in range(2)]
        hs = [mem.sb(f"m_h{u}", [P, F]) for u in range(2)]
        ht = [mem.sb(f"m_ht{u}", [P, FC, P]) for u in range(2)]
        ys = [mem.sb(f"m_y{u}", [P, D]) for u in range(2)]
        p_x, p_y = mem.ps("m_ps_x"), mem.ps("m_ps_y")
        BUFS = 2 if F <= HALF else 1
        p_hs = [mem.ps(f"m_ps_h{u}", (P, max(F, HALF))) for u in range(BUFS)]
        p_t = mem.ps("m_ps_t", (P, max(F, HALF)))
        idx_g, idx_s = mem.sem("m_idx_g"), mem.sem("m_idx_s")
        gathered = [mem.sem(f"m_gathered{u}") for u in range(AHEAD)]
        added = [mem.sem(f"m_added{u}") for u in range(2)]
        x_turned, x_copied = mem.sem("m_x_turned"), mem.sem("m_x_copied")
        h_made, biased, act_done = mem.sem("m_h_made"), mem.sem("m_biased"), mem.sem("m_act_done")
        h_turned, h_copied = mem.sem("m_h_turned"), mem.sem("m_h_copied")
        y_made, y_biased, y_scaled = mem.sem("m_y_made"), mem.sem("m_y_biased"), mem.sem("m_y_scaled")
        spare_p = mem.sem("m_spare")
        halves = F // HW
        with nc.Block() as block:
            def steps(eng, body):
                peeled_ends(eng, tiles // STEP, body)

            @block.gpsimd
            def _(pool):
                def gather(t, u):
                    wait_apart(pool, spare_p, idx_g, t + 1)
                    pool.indirect_dma_start(out=xg[u][:, :], out_offset=None, in_=rows,
                                            in_offset=bass.IndirectOffsetOnAxis(ap=ig[u][:, :], axis=0))\
                        .then_inc(gathered[u], 16)

                def add(t, u):
                    wait_apart(pool, spare_p, idx_s, t + 1)
                    wait_apart(pool, spare_p, y_scaled, t + 1)
                    pool.indirect_dma_start(out=sums, out_offset=bass.IndirectOffsetOnAxis(ap=isc[u][:, :], axis=0),
                                            in_=ys[u][:, :], in_offset=None, bounds_check=N - 1, oob_is_err=False,
                                            compute_op=ALU.add).then_inc(added[u], 16)

                for u in range(AHEAD):
                    gather(u, u)

                def body(g, first, last):
                    t = g * STEP
                    for u in range(STEP):
                        if not (last and u >= STEP - AHEAD):
                            gather(t + u + AHEAD, u % AHEAD)
                        if first and u == 0:
                            continue
                        before = [t * 8 + (u // 2) * 16, t * 8 + ((u - 1) // 2) * 16]
                        if fixed is None:
                            wait_apart(pool, spare_p, added[u % 2], before[u % 2])
                        elif u - 1 in (0, fixed):
                            wait_apart(pool, spare_p, added[0], before[0])
                            wait_apart(pool, spare_p, added[1], before[1])
                        add(t + u - 1, (u - 1) % 2)
                steps(pool, body)
                if fixed is None:
                    pool.wait_ge(added[0], 8 * tiles)
                add(tiles - 1, 1)
                for u in range(2):
                    pool.wait_ge(added[u], 8 * tiles)

            @block.tensor
            def _(pe):
                def turn_x(g, u):
                    t, a = g * STEP + u, u % AHEAD
                    pe.wait_ge(gathered[a], g * (STEP // AHEAD * 16) + (u // AHEAD * 16 + 16))
                    wait_from(pe, x_copied, t)
                    for k in range(KC):
                        mm = nc.tensor.transpose(p_x[:, k * P:(k + 1) * P], xg[a][:, k * P:(k + 1) * P], c.ident[:, :])
                    mm.then_inc(x_turned, 1)

                owner = [pe.alloc_register(Mem.label("owner_pe")) for u in range(2)]

                def load_owner(t, u):
                    if fixed is None:
                        pe.reg_load(owner[u], c.owner[0:1, bass.ds(t, 1)])

                def expert(g, u):
                    if fixed is None:
                        return pe.snap(owner[u % 2], min_val=0, max_val=E - 1)
                    return g * 2 + u // fixed

                def first_product(t, u, e):
                    pe.wait_ge(x_copied, t + 1)
                    for half in range(halves):
                        wait_from(pe, biased, t * halves + (half - BUFS * halves + 1))
                        for k in range(KC):
                            mm = nc.tensor.matmul(p_hs[u % BUFS][:, half * HW:(half + 1) * HW], xt[u][:, k, :],
                                                  w1[:, bass.ds(e * KC + k, 1), half * HW:(half + 1) * HW]
                                                  .rearrange("p a f -> p (a f)"),
                                                  start=(k == 0), stop=(k == KC - 1))
                        mm.then_inc(h_made, 1)

                def turn_h(t, u):
                    for half in range(halves):
                        pe.wait_ge(act_done, t * halves + half + 1)
                        wait_from(pe, h_copied, t * halves + half - halves + 1)
                        for j in range(HW // P):
                            at = half * HW + j * P
                            mm = nc.tensor.transpose(p_t[:, at:at + P], hs[u][:, at:at + P], c.ident[:, :])
                        mm.then_inc(h_turned, 1)

                def second_product(t, u, e):
                    wait_from(pe, y_biased, t)
                    for f in range(FC):
                        if f % (HW // P) == 0:
                            pe.wait_ge(h_copied, t * halves + f // (HW // P) + 1)
                        mm = nc.tensor.matmul(p_y[:, 0:D], ht[u][:, f, :],
                                              w2[:, bass.ds(e * FC + f, 1), :].rearrange("p a d -> p (a d)"),
                                              start=(f == 0), stop=(f == FC - 1))
                    mm.then_inc(y_made, 1)

                def body(g, first, last):
                    t = g * STEP
                    for u in range(STEP):
                        first_product(t + u, u % 2, expert(g, u))
                        if not (last and u == STEP - 1):
                            turn_x(g + (u + 1) // STEP, (u + 1) % STEP)
                        if not (first and u == 0):
                            second_product(t + u - 1, (u + 1) % 2, expert(g, u - 1))
                        if not (last and u == STEP - 1):
                            load_owner(t + u + 1, (u + 1) % 2)
                        turn_h(t + u, u % 2)
                load_owner(0, 0)
                turn_x(0, 0)
                steps(pe, body)
                second_product(tiles - 1, 1, expert(tiles // STEP - 1, STEP - 1))

            @block.scalar
            def _(act):
                def scale_y(t, u):
                    act.wait_ge(y_biased, t + 1)
                    nc.scalar.activation(ys[u][:, :], ys[u][:, :], ACT.Copy, scale=c.gains[:, bass.ds(t, 1)])\
                        .then_inc(y_scaled, 1)

                def copy_x(t, u):
                    act.wait_ge(x_turned, t + 1)
                    wait_from(act, h_made, (t - 1) * halves)
                    nc.scalar.activation(xt[u][:, :, :].rearrange("p c n -> p (c n)"), p_x[:, 0:D], ACT.Identity)\
                        .then_inc(x_copied, 1)

                def body(g, first, last):
                    t = g * STEP
                    for u in range(STEP):
                        for half in range(halves):
                            act.wait_ge(biased, (t + u) * halves + half + 1)
                            span = hs[u % 2][:, half * HW:(half + 1) * HW]
                            nc.scalar.activation(span, span, func).then_inc(act_done, 1)
                        if not (last and u == STEP - 1):
                            copy_x(t + u + 1, (u + 1) % 2)
                        if not (first and u == 0):
                            scale_y(t + u - 1, (u + 1) % 2)
                copy_x(0, 0)
                steps(act, body)
                scale_y(tiles - 1, 1)

            @block.vector
            def _(dve):
                owner = [dve.alloc_register(Mem.label("owner_dve")) for u in range(2)]

                def load_owner(t, u):
                    if fixed is None:
                        dve.reg_load(owner[u], c.owner[0:1, bass.ds(t, 1)])

                def expert(g, u):
                    if fixed is None:
                        return dve.snap(owner[u % 2], min_val=0, max_val=E - 1)
                    return g * 2 + u // fixed

                def gather_indices(t, u):
                    nc.vector.tensor_copy(ig[u][:, :], c.gather[:, bass.ds(t, 1)]).then_inc(idx_g, 1)

                def bias_h(t, u, e):
                    wait_from(dve, h_turned, (t - 1) * halves)
                    for half in range(halves):
                        dve.wait_ge(h_made, t * halves + half + 1)
                        nc.vector.tensor_tensor(hs[u][:, half * HW:(half + 1) * HW],
                                                p_hs[u % BUFS][:, half * HW:(half + 1) * HW],
                                                b1[:, bass.ds(e, 1), half * HW:(half + 1) * HW]
                                                .rearrange("p a f -> p (a f)"), ALU.add).then_inc(biased, 1)

                def copy_h(t, u):
                    wait_from(dve, y_made, t - 1)
                    for half in range(halves):
                        dve.wait_ge(h_turned, t * halves + half + 1)
                        nc.vector.tensor_copy(ht[u][:, :, :].rearrange("p f n -> p (f n)")[:, half * HW:(half + 1) * HW],
                                              p_t[:, half * HW:(half + 1) * HW]).then_inc(h_copied, 1)

                def bias_y(t, u, e):
                    dve.wait_ge(y_made, t + 1)
                    wait_from(dve, added[u], (t - u) * 8)
                    nc.vector.tensor_copy(isc[u][:, :], c.scatter[:, bass.ds(t, 1)]).then_inc(idx_s, 1)
                    nc.vector.tensor_tensor(ys[u][:, :], p_y[:, 0:D], b2[:, bass.ds(e, 1), :]
                                            .rearrange("p a d -> p (a d)"), ALU.add).then_inc(y_biased, 1)

                def body(g, first, last):
                    t = g * STEP
                    for u in range(STEP):
                        bias_h(t + u, u % 2, expert(g, u))
                        if not (last and u >= STEP - AHEAD):
                            gather_indices(t + u + AHEAD, u % AHEAD)
                        if not (first and u == 0):
                            bias_y(t + u - 1, (u + 1) % 2, expert(g, u - 1))
                        if not (last and u == STEP - 1):
                            load_owner(t + u + 1, (u + 1) % 2)
                        copy_h(t + u, u % 2)
                for u in range(AHEAD):
                    gather_indices(u, u)
                load_owner(0, 0)
                steps(dve, body)
                bias_y(tiles - 1, 1, expert(tiles // STEP - 1, STEP - 1))
        mem.clear()


def stage_to_channels(nc, c):
    with ExitStack() as stack:
        mem = Mem(nc, stack)
        p_tr = [mem.ps(f"t_ps{u}") for u in range(4)]
        ready, turned, copied = mem.sem("t_ready"), mem.sem("t_turned"), mem.sem("t_copied")
        PAIRS = [(0, 2), (1, 3), (4, 6), (5, 7)]
        with nc.Block() as block:
            @block.vector
            def _(dve):
                nc.vector.memset(c.xe[:, :, :, L1:L1 + 2], 0.0)
                nc.vector.memset(c.xo[:, :, :, 0:1], 0.0)
                with dve.Fori(0, B) as b:
                    for t in range(TB):
                        normalised(nc, c, c.x2[:, bass.ds(b * TB + t, 1), :].rearrange("p a d -> p (a d)"),
                                   b * TB + t).then_inc(ready, 1)

            @block.tensor
            def _(pe):
                for b in range(B):
                    for s, pair in enumerate(PAIRS):
                        pe.wait_ge(ready, b * TB + pair[1] + 1)
                        wait_from(pe, copied, (b - 1) * len(PAIRS) + s + 1)
                        for k in range(KC):
                            for j, t in enumerate(pair):
                                at = (k * 2 + j) * P
                                mm = nc.tensor.transpose(p_tr[s][:, at:at + P],
                                                         c.x2[:, b * TB + t, k * P:(k + 1) * P], c.ident[:, :])
                        mm.then_inc(turned, 1)

            @block.scalar
            def _(act):
                with act.Fori(0, B) as b:
                    for s, pair in enumerate(PAIRS):
                        act.wait_ge(turned, b * len(PAIRS) + s + 1)
                        dst, at = (c.xe, 0) if s % 2 == 0 else (c.xo, 1)
                        at += (pair[0] // 2) * P
                        nc.scalar.activation(
                            dst[:, :, bass.ds(b, 1), at:at + 2 * P].rearrange("p c b n -> p (c b) n"),
                            p_tr[s][:, :].rearrange("p (c n) -> p c n", c=KC), ACT.Copy).then_inc(copied, 1)
        mem.clear()


def stage_wavelet(nc, a, c):
    with ExitStack() as stack:
        mem = Mem(nc, stack)
        fil = mem.sb("w_filters", [P, KC, 4, 4])
        fs = mem.sb("w_sums", [P, KC, 2, 5])
        diag = mem.sb("w_diag", [P, KC, 9, P])
        blocks = mem.sb("w_blocks", [P, P])
        low1 = mem.sb("w_low1", [P, KC, B, L1 + 2])
        high1 = mem.sb("w_high1", [P, KC, B, L1 + 2])
        low2 = mem.sb("w_low2", [P, KC, B, L2])
        high2 = mem.sb("w_high2", [P, KC, B, L2 + 2])
        q = mem.sb("w_q", [P, KC, B, L2])
        z = mem.sb("w_z", [P, KC, B])
        al = mem.sb("w_attn", [P, KC, B, L2 + 2])
        qt = mem.sb("w_qt", [P, B, KC, 2, P])
        kvm = mem.sb("w_kv", [P, B, KC, P])
        zm = mem.sb("w_zm", [P, B, KC, P])
        den = mem.sb("w_den", [P, KC, L2])
        htt = mem.sb("w_ht", [P, B, KC, 2, P])
        se, so = c.xe, c.xo
        banks = [mem.ps(f"w_ps{n}") for n in range(8)]
        loaded, order, made = mem.sem("w_loaded"), mem.sem("w_order"), mem.sem("w_made")
        diag_ready, sums_ready = mem.sem("w_diag_ready"), mem.sem("w_sums_ready")
        high_made, high_copied = mem.sem("w_high_made"), mem.sem("w_high_copied")
        high2_made, high2_copied = mem.sem("w_high2_made"), mem.sem("w_high2_copied")
        low1_begun, low1_ready = mem.sem("w_low1_begun"), mem.sem("w_low1_ready")
        low2_begun = mem.sem("w_low2_begun")
        syn2_begun, syn2_ready = mem.sem("w_syn2_begun"), mem.sem("w_syn2_ready")
        syn1_begun, syn1_ready = mem.sem("w_syn1_begun"), mem.sem("w_syn1_ready")
        min_ready, exp_ready, q_ready = mem.sem("w_min"), mem.sem("w_exp"), mem.sem("w_q_ready")
        turned, qt_copied, ht_copied = mem.sem("w_turned"), mem.sem("w_qt_copied"), mem.sem("w_ht_copied")
        kv_made, kv_ready, nd_made, nd_used = mem.sem("w_kv_made"), mem.sem("w_kv_ready"), mem.sem("w_nd"), mem.sem("w_nd_used")
        tile_made, tile_used = mem.sem("w_tile_made"), mem.sem("w_tile_used")
        PAIRS = TB // 2
        SUMS = ((0,), (1, 2), (3,), (0, 1), (2, 3))
        EVEN, ODD = ((0, 0), (1, 1), (2, 2)), ((1, 3), (2, 4))

        def tap(f, n):
            return lambda k: fil[:, k, f, n:n + 1]

        def total(f, n):
            return lambda k: fs[:, k, f, n:n + 1]

        def part(x, at, n, step=1):
            return lambda k: x[:, k, :, at:at + (n - 1) * step + 1:step]

        def of_batch(x, b, at, n, step=1):
            return lambda k: x[:, k, b, at:at + (n - 1) * step + 1:step]

        with nc.Block() as block:
            @block.sync
            def _(sp):
                sp.dma_start(fil[:, :, :, :], a.filters).then_inc(loaded, 16)

            @block.gpsimd
            def _(pool):
                nc.gpsimd.memset(blocks[:, :], 1.0).then_inc(made, 1)
                pool.wait_ge(made, 1)
                bl = blocks[:, :].rearrange("p (h r) -> p h r", r=HD)
                nc.gpsimd.affine_select(out=bl, in_=bl, compare_op=ALU.is_ge, fill=0.0, base=0,
                                        pattern=[[-HD, P // HD], [0, HD]], channel_multiplier=1).then_inc(made, 1)
                pool.wait_ge(made, 2)
                nc.gpsimd.affine_select(out=bl, in_=bl, compare_op=ALU.is_ge, fill=0.0, base=HD - 1,
                                        pattern=[[HD, P // HD], [0, HD]], channel_multiplier=-1).then_inc(made, 1)

            @block.vector
            def _(dve):
                v = nc.vector
                link = Chain(dve, order)
                for x in (low1, high1, high2, al):
                    v.memset(x[:, :, :, 0:1], 0.0)
                    n = x.shape[3]
                    v.memset(x[:, :, :, n - 1:n], 0.0)
                dve.wait_ge(loaded, 16)

                def add_tap(dst, src, scalar, begin=False):
                    if begin:
                        return v.tensor_scalar(dst, src, scalar, None, ALU.mult)
                    return v.scalar_tensor_tensor(out=dst, in0=src, scalar=scalar, in1=dst, op0=ALU.mult, op1=ALU.add)

                analysis = ((c.xo, 0), (c.xe, 0), (c.xo, 1), (c.xe, 1))
                for k in range(KC):
                    for n, (src, at) in enumerate(analysis):
                        if k == 1 and n == 0:
                            dve.wait_ge(low1_begun, 1)
                            continue
                        one = add_tap(part(low1, 1, L1)(k), part(src, at, L1)(k), tap(0, n)(k), begin=(n == 0))
                        if n < 3:
                            link(one)
                    one.then_inc(low1_ready, 1)
                for k in range(KC):
                    dve.wait_ge(low2_begun, k + 1)
                    for n in range(1, 4):
                        link(add_tap(low2[:, k, :, :], part(low1, n, L2, 2)(k), tap(0, n)(k)))
                flat = low2[:, :, :, :].rearrange("p c b n -> p (c b n)")
                qf = q[:, :, :, :].rearrange("p c b n -> p (c b n)")
                v.tensor_scalar(qf, flat, 0.0, None, ALU.min).then_inc(min_ready, 1)
                for f in range(2):
                    for n, taps in enumerate(SUMS):
                        for k in range(KC):
                            src = fil[:, k, 2 + f, taps[0]:taps[0] + 1]
                            dst = fs[:, k, f, n:n + 1]
                            last = (v.tensor_copy(dst, src) if len(taps) == 1 else
                                    v.tensor_tensor(dst, src, fil[:, k, 2 + f, taps[1]:taps[1] + 1], ALU.add))
                last.then_inc(sums_ready, 1)
                dve.wait_ge(exp_ready, 1)
                v.scalar_tensor_tensor(out=qf, in0=flat, scalar=0.0, in1=qf, op0=ALU.max, op1=ALU.add)\
                    .then_inc(q_ready, 1)
                dve.wait_ge(q_ready, 1)
                link(v.tensor_reduce(z[:, :, :], q[:, :, :, :], axis=AX.X, op=ALU.add))
                dve.wait_ge(made, 3)
                for b in range(B):
                    for k in range(KC):
                        v.tensor_scalar(zm[:, b, k, :], blocks[:, :], z[:, k, b:b + 1], None, ALU.mult)
                    dve.wait_ge(turned, 2 * b + 1)
                    v.tensor_copy(qt[:, b, :, :, :].rearrange("p c j n -> p (c j n)"), banks[2 * b][:, :])\
                        .then_inc(qt_copied, 1)
                for b in range(B):
                    dve.wait_ge(kv_made, b + 1)
                    for k in range(KC):
                        last = v.tensor_tensor(kvm[:, b, k, :], banks[b][:, k * P:(k + 1) * P], blocks[:, :], ALU.mult)
                    last.then_inc(kv_ready, 1)

                dve.wait_ge(syn2_begun, 2 * KC)
                even, odd = part(low1, 1, L2, 2), part(low1, 2, L2, 2)
                for n in range(2):
                    for dst, terms in ((even, EVEN), (odd, ODD)):
                        for k in range(KC):
                            if n + 1 < len(terms):
                                off, t = terms[n + 1]
                                last = add_tap(dst(k), part(high2, off, L2)(k), total(1, t)(k))
                    link(last)

                def attention(b):
                    dve.wait_ge(nd_made, b + 1)
                    n, d = 2 * (b % 2) + 4, 2 * (b % 2) + 5
                    dn = den[:, :, :].rearrange("p c n -> p (c n)")
                    link(v.tensor_scalar(dn, banks[d][:, :], 1e-6, None, ALU.add))
                    link(v.reciprocal(dn, dn))
                    v.tensor_tensor(al[:, :, b, 1:1 + L2], banks[n][:, :].rearrange("p (c n) -> p c n", c=KC),
                                    den[:, :, :], ALU.mult).then_inc(nd_used, 1)
                    dve.wait_ge(nd_used, b + 1)
                    even, odd = of_batch(low1, b, 1, L2, 2), of_batch(low1, b, 2, L2, 2)
                    for n in range(3):
                        for dst, terms in ((odd, ODD), (even, EVEN)):
                            for k in range(KC):
                                if n < len(terms):
                                    off, t = terms[n]
                                    last = add_tap(dst(k), of_batch(al, b, off, L2)(k), total(0, t)(k))
                        if n < 2:
                            link(last)
                    last.then_inc(syn2_ready, 1)

                def synthesis(b):
                    dve.wait_ge(syn1_begun, (b + 1) * 2 * KC)
                    for n in (1, 2):
                        for dst, terms in ((of_batch(so, b, 1, L1), ODD), (of_batch(se, b, 0, L1), EVEN)):
                            for k in range(KC):
                                if n < len(terms):
                                    off, t = terms[n]
                                    last = add_tap(dst(k), of_batch(low1, b, off, L1)(k), total(0, t)(k))
                        if n == 1:
                            link(last)
                    last.then_inc(syn1_ready, 1)

                def tiles(b):
                    for i in range(b * PAIRS, (b + 1) * PAIRS):
                        dve.wait_ge(tile_made, i + 1)
                        v.tensor_tensor(c.y[:, 2 * i:2 * i + 2, :].rearrange("p a d -> p (a d)"), banks[i % 4][:, :],
                                        c.x2[:, 2 * i:2 * i + 2, :].rearrange("p a d -> p (a d)"), ALU.add)\
                            .then_inc(tile_used, 1)
                        dve.wait_ge(tile_used, i + 1)
                        for j in range(2):
                            row_stats(nc, c, 2 * i + j)
                for b in range(B + 2):
                    if b < B:
                        attention(b)
                    if 1 <= b <= B:
                        synthesis(b - 1)
                    if b >= 2:
                        tiles(b - 2)

            @block.scalar
            def _(act):
                def first_tap(dst, src, scalar, sem):
                    nc.scalar.activation(dst, src, ACT.Copy, scale=scalar).then_inc(sem, 1)

                def diagonals(n, count, scalar):
                    for k in range(KC):
                        for j in range(count):
                            last = nc.scalar.activation(diag[:, k, n + j, :], c.ident[:, :], ACT.Copy,
                                                        scale=scalar(j)(k))
                    last.then_inc(diag_ready, 1)

                def copy_high1(n):
                    act.wait_ge(high_made, n + 1)
                    b, k = n // KC, n % KC
                    nc.scalar.activation(high1[:, k, b, 1:1 + L1], banks[n % 4][:, :], ACT.Copy)\
                        .then_inc(high_copied, 1)

                def copy_high2(n):
                    act.wait_ge(high2_made, n + 1)
                    b, k = n // KC * 2, n % KC
                    nc.scalar.activation(high2[:, k, b:b + 2, 1:1 + L2],
                                         banks[4 + n][:, :].rearrange("p (b n) -> p b n", b=2), ACT.Copy)\
                        .then_inc(high2_copied, 1)

                def begin_low2(k):
                    act.wait_ge(low1_ready, k + 1)
                    first_tap(low2[:, k, :, :], part(low1, 0, L2, 2)(k), tap(0, 0)(k), low2_begun)

                def begin_synthesis(b):
                    act.wait_ge(syn2_ready, b + 1)
                    for k in range(KC):
                        first_tap(of_batch(so, b, 1, L1)(k), of_batch(low1, b, 1, L1)(k), total(0, 3)(k), syn1_begun)
                        first_tap(of_batch(se, b, 0, L1)(k), of_batch(low1, b, 0, L1)(k), total(0, 0)(k), syn1_begun)
                act.wait_ge(loaded, 16)
                diagonals(0, 4, lambda j: tap(1, j))
                first_tap(part(low1, 1, L1)(1), part(c.xo, 0, L1)(1), tap(0, 0)(1), low1_begun)
                copy_high1(0)
                copy_high1(1)
                begin_low2(0)
                copy_high1(2)
                copy_high1(3)
                begin_low2(1)
                copy_high2(0)
                copy_high2(1)
                act.wait_ge(min_ready, 1)
                qf = q[:, :, :, :].rearrange("p c b n -> p (c b n)")
                nc.scalar.activation(qf, qf, ACT.Exp).then_inc(exp_ready, 1)
                copy_high2(2)
                copy_high2(3)
                for b in range(B):
                    act.wait_ge(turned, 2 * b + 2)
                    nc.scalar.activation(htt[:, b, :, :, :].rearrange("p c j n -> p (c j n)"),
                                         banks[2 * b + 1][:, :], ACT.Copy).then_inc(ht_copied, 1)
                act.wait_ge(high2_copied, B // 2 * KC)
                act.wait_ge(sums_ready, 1)
                for k in range(KC):
                    first_tap(part(low1, 1, L2, 2)(k), part(high2, 0, L2)(k), total(1, 0)(k), syn2_begun)
                    first_tap(part(low1, 2, L2, 2)(k), part(high2, 1, L2)(k), total(1, 3)(k), syn2_begun)
                diagonals(4, 5, lambda j: total(1, j))
                copy_high1(4)
                begin_synthesis(0)
                copy_high1(5)
                copy_high1(6)
                begin_synthesis(1)
                copy_high1(7)
                begin_synthesis(2)
                begin_synthesis(3)

            @block.tensor
            def _(pe):
                def make_high1(n):
                    b, k = n // KC, n % KC
                    for j, (src, at) in enumerate(((c.xo, 0), (c.xe, 0), (c.xo, 1), (c.xe, 1))):
                        mm = nc.tensor.matmul(banks[n % 4][:, :], diag[:, k, j, :], src[:, k, b, at:at + L1],
                                              start=(j == 0), stop=(j == 3))
                    mm.then_inc(high_made, 1)

                def numerators(b):
                    pe.wait_ge(kv_ready, b + 1)
                    wait_from(pe, nd_used, b - 1)
                    for m, w in enumerate((kvm, zm)):
                        for k in range(KC):
                            mm = nc.tensor.matmul(banks[2 * (b % 2) + 4 + m][:, k * L2:(k + 1) * L2], w[:, b, k, :],
                                                  q[:, k, b, :], start=True, stop=True)
                    mm.then_inc(nd_made, 1)

                pe.wait_ge(diag_ready, 1)
                for n in range(4):
                    make_high1(n)
                for n in range(B // 2 * KC):
                    b, k = n // KC * 2, n % KC
                    pe.wait_ge(low1_ready, KC)
                    for j in range(4):
                        mm = nc.tensor.matmul(banks[4 + n][:, :], diag[:, k, j, :],
                                              low1[:, k, b:b + 2, j:j + 2 * L2 - 1:2], start=(j == 0), stop=(j == 3))
                    mm.then_inc(high2_made, 1)
                pe.wait_ge(high_copied, 4)
                pe.wait_ge(high2_copied, B // 2 * KC)
                pe.wait_ge(q_ready, 1)
                for b in range(B):
                    for m, src in enumerate((q, low2)):
                        for k in range(KC):
                            for j in range(2):
                                at = (k * 2 + j) * P
                                mm = nc.tensor.transpose(banks[2 * b + m][:, at:at + P], src[:, k, b, j * P:(j + 1) * P],
                                                         c.ident[:, :])
                        mm.then_inc(turned, 1)
                pe.wait_ge(qt_copied, B)
                pe.wait_ge(ht_copied, B)
                for b in range(B):
                    for k in range(KC):
                        for j in range(2):
                            mm = nc.tensor.matmul(banks[b][:, k * P:(k + 1) * P], qt[:, b, k, j, :], htt[:, b, k, j, :],
                                                  start=(j == 0), stop=(j == 1))
                    mm.then_inc(kv_made, 1)
                numerators(0)
                numerators(1)
                pe.wait_ge(kv_ready, B)
                make_high1(4)
                make_high1(5)
                numerators(2)
                make_high1(6)
                make_high1(7)
                numerators(3)
                pe.wait_ge(diag_ready, 2)
                pe.wait_ge(high_copied, B * KC)
                for i in range(NT // 2):
                    b, at = i // PAIRS, i % PAIRS * P
                    pe.wait_ge(syn1_ready, b + 1)
                    wait_from(pe, tile_used, i - 3)
                    for j, (low, terms) in enumerate(((se[:, :, b, at:at + P], EVEN), (so[:, :, b, at + 1:at + 1 + P], ODD))):
                        for k in range(KC):
                            dst = banks[i % 4][:, j * D + k * P:j * D + (k + 1) * P]
                            mm = nc.tensor.matmul(dst, low[:, k, :], c.ident[:, :], start=True, stop=False)
                            for off, n in terms:
                                mm = nc.tensor.matmul(dst, high1[:, k, b, at + off:at + off + P], diag[:, k, 4 + n, :],
                                                      start=False, stop=(n == terms[-1][1]))
                    mm.then_inc(tile_made, 1)
        mem.clear()


def stage_affine(nc, a, c):
    HB = TB // 2
    with ExitStack() as stack:
        mem = Mem(nc, stack)
        gamma = mem.sb("n_gamma", [P, D])
        beta = mem.sb("n_beta", [P, D])
        loaded, moved, scaled = mem.sem("n_loaded"), mem.sem("n_moved"), mem.sem("n_scaled")
        summed, spare = mem.sem("n_summed"), mem.sem("n_spare")
        loaded_b = mem.sem("n_loaded_beta")
        with nc.Block() as block:
            @block.sync
            def _(sp):
                sp.dma_start(beta[:, :], a.beta.partition_broadcast(P)).then_inc(loaded_b, 16)
                sp.dma_start(gamma[:, :], a.gamma.partition_broadcast(P)).then_inc(loaded, 16)

            @block.gpsimd
            def _(pool):
                pool.wait_ge(loaded_b, 16)
                with pool.Fori(0, B * 2) as h:
                    part = c.x2[:, bass.ds(h * HB, HB), :]
                    nc.gpsimd.tensor_tensor(part, part, bcast(beta[:, :].unsqueeze(1), [P, HB, D]), ALU.add)\
                        .then_inc(moved, 1)

            @block.vector
            def _(dve):
                def flat(x, i):
                    return x[:, bass.ds(i, 1), :].rearrange("p a d -> p (a d)")

                def scale(i):
                    nc.vector.scalar_tensor_tensor(out=flat(c.y, i), in0=flat(c.y, i), scalar=c.mean[:, bass.ds(i, 1)],
                                                   in1=gamma[:, :], op0=ALU.subtract, op1=ALU.mult).then_inc(scaled, 1)

                def add(i):
                    dve.wait_ge(scaled, i + 1)
                    nc.vector.scalar_tensor_tensor(out=flat(c.y, i), in0=flat(c.y, i), scalar=c.rstd[:, bass.ds(i, 1)],
                                                   in1=flat(c.x2, i), op0=ALU.mult, op1=ALU.add).then_inc(summed, 1)

                def stats(i):
                    wait_apart(dve, spare, summed, i + 1)
                    row_stats(nc, c, i)

                dve.wait_ge(loaded, 16)
                with dve.Fori(0, B * 2) as g:
                    for t in range(HB + 2):
                        if t < HB:
                            scale(g * HB + t)
                        if t == 1:
                            dve.wait_ge(moved, g + 1)
                        if 1 <= t <= HB:
                            add(g * HB + t - 1)
                        if t >= 2:
                            stats(g * HB + t - 2)
        mem.clear()


def stage_store(nc, c, out):
    HB, HALVES, BUFS = TB // 2, B * 2, 4
    with ExitStack() as stack:
        mem = Mem(nc, stack)
        st = [mem.sb(f"s_rows{u}", [P, HB, D]) for u in range(BUFS)]
        ready = mem.sem("s_ready")
        stored = [mem.sem(f"s_stored{u}") for u in range(BUFS)]
        rows = out.rearrange("(i p) d -> p i d", p=P)
        with nc.Block() as block:
            @block.vector
            def _(dve):
                for h in range(HALVES):
                    wait_from(dve, stored[h % BUFS], 16 * (h // BUFS))
                    for t in range(HB):
                        last = normalised(nc, c, st[h % BUFS][:, t, :], h * HB + t)
                    last.then_inc(ready, 1)

            @block.sync
            def _(sp):
                for h in range(HALVES):
                    sp.wait_ge(ready, h + 1)
                    sp.dma_start(rows[:, h * HB:(h + 1) * HB, :], st[h % BUFS][:, :, :]).then_inc(stored[h % BUFS], 16)
                for u in range(BUFS):
                    sp.wait_ge(stored[u], 16 * (HALVES // BUFS))


class Names:
    pass


def build(nc, a, out):
    Mem.uses = {}
    c = Names()

    def dram(name, shape, dt=FP32):
        return nc.dram_tensor(name, shape, dt).ap()
    c.q_parts, c.k_parts = dram("q_parts", [NH, HD, PARTS, S], BF16), dram("k_parts", [NH, HD, PARTS, S], BF16)
    rows = [dram(f"rows{n}", [N, D]) for n in range(2)]
    sums = [dram(f"sums{n}", [N, D]) for n in range(2)]
    F0 = 4 * D
    most = N * 2 // P + E - 1
    most += most % 2
    CAP = int(1.25 * N / E) // P
    with ExitStack() as stack:
        mem = Mem(nc, stack)
        stage_constants(nc, mem, c)
        c.six = mem.sb("six", [P, NT, 6])
        c.rstd = mem.sb("rstd", [P, NT])
        c.mean = mem.sb("mean", [P, NT])
        c.nmr = mem.sb("nmr", [P, NT])
        c.logits = mem.sb("logits", [P, NT * E])
        c.gather = mem.sb("gather", [P, most], I32)
        c.scatter = mem.sb("scatter", [P, most], I32)
        c.gains = mem.sb("gains", [P, most])
        c.owner = mem.sb("owner", [P, most], I32)
        with ExitStack() as inner:
            m = Mem(nc, inner)
            w1 = m.sb("w1", [P, E * KC, F0])
            w2 = m.sb("w2", [P, E * (F0 // P), D])
            late = m.sb("biases", [P, E * (F0 + D)])
            w1_loaded, w2_loaded, b_loaded = m.sem("w1_loaded"), m.sem("w2_loaded"), m.sem("b_loaded")
            flat = w2[:, :, :].rearrange("p f d -> p (f d)")
            half = E * (F0 // P) * D // 2
            c.v = flat[:, 0:half].rearrange("p (n t r) -> p n t r", n=NH, t=TB)
            c.probs = flat[:, half:2 * half].rearrange("p (t s) -> p t s", t=TB)
            c.y = flat[:, half:2 * half].rearrange("p (i d) -> p i d", d=D)
            c.ao = late[:, 0:NH * TB * HD].rearrange("p (n t r) -> p n t r", n=NH, t=TB)
            stage_project(nc, a, c)
            stage_attention(nc, a, c, w1, w1_loaded)
            FC = F0 // P
            stage_output(nc, a, c, w2, w2_loaded)
            stage_rstd(nc, c)
            b1 = late[:, 0:E * F0].rearrange("p (e f) -> p e f", e=E)
            b2 = late[:, E * F0:E * (F0 + D)].rearrange("p (e d) -> p e d", e=E)
            stage_gate(nc, c, a.gate_0, rows[0])
            with nc.Block() as block:
                @block.scalar
                def _(act):
                    act.dma_start(b1, a.b1_0.partition_broadcast(P)).then_inc(b_loaded, 16)
                    act.dma_start(b2, a.b2_0.partition_broadcast(P)).then_inc(b_loaded, 16)
                    for e in range(E // 2, E):
                        act.dma_start(w2[:, e * FC:(e + 1) * FC, :], a.w2_0[e].rearrange("(f p) d -> p f d", p=P))\
                            .then_inc(w2_loaded, 16)
            stage_route(nc, c, most, None, rows[0], sums[0])
            with nc.Block() as block:
                @block.tensor
                def _(pe):
                    pe.wait_ge(w1_loaded, 16 * E * KC)
                    pe.wait_ge(w2_loaded, 16 * E)

                @block.vector
                def _(dve):
                    dve.wait_ge(b_loaded, 32)
            stage_experts(nc, c, most, None, F0, w1, w2, b1, b2, ACT.Gelu, rows[0], sums[0])
            m.clear()
        with ExitStack() as inner:
            m = Mem(nc, inner)
            c.y = m.sb("y", [P, NT, D])
            c.x2 = m.sb("x2", [P, NT, D])
            with ExitStack() as inner2:
                m2 = Mem(nc, inner2)
                c.xe = m2.sb("x_even", [P, KC, B, L1 + 2])
                c.xo = m2.sb("x_odd", [P, KC, B, L1 + 2])
                stage_load_stats(nc, c, sums[0])
                stage_rstd(nc, c)
                stage_to_channels(nc, c)
                stage_wavelet(nc, a, c)
            stage_rstd(nc, c)
            w1 = m.sb("w1_1", [P, E * KC, D])
            w2 = m.sb("w2_1", [P, E * KC, D])
            b1 = m.sb("b1_1", [P, E, D])
            b2 = m.sb("b2_1", [P, E, D])
            loaded = m.sem("loaded_1")
            stage_affine(nc, a, c)
            stage_rstd(nc, c)
            stage_gate(nc, c, a.gate_1, rows[1])
            with nc.Block() as block:
                @block.scalar
                def _(act):
                    act.dma_start(w1[:, :, :], a.w1_1.rearrange("e (c p) f -> p (e c) f", p=P)).then_inc(loaded, 16)
                    act.dma_start(w2[:, :, :], a.w2_1.rearrange("e (c p) f -> p (e c) f", p=P)).then_inc(loaded, 16)
                    act.dma_start(b1[:, :, :], a.b1_1.partition_broadcast(P)).then_inc(loaded, 16)
                    act.dma_start(b2[:, :, :], a.b2_1.partition_broadcast(P)).then_inc(loaded, 16)
            stage_route(nc, c, CAP * E, CAP, rows[1], sums[1])
            with nc.Block() as block:
                @block.tensor
                def _(pe):
                    pe.wait_ge(loaded, 64)

                @block.vector
                def _(dve):
                    dve.wait_ge(loaded, 64)
            stage_experts(nc, c, CAP * E, CAP, D, w1, w2, b1, b2, ACT.Silu, rows[1], sums[1])
            stage_load_stats(nc, c, sums[1])
            stage_rstd(nc, c)
            stage_store(nc, c, out)


def kernel(**inputs):
    import numpy as np
    import concourse.bacc as bacc
    from concourse.bass_utils import run_bass_kernel_spmd

    g = {k: np.asarray(v) for k, v in inputs.items()}
    J = S // (2 * P)
    x = g["L0_attn_x"].reshape(B, J, P, 2, D).transpose(0, 1, 3, 2, 4).reshape(N, D)
    taps = np.stack([g["L1_attn_" + n] for n in ("h_filter", "g_filter", "h_synth", "g_synth")])
    arrays = {
        "x": x, "xt": x.T,
        "wqkv": np.concatenate([g["L0_attn_W" + n].T for n in "qkv"], axis=1),
        "bqk": np.stack([g["L0_attn_b" + n].reshape(KC, P) for n in "qk"]).transpose(2, 0, 1),
        "bv": g["L0_attn_bv"], "wo": g["L0_attn_Wo"].T, "bo": g["L0_attn_bo"],
        "gate_0": g["L0_ffn_w_gate"].T, "w1_0": g["L0_ffn_W1"], "b1_0": g["L0_ffn_b1"],
        "w2_0": g["L0_ffn_W2"], "b2_0": g["L0_ffn_b2"],
        "filters": taps.reshape(4, 4, KC, P).transpose(3, 2, 0, 1),
        "gamma": g["L1_attn_norm_gamma"], "beta": g["L1_attn_norm_beta"],
        "gate_1": g["L1_ffn_gate_w"].T, "w1_1": g["L1_ffn_w1"].transpose(0, 2, 1), "b1_1": g["L1_ffn_b1"],
        "w2_1": g["L1_ffn_w2"].transpose(0, 2, 1), "b2_1": g["L1_ffn_b2"],
    }
    nc = bacc.Bacc("TRN2", target_bir_lowering=False, num_devices=1)
    a = Names()
    feed = {}
    for name, array in arrays.items():
        feed["in_" + name] = np.ascontiguousarray(array)
        handle = nc.dram_tensor("in_" + name, array.shape, mybir.dt.from_np(array.dtype), kind="ExternalInput")
        a.__dict__[name] = handle.ap()
    out = nc.dram_tensor("out_rows", [N, D], FP32, kind="ExternalOutput").ap()
    build(nc, a, out)
    r = run_bass_kernel_spmd(nc, [feed], core_ids=[0])
    rows = r.results[0]["out_rows"]
    return rows.reshape(B, J, 2, P, D).transpose(0, 1, 3, 2, 4).reshape(B, S, D)
```
